# Optimizing a Trainium2 kernel written in Bass

```python
import numpy as np
import jax
import jax.numpy as jnp

def _softmax(x, axis=-1):
    return jax.nn.softmax(x, axis=axis)

def _gelu(x):
    return jax.nn.gelu(x, approximate=True)

def _silu(x):
    return jax.nn.silu(x)

def _sigmoid(x):
    return jax.nn.sigmoid(x)

def _layernorm(x, axis=-1, eps=1e-05):
    m = jnp.mean(x, axis=axis, keepdims=True)
    v = jnp.var(x, axis=axis, keepdims=True)
    return (x - m) / jnp.sqrt(v + eps)

def _scatter_add(tgt, idx, src, axis=0):
    return tgt.at[idx].add(src)

def _segment_sum(src, seg, n):
    return jax.ops.segment_sum(src, seg, n)
kernel_name = 'mk_hybrid_d1_jaxref_r8_94b945'

def setup_inputs(seed: int=0):
    np.random.seed(seed)
    _w = jnp.asarray

    def _L0_attn_a_setup():
        import jax, jax.numpy as jnp
        import numpy as np
        B, N, D = (4, 512, 128)
        H, DH = (16, 64)
        DFF = 512
        M = 64
        EPS_KERN = 1e-06
        EPS_LN = 1e-06

        def _softmax_kernel_feats(data, proj, is_query):
            dn = 1.0 / jnp.sqrt(jnp.sqrt(jnp.float32(data.shape[-1])))
            ratio = 1.0 / jnp.sqrt(jnp.float32(proj.shape[0]))
            data_dash = jnp.einsum('bnhd,md->bnhm', data * dn, proj)
            diag = jnp.sum(jnp.square(data), axis=-1, keepdims=True) * (dn * dn) / 2.0
            if is_query:
                mx = jnp.max(data_dash, axis=-1, keepdims=True)
            else:
                mx = jnp.max(data_dash)
            return ratio * (jnp.exp(data_dash - diag - mx) + EPS_KERN)

        def _layernorm(x, g, b):
            mu = jnp.mean(x, axis=-1, keepdims=True)
            var = jnp.mean(jnp.square(x - mu), axis=-1, keepdims=True)
            return (x - mu) * jax.lax.rsqrt(var + EPS_LN) * g + b

        def _encoder_forward(x, Wq, Wk, Wv, Wo, proj, W1, b1, W2, b2, ln1_g, ln1_b, ln2_g, ln2_b):
            q = jnp.einsum('bnd,dhk->bnhk', x, Wq)
            k = jnp.einsum('bnd,dhk->bnhk', x, Wk)
            v = jnp.einsum('bnd,dhk->bnhk', x, Wv)
            qf = _softmax_kernel_feats(q, proj, True)
            kf = _softmax_kernel_feats(k, proj, False)
            kv = jnp.einsum('bnhm,bnhd->bhmd', kf, v)
            num = jnp.einsum('bnhm,bhmd->bnhd', qf, kv)
            den = jnp.einsum('bnhm,bhm->bnh', qf, jnp.sum(kf, axis=1))
            attn = num / den[..., None]
            attn_out = jnp.einsum('bnhd,hdo->bno', attn, Wo)
            out1 = _layernorm(x + attn_out, ln1_g, ln1_b)
            h = jax.nn.elu(out1 @ W1 + b1)
            ffn_out = h @ W2 + b2
            return _layernorm(out1 + ffn_out, ln2_g, ln2_b)
        key = jax.random.key(seed)
        ks = jax.random.split(key, 12)
        s = 0.02
        inp = {'x': jax.random.normal(ks[0], (B, N, D), jnp.float32), 'Wq': jax.random.normal(ks[1], (D, H, DH), jnp.float32) * s, 'Wk': jax.random.normal(ks[2], (D, H, DH), jnp.float32) * s, 'Wv': jax.random.normal(ks[3], (D, H, DH), jnp.float32) * s, 'Wo': jax.random.normal(ks[4], (H, DH, D), jnp.float32) * s, 'proj': jax.random.normal(ks[5], (M, DH), jnp.float32), 'W1': jax.random.normal(ks[6], (D, DFF), jnp.float32) * s, 'b1': jnp.zeros((DFF,), jnp.float32), 'W2': jax.random.normal(ks[7], (DFF, D), jnp.float32) * s, 'b2': jnp.zeros((D,), jnp.float32), 'ln1_g': jnp.ones((D,), jnp.float32), 'ln1_b': jnp.zeros((D,), jnp.float32), 'ln2_g': jnp.ones((D,), jnp.float32), 'ln2_b': jnp.zeros((D,), jnp.float32)}
        return inp
    _L0_attn_a_in = _L0_attn_a_setup()

    def _L0_attn_b_setup():
        import jax, jax.numpy as jnp
        import numpy as np
        B, S, D, H = (4, 256, 128, 16)
        HD = D // H
        key = jax.random.key(seed)
        ks = jax.random.split(key, 5)
        s = 1.0 / np.sqrt(D)
        return {'x': jax.random.normal(ks[0], (B, S, D), dtype=jnp.float32), 'Wq': jax.random.normal(ks[1], (D, D), dtype=jnp.float32) * s, 'Wk': jax.random.normal(ks[2], (D, D), dtype=jnp.float32) * s, 'Wv': jax.random.normal(ks[3], (D, D), dtype=jnp.float32) * s, 'Wo': jax.random.normal(ks[4], (D, D), dtype=jnp.float32) * s, 'bo': jnp.zeros((D,), dtype=jnp.float32)}
    _L0_attn_b_in = _L0_attn_b_setup()

    def _L0_ffn_setup():
        import jax, jax.numpy as jnp
        import numpy as np
        NUM_EXPERTS = 160
        TOP_K = 8
        ROUTED_SCALE = 2.5
        HIDDEN = 128
        INTER = 64
        key = jax.random.key(seed)
        ks = jax.random.split(key, 7)
        B, S = (1, 256)
        return {'hidden_states': jax.random.normal(ks[0], (B, S, HIDDEN), dtype=jnp.float32), 'router_w': jax.random.normal(ks[1], (NUM_EXPERTS, HIDDEN), dtype=jnp.float32) * 0.02, 'expert_bias': jnp.zeros((NUM_EXPERTS,), dtype=jnp.float32), 'w_gate': jax.random.normal(ks[2], (NUM_EXPERTS, INTER, HIDDEN), dtype=jnp.float32) * 0.02, 'w_down': jax.random.normal(ks[3], (NUM_EXPERTS, HIDDEN, INTER), dtype=jnp.float32) * 0.02, 'w_gate_shared': jax.random.normal(ks[4], (INTER, HIDDEN), dtype=jnp.float32) * 0.02, 'w_down_shared': jax.random.normal(ks[5], (HIDDEN, INTER), dtype=jnp.float32) * 0.02}
    _L0_ffn_in = _L0_ffn_setup()
    _d = {'L0_attn_a_x': _L0_attn_a_in['x'], 'L0_attn_a_Wq': _L0_attn_a_in['Wq'], 'L0_attn_a_Wk': _L0_attn_a_in['Wk'], 'L0_attn_a_Wv': _L0_attn_a_in['Wv'], 'L0_attn_a_Wo': _L0_attn_a_in['Wo'], 'L0_attn_a_proj': _L0_attn_a_in['proj'], 'L0_attn_a_W1': _L0_attn_a_in['W1'], 'L0_attn_a_b1': _L0_attn_a_in['b1'], 'L0_attn_a_W2': _L0_attn_a_in['W2'], 'L0_attn_a_b2': _L0_attn_a_in['b2'], 'L0_attn_a_ln1_g': _L0_attn_a_in['ln1_g'], 'L0_attn_a_ln1_b': _L0_attn_a_in['ln1_b'], 'L0_attn_a_ln2_g': _L0_attn_a_in['ln2_g'], 'L0_attn_a_ln2_b': _L0_attn_a_in['ln2_b'], 'L0_attn_b_Wq': _L0_attn_b_in['Wq'], 'L0_attn_b_Wk': _L0_attn_b_in['Wk'], 'L0_attn_b_Wv': _L0_attn_b_in['Wv'], 'L0_attn_b_Wo': _L0_attn_b_in['Wo'], 'L0_attn_b_bo': _L0_attn_b_in['bo'], 'L0_ffn_router_w': _L0_ffn_in['router_w'], 'L0_ffn_expert_bias': _L0_ffn_in['expert_bias'], 'L0_ffn_w_gate': _L0_ffn_in['w_gate'], 'L0_ffn_w_down': _L0_ffn_in['w_down'], 'L0_ffn_w_gate_shared': _L0_ffn_in['w_gate_shared'], 'L0_ffn_w_down_shared': _L0_ffn_in['w_down_shared']}
    _x0 = _d['L0_attn_a_x']
    _d['L0_attn_a_x'] = jax.random.normal(jax.random.fold_in(jax.random.key(seed), 1), (4, 1024, 128), dtype=_x0.dtype)
    del _x0
    return _d

def reference(L0_attn_a_x, L0_attn_a_Wq, L0_attn_a_Wk, L0_attn_a_Wv, L0_attn_a_Wo, L0_attn_a_proj, L0_attn_a_W1, L0_attn_a_b1, L0_attn_a_W2, L0_attn_a_b2, L0_attn_a_ln1_g, L0_attn_a_ln1_b, L0_attn_a_ln2_g, L0_attn_a_ln2_b, L0_attn_b_Wq, L0_attn_b_Wk, L0_attn_b_Wv, L0_attn_b_Wo, L0_attn_b_bo, L0_ffn_router_w, L0_ffn_expert_bias, L0_ffn_w_gate, L0_ffn_w_down, L0_ffn_w_gate_shared, L0_ffn_w_down_shared):

    def _L0_attn_a_ref(x, Wq, Wk, Wv, Wo, proj, W1, b1, W2, b2, ln1_g, ln1_b, ln2_g, ln2_b):
        import jax, jax.numpy as jnp
        import numpy as np
        B, N, D = (4, 512, 128)
        H, DH = (16, 64)
        DFF = 512
        M = 64
        EPS_KERN = 1e-06
        EPS_LN = 1e-06

        def _softmax_kernel_feats(data, proj, is_query):
            dn = 1.0 / jnp.sqrt(jnp.sqrt(jnp.float32(data.shape[-1])))
            ratio = 1.0 / jnp.sqrt(jnp.float32(proj.shape[0]))
            data_dash = jnp.einsum('bnhd,md->bnhm', data * dn, proj)
            diag = jnp.sum(jnp.square(data), axis=-1, keepdims=True) * (dn * dn) / 2.0
            if is_query:
                mx = jnp.max(data_dash, axis=-1, keepdims=True)
            else:
                mx = jnp.max(data_dash)
            return ratio * (jnp.exp(data_dash - diag - mx) + EPS_KERN)

        def _layernorm(x, g, b):
            mu = jnp.mean(x, axis=-1, keepdims=True)
            var = jnp.mean(jnp.square(x - mu), axis=-1, keepdims=True)
            return (x - mu) * jax.lax.rsqrt(var + EPS_LN) * g + b

        def _encoder_forward(x, Wq, Wk, Wv, Wo, proj, W1, b1, W2, b2, ln1_g, ln1_b, ln2_g, ln2_b):
            q = jnp.einsum('bnd,dhk->bnhk', x, Wq)
            k = jnp.einsum('bnd,dhk->bnhk', x, Wk)
            v = jnp.einsum('bnd,dhk->bnhk', x, Wv)
            qf = _softmax_kernel_feats(q, proj, True)
            kf = _softmax_kernel_feats(k, proj, False)
            kv = jnp.einsum('bnhm,bnhd->bhmd', kf, v)
            num = jnp.einsum('bnhm,bhmd->bnhd', qf, kv)
            den = jnp.einsum('bnhm,bhm->bnh', qf, jnp.sum(kf, axis=1))
            attn = num / den[..., None]
            attn_out = jnp.einsum('bnhd,hdo->bno', attn, Wo)
            out1 = _layernorm(x + attn_out, ln1_g, ln1_b)
            h = jax.nn.elu(out1 @ W1 + b1)
            ffn_out = h @ W2 + b2
            return _layernorm(out1 + ffn_out, ln2_g, ln2_b)
        return _encoder_forward(x, Wq, Wk, Wv, Wo, proj, W1, b1, W2, b2, ln1_g, ln1_b, ln2_g, ln2_b)

    def _L0_attn_b_ref(x, Wq, Wk, Wv, Wo, bo):
        import jax, jax.numpy as jnp
        import numpy as np
        B, S, D, H = (4, 256, 128, 16)
        HD = D // H
        b, n, _ = x.shape

        def proj(W):
            return (x @ W.T).reshape(b, n, H, HD).transpose(0, 2, 1, 3)
        q, k, v = (proj(Wq), proj(Wk), proj(Wv))
        scores = jnp.einsum('bhqd,bhkd->bhqk', q, k)
        causal = jnp.triu(jnp.ones((n, n), dtype=bool), k=1)
        scores = jnp.where(causal, -jnp.inf, scores)
        attn = jax.nn.softmax(scores / np.sqrt(HD), axis=-1)
        ctx = jnp.einsum('bhqk,bhkd->bhqd', attn, v)
        ctx = ctx.transpose(0, 2, 1, 3).reshape(b, n, D)
        return ctx @ Wo.T + bo

    def _L0_ffn_ref(hidden_states, router_w, expert_bias, w_gate, w_down, w_gate_shared, w_down_shared):
        import jax, jax.numpy as jnp
        import numpy as np
        NUM_EXPERTS = 160
        TOP_K = 8
        ROUTED_SCALE = 2.5
        HIDDEN = 128
        INTER = 64
        B, S, H = hidden_states.shape
        x = hidden_states.reshape(-1, H)
        T = x.shape[0]
        logits = x @ router_w.T + expert_bias[None, :]
        probs = jax.nn.sigmoid(logits)
        top_w, top_idx = jax.lax.top_k(probs, TOP_K)
        top_w = top_w / (jnp.sum(top_w, axis=-1, keepdims=True) + 1e-09)
        top_w = top_w * ROUTED_SCALE
        combine = jnp.zeros((T, NUM_EXPERTS), dtype=x.dtype)
        combine = combine.at[jnp.arange(T)[:, None], top_idx].set(top_w)
        h1 = jax.nn.silu(jnp.einsum('th,eih->eti', x, w_gate))
        h1w = h1 * combine.T[:, :, None]
        routed = jnp.einsum('eti,ehi->th', h1w, w_down)
        shared = jax.nn.silu(x @ w_gate_shared.T) @ w_down_shared.T
        return (routed + shared).reshape(B, S, H)
    x = L0_attn_a_x
    x = x + _L0_attn_a_ref(_layernorm(x, axis=-1), L0_attn_a_Wq, L0_attn_a_Wk, L0_attn_a_Wv, L0_attn_a_Wo, L0_attn_a_proj, L0_attn_a_W1, L0_attn_a_b1, L0_attn_a_W2, L0_attn_a_b2, L0_attn_a_ln1_g, L0_attn_a_ln1_b, L0_attn_a_ln2_g, L0_attn_a_ln2_b)
    x = x + _L0_ffn_ref(_layernorm(x, axis=-1), L0_ffn_router_w, L0_ffn_expert_bias, L0_ffn_w_gate, L0_ffn_w_down, L0_ffn_w_gate_shared, L0_ffn_w_down_shared)
    x = x + _L0_attn_b_ref(_layernorm(x, axis=-1), L0_attn_b_Wq, L0_attn_b_Wk, L0_attn_b_Wv, L0_attn_b_Wo, L0_attn_b_bo)
    x = x + _L0_ffn_ref(_layernorm(x, axis=-1), L0_ffn_router_w, L0_ffn_expert_bias, L0_ffn_w_gate, L0_ffn_w_down, L0_ffn_w_gate_shared, L0_ffn_w_down_shared)
    return x

_drawn_inputs = setup_inputs


def setup_inputs(seed=0):
    import zlib

    import numpy as np

    out = dict(_drawn_inputs(seed))
    spreads = {'L0_attn_a_b1': (0.0, 0.339),
     'L0_attn_a_b2': (0.0, 0.1),
     'L0_attn_a_ln1_g': (1.0, 0.2),
     'L0_attn_a_ln1_b': (0.0, 0.1),
     'L0_attn_a_ln2_g': (1.0, 0.2),
     'L0_attn_a_ln2_b': (0.0, 0.1),
     'L0_attn_b_bo': (0.0, 0.1),
     'L0_ffn_expert_bias': (0.0, 0.615)}
    factors = {'L0_attn_a_Wq': 64.0,
     'L0_attn_a_Wk': 64.0,
     'L0_attn_a_Wv': 8.0,
     'L0_attn_a_Wo': 8.0,
     'L0_attn_a_proj': 64.0,
     'L0_ffn_router_w': 3.779,
     'L0_ffn_w_gate': 3.606,
     'L0_ffn_w_down': 3.585,
     'L0_ffn_w_gate_shared': 3.118,
     'L0_ffn_w_down_shared': 3.078}
    for name, (base, spread) in spreads.items():
        noise = np.random.default_rng([zlib.crc32(name.encode()), seed]).standard_normal(out[name].shape)
        drawn = base * np.exp(spread * noise) if base else spread * noise
        out[name] = jnp.asarray(drawn.astype(out[name].dtype))
    for name, factor in factors.items():
        out[name] = (out[name] * factor).astype(out[name].dtype)
    return out
```

```python
from contextlib import ExitStack

import concourse.bass as bass
import numpy as np
from concourse import mybir

F32 = mybir.dt.float32
BF16 = mybir.dt.bfloat16
I32 = mybir.dt.int32
ALU = mybir.AluOpType
ACT = mybir.ActivationFunctionType
AX = mybir.AxisListType
PE_ENGINE = [mybir.EngineType.PE]

P = 128
BATCH, SEQ, DM = 4, 1024, 128
TOKENS = BATCH * SEQ
TILES = TOKENS // P
TPB = SEQ // P
HALF = 512

HA, DH, MF = 16, 64, 64
PAIRS = HA // 2
HD = HA * DH
DFF = 512
FFC = DFF // P
EPS_KERNEL = 1e-6
EPS_LN_A = 1e-6
EPS_LN = 1e-5
DN = float(np.float32(1.0) / np.sqrt(np.sqrt(np.float32(DH))))
RATIO = float(np.float32(1.0) / np.sqrt(np.float32(MF)))

HB, WB = 16, 8
VW = 32
STACK = 9 * WB
MASKED = -1e30

EXPERTS, TOPK, INTER = 160, 8, 64
ROUTED_SCALE = 2.5
GROUP = 4
GROUPS = -(-(TOKENS * TOPK // P + EXPERTS) // GROUP)
SLOTS = GROUPS * GROUP * P
ZERO_FILLS = GROUPS // 4


class Shared:
    pass


class Memory:

    def __init__(self, nc, stage):
        self.nc, self.stage, self.ctx, self.sems = nc, stage, ExitStack(), []

    def __enter__(self):
        return self

    def __exit__(self, *a):
        self.ctx.__exit__(*a)
        self.nc.clear_and_free_semaphores(self.sems)
        self.nc.all_engine_barrier()

    def sbuf(self, name, shape, dtype=F32):
        return self.ctx.enter_context(self.nc.sbuf_tensor(f"{self.stage}_{name}", shape, dtype))

    def psum(self, name, shape, dtype=F32):
        return self.ctx.enter_context(self.nc.psum_tensor(f"{self.stage}_{name}", shape, dtype))

    def sem(self, name):
        self.sems.append(self.nc.alloc_semaphore(name=f"{self.stage}_{name}"))
        return self.sems[-1]

    def block(self):
        return self.ctx.enter_context(self.nc.Block())


def bc(ap, n):
    return ap.unsqueeze(2).to_broadcast([ap.shape[0], ap.shape[1], n])


def rsqrt(nc, out, var, eps, guess, half):
    dve = nc.vector
    dve.tensor_scalar(half, var, eps, None, ALU.add)
    dve.drain()
    dve.tensor_scalar(out.bitcast(I32), half.bitcast(I32), -0.5, float(0x5F3759DF), ALU.mult, ALU.add)
    dve.tensor_scalar(half, half, -0.5, None, ALU.mult)
    for _ in range(4):
        dve.drain()
        dve.tensor_tensor(guess, out, out, ALU.mult)
        dve.drain()
        dve.tensor_tensor(guess, guess, half, ALU.mult)
        dve.drain()
        dve.scalar_tensor_tensor(out, guess, 1.5, out, ALU.add, ALU.mult)
    dve.drain()


def setup(nc, x, G):
    with Memory(nc, "setup") as m:
        zeros = m.sbuf("zeros", [P, SLOTS // ZERO_FILLS // P * DM])
        zeros_made = m.sem("zeros_made")
        zeroed, made = m.sem("zeroed"), m.sem("made")
        x_landed = m.sem("x_landed")
        block = m.block()

        @block.sync
        def _(sp):
            sp.dma_start(G.x[:], x.rearrange("b (t p) d -> p b t d", p=P)).then_inc(x_landed, 16)
            sp.wait_ge(zeros_made, 1)
            fill = G.slots_in.rearrange("(n p j) d -> n p (j d)", n=ZERO_FILLS, p=P)
            for n in range(ZERO_FILLS):
                sp.dma_start(fill[n], zeros[:]).then_inc(G.slots_zeroed, 16)
            sp.wait_ge(x_landed, 16)
            sp.wait_ge(G.slots_zeroed, 16 * ZERO_FILLS)

        @block.vector
        def _(dve):
            nc.vector.memset(zeros[:], 0.0).then_inc(zeros_made, 1)

        @block.gpsimd
        def _(pool):
            pool.memset(G.ident[:], 0.0).then_inc(zeroed, 1)
            pool.memset(G.ones[:], 1.0)
            pool.memset(G.ratio_eps[:], RATIO * EPS_KERNEL)
            pool.wait_ge(zeroed, 1)
            pool.affine_select(out=G.ident[:], in_=G.ident[:], compare_op=ALU.not_equal, fill=1.0, base=0,
                               pattern=[[-1, P]], channel_multiplier=1).then_inc(made, 1)
            pool.wait_ge(made, 1)


def layernorm(nc, stage, G):
    with Memory(nc, stage) as m:
        stats = m.sbuf("stats", [P, TPB, 6])
        mv = m.sbuf("mv", [P, TPB, 2])
        var, half = m.sbuf("var", [P, TPB]), m.sbuf("half", [P, TPB])
        rstd = m.sbuf("rstd", [P, TPB])
        xnb = m.sbuf("xnb", [P, TPB, DM])
        ps = m.psum("ps", [P, 2, HALF])
        xn_ready = m.sem("xn_ready")
        xnb_free, turned, bank_free = m.sem("xnb_free"), m.sem("turned"), m.sem("bank_free")
        copied = m.sem("copied")
        block = m.block()

        @block.vector
        def _(dve):
            with dve.Fori(0, BATCH) as b:
                xb = G.x[:, bass.ds(b, 1), :, :].rearrange("p b t d -> p (b t) d")
                for t in range(TPB):
                    nc.vector.bn_stats(stats[:, t, :], xb[:, t, :])
                nc.vector.drain()
                for t in range(TPB):
                    nc.vector.bn_aggr(mv[:, t, :], stats[:, t, :])
                nc.vector.drain()
                rsqrt(nc, rstd[:], mv[:, :, 1], EPS_LN, var[:], half[:])
                dve.wait_ge(xnb_free, 2 * b + 2)
                for t in range(TPB):
                    last = nc.vector.tensor_scalar(xnb[:, t, :], xb[:, t, :], mv[:, t, 0:1], rstd[:, t:t + 1],
                                                   ALU.subtract, ALU.mult)
                    if t % 4 == 3:
                        last.then_inc(xn_ready, 1)

        @block.tensor
        def _(pe):
            pe.sem_inc(xnb_free, 1)
            with pe.Fori(0, BATCH) as b:
                pe.wait_ge(bank_free, 2 * b + 2)
                for u in range(2):
                    pe.wait_ge(xn_ready, 2 * b + u + 1)
                    for t in range(4):
                        last = nc.tensor.transpose(ps[:, u, t * P:(t + 1) * P], xnb[:, 4 * u + t, :], G.ident[:])
                    last.then_inc(turned, 1)
                pe.wait_ge(turned, 2 * b + 2)
                pe.sem_inc(xnb_free, 1)

        @block.scalar
        def _(act):
            act.sem_inc(bank_free, 2)
            with act.Fori(0, BATCH) as b:
                for u in range(2):
                    act.wait_ge(turned, 2 * b + u + 1)
                    nc.scalar.activation(G.xnT[:, bass.ds(b, 1), u * HALF:(u + 1) * HALF].rearrange("p b n -> p (b n)"),
                                         ps[:, u, :], ACT.Copy).then_inc(bank_free, 1)

        @block.gpsimd
        def _(pool):
            pool.sem_inc(xnb_free, 1)
            with pool.Fori(0, BATCH) as b:
                pool.wait_ge(xn_ready, 2 * b + 2)
                nc.gpsimd.tensor_copy(G.xn[:, bass.ds(b, 1), :, :].rearrange("p b t d -> p (b t) d"),
                                      xnb[:]).then_inc(copied, 1)
                pool.wait_ge(copied, b + 1)
                pool.sem_inc(xnb_free, 1)


def attn_a(nc, G, W):
    with Memory(nc, "a") as m:
        wq, wk, wv = (m.sbuf(n, [P, HD]) for n in ("wq", "wk", "wv"))
        wqT, wkT = (m.sbuf(n, [P, PAIRS, DM]) for n in ("wqT", "wkT"))
        wqp, wkp = (m.sbuf(n, [P, PAIRS, P]) for n in ("wqp", "wkp"))
        proj2 = m.sbuf("proj2", [P, P])
        wo = m.sbuf("wo", [P, PAIRS, DM])
        ngmax = m.sbuf("ngmax", [P, 1])

        with Memory(nc, "a1") as m1:
            pmax = m1.sbuf("pmax", [P, TOKENS // HALF, PAIRS])
            rowmax = m1.sbuf("rowmax", [P, 1])
            allmax = m1.sbuf("allmax", [1, 1])
            ps = m1.psum("ps", [P, 4, HALF])
            psw = m1.psum("psw", [P, 4, HALF])
            zeroed, landed = m1.sem("zeroed"), m1.sem("landed")
            proj_landed, fold_done, folded = m1.sem("proj_landed"), m1.sem("fold_done"), m1.sem("folded")
            feats, taken = m1.sem("feats"), m1.sem("taken")
            row_ready, turned, one_ready, spread = m1.sem("row_ready"), m1.sem("turned"), m1.sem("one"), m1.sem("spread")
            neg_ready = m1.sem("neg_ready")
            block = m1.block()

            @block.sync
            def _(sp):
                sp.dma_start(wkT[:], W["wkT"].rearrange("(c p) d -> p c d", p=P)).then_inc(landed, 16)
                sp.dma_start(wqT[:], W["wqT"].rearrange("(c p) d -> p c d", p=P)).then_inc(landed, 16)
                sp.wait_ge(zeroed, 1)
                for h in range(2):
                    sp.dma_start(proj2[h * DH:(h + 1) * DH, h * MF:(h + 1) * MF], W["projT"]).then_inc(proj_landed, 16)
                for dst, src in ((wq, W["wq"]), (wk, W["wk"]), (wv, W["wv"])):
                    sp.dma_start(dst[:], src.rearrange("d h k -> d (h k)")).then_inc(landed, 16)
                sp.dma_start(wo[:], W["wo"].rearrange("h k o -> (h k) o").rearrange("(c p) o -> p c o", p=P)).then_inc(landed, 16)
                sp.wait_ge(landed, 96)

            @block.gpsimd
            def _(pool):
                pool.memset(proj2[:], 0.0).then_inc(zeroed, 1)

            @block.tensor
            def _(pe):
                pe.wait_ge(landed, 32)
                pe.wait_ge(proj_landed, 32)
                for n, w in enumerate((wkT, wqT)):
                    for c in range(PAIRS):
                        last = nc.tensor.matmul(psw[:, 2 * n + c // 4, (c % 4) * P:(c % 4 + 1) * P], w[:, c, :], proj2[:],
                                                start=True, stop=True)
                    last.then_inc(fold_done, 1)
                pe.wait_ge(folded, 1)
                with pe.Fori(0, TOKENS // HALF) as g:
                    xg = G.xnT[:].rearrange("p b n -> p (b n)")[:, bass.ds(g * HALF, HALF)]
                    for c in range(PAIRS):
                        pe.wait_ge(taken, PAIRS * g + c + 1)
                        nc.tensor.matmul(ps[:, c % 4, :], wkp[:, c, :], xg, start=True, stop=True).then_inc(feats, 1)
                pe.wait_ge(row_ready, 1)
                nc.tensor.transpose(ps[0:1, 0, 0:P], rowmax[:], G.ident[:]).then_inc(turned, 1)
                pe.wait_ge(one_ready, 1)
                nc.tensor.matmul(ps[:, 1, 0:1], G.ones[0:1, :], allmax[:], start=True, stop=True).then_inc(spread, 1)

            @block.scalar
            def _(act):
                for n, w in enumerate((wkp, wqp)):
                    act.wait_ge(fold_done, n + 1)
                    nc.scalar.activation(w[:].rearrange("p c m -> p (c m)"),
                                         psw[:, 2 * n:2 * n + 2, :].rearrange("p a n -> p (a n)"), ACT.Copy,
                                         scale=DN).then_inc(folded, 1)
                act.wait_ge(folded, 2)

            @block.vector
            def _(dve):
                dve.sem_inc(taken, 4)
                with dve.Fori(0, TOKENS // HALF) as g:
                    for c in range(PAIRS):
                        dve.wait_ge(feats, PAIRS * g + c + 1)
                        nc.vector.reduce_max(pmax[:, bass.ds(g, 1), c:c + 1].rearrange("p a b -> p (a b)"),
                                             ps[:, c % 4, :], AX.X).then_inc(taken, 1)
                nc.vector.drain()
                nc.vector.reduce_max(rowmax[:], pmax[:].rearrange("p a b -> p (a b)"), AX.X).then_inc(row_ready, 1)
                dve.wait_ge(turned, 1)
                nc.vector.reduce_max(allmax[:], ps[0:1, 0, 0:P], AX.X).then_inc(one_ready, 1)
                dve.wait_ge(spread, 1)
                nc.vector.tensor_scalar(ngmax[:], ps[:, 1, 0:1], -1.0, None, ALU.mult).then_inc(neg_ready, 1)
                dve.wait_ge(neg_ready, 1)

        with Memory(nc, "a2") as m2:
            xT = m2.sbuf("xT", [P, SEQ])
            sq = m2.sbuf("sq", [P, HD])
            diag = m2.sbuf("diag", [P, HA])
            qmax = m2.sbuf("qmax", [P, HA])
            shift = m2.sbuf("shift", [P, HA])
            arg = m2.sbuf("arg", [P, 2, HD])
            qf = m2.sbuf("qf", [P, TPB, HD])
            kf = m2.sbuf("kf", [P, 2, HD])
            kfe = m2.sbuf("kfe", [P, HD])
            v = m2.sbuf("v", [P, 2, HD])
            kvbd = m2.sbuf("kvbd", [P, PAIRS, P])
            ksbd = m2.sbuf("ksbd", [P, PAIRS, P])
            qfT = m2.sbuf("qfT", [P, 2, HD])
            rden = m2.sbuf("rden", [P, 2, HALF])
            atT = m2.sbuf("atT", [P, 2, HD])
            psA = m2.psum("psA", [P, 2, HALF])
            psB = m2.psum("psB", [P, 4, HALF])
            psC = m2.psum("psC", [P, 2, HALF])
            xT_ready = m2.sem("xT_ready")
            rounds = m2.sem("rounds")
            cleared = m2.sem("cleared")
            q_done, qd_done, q_squared, q_diag, q_arg, q_exp = (m2.sem(n) for n in (
                "q_done", "qd_done", "q_squared", "q_diag", "q_arg", "q_exp"))
            k_done, kd_done, v_done, k_squared, k_diag, k_arg, k_exp, kf_ready, v_ready, kv_tile, kv_out = (
                m2.sem(n) for n in ("k_done", "kd_done", "v_done", "k_squared", "k_diag", "k_arg", "k_exp", "kf_ready",
                                    "v_ready", "kv_tile", "kv_out"))
            qT_done, qfT_ready, nd_done, at_ready, ao_done, ao_taken = (m2.sem(n) for n in (
                "qT_done", "qfT_ready", "nd_done", "at_ready", "ao_done", "ao_taken"))
            block = m2.block()
            WORKERS = 3
            heads = "p (h k) -> p h k"

            def end_round(eng):
                eng.drain()
                eng.sem_inc(rounds, 1)

            @block.gpsimd
            def _(pool):
                nc.gpsimd.memset(kvbd[:], 0.0).then_inc(cleared, 1)
                nc.gpsimd.memset(ksbd[:], 0.0).then_inc(cleared, 1)
                with pool.Fori(0, BATCH) as b:
                    pool.wait_ge(rounds, WORKERS * b + WORKERS)
                    nc.gpsimd.tensor_copy(xT[:], G.xnT[:, bass.ds(b, 1), :].rearrange("p b n -> p (b n)")).then_inc(xT_ready, 1)

            @block.tensor
            def _(pe):
                end_round(pe)
                pe.wait_ge(cleared, 2)
                with pe.Fori(0, BATCH) as b:
                    pe.wait_ge(xT_ready, b + 1)
                    for t in range(TPB):
                        xt = xT[:, t * P:(t + 1) * P]
                        if t >= 1:
                            pe.wait_ge(q_squared, TPB * b + t)
                        for u in range(2):
                            last = nc.tensor.matmul(psA[:, u, :], xt, wq[:, u * HALF:(u + 1) * HALF], start=True, stop=True)
                        last.then_inc(q_done, 1)
                        if t >= 2:
                            pe.wait_ge(q_arg, TPB * b + t - 1)
                        for u in range(2):
                            last = nc.tensor.matmul(psB[:, 2 * (t % 2) + u, :], xt,
                                                    wqp[:, 4 * u:4 * u + 4, :].rearrange("p c m -> p (c m)"), start=True, stop=True)
                        last.then_inc(qd_done, 1)
                    pe.wait_ge(q_squared, TPB * b + TPB)
                    pe.wait_ge(q_arg, TPB * b + TPB)

                    def add_kv(t):
                        pe.wait_ge(kf_ready, TPB * b + t + 1)
                        pe.wait_ge(v_ready, 2 * TPB * b + 2 * t + 2)
                        for c in range(PAIRS):
                            cols = slice(c * P, (c + 1) * P)
                            nc.tensor.matmul(psC[:, c // 4, (c % 4) * P:(c % 4 + 1) * P], kf[:, t % 2, cols], v[:, t % 2, cols],
                                             start=(t == 0 and c % 4 == 0), stop=(t == TPB - 1), skip_group_check=True)
                        for c in range(PAIRS):
                            last = nc.tensor.matmul(psB[:, 3, c:c + 1], kf[:, t % 2, c * P:(c + 1) * P], G.ones[:, 0:1],
                                                    start=(t == 0 and c == 0), stop=(t == TPB - 1), skip_group_check=True)
                        last.then_inc(kv_tile, 1)

                    for t in range(TPB):
                        xt = xT[:, t * P:(t + 1) * P]
                        for u in range(2):
                            if t + u >= 1:
                                pe.wait_ge(v_ready, 2 * TPB * b + 2 * t + u)
                            nc.tensor.matmul(psB[:, 2, :], xt, wv[:, u * HALF:(u + 1) * HALF], start=True, stop=True).then_inc(v_done, 1)
                            if u == 0:
                                if t >= 1:
                                    pe.wait_ge(k_squared, TPB * b + t)
                                for w in range(2):
                                    last = nc.tensor.matmul(psA[:, w, :], xt, wk[:, w * HALF:(w + 1) * HALF], start=True, stop=True)
                                last.then_inc(k_done, 1)
                        if t >= 1:
                            pe.wait_ge(k_arg, TPB * b + t)
                        for u in range(2):
                            last = nc.tensor.matmul(psB[:, u, :], xt, wkp[:, 4 * u:4 * u + 4, :].rearrange("p c m -> p (c m)"),
                                                    start=True, stop=True)
                        last.then_inc(kd_done, 1)
                        if t >= 1:
                            add_kv(t - 1)
                    add_kv(TPB - 1)

                    def project(t):
                        pe.wait_ge(at_ready, 2 * TPB * b + 2 * t + 2)
                        if t >= 2:
                            pe.wait_ge(ao_taken, TPB * b + t - 1)
                        for c in range(PAIRS):
                            last = nc.tensor.matmul(psC[:, t % 2, 0:DM], atT[:, t % 2, c * P:(c + 1) * P], wo[:, c, :],
                                                    start=(c == 0), stop=(c == PAIRS - 1))
                        last.then_inc(ao_done, 1)

                    pe.wait_ge(k_squared, TPB * b + TPB)
                    for t in range(TPB):
                        pe.wait_ge(q_exp, TPB * b + t + 1)
                        for u in range(2):
                            if t >= 1:
                                pe.wait_ge(qfT_ready, 2 * TPB * b + 2 * t + u - 1)
                            for c in range(4):
                                last = nc.tensor.transpose(psA[:, u, c * P:(c + 1) * P], qf[:, t, (4 * u + c) * P:(4 * u + c + 1) * P],
                                                           G.ident[:])
                            last.then_inc(qT_done, 1)
                        if t >= 1:
                            project(t - 1)
                        if t == 0:
                            pe.wait_ge(kv_out, b + 1)
                        for u in range(2):
                            pe.wait_ge(qfT_ready, 2 * TPB * b + 2 * t + u + 1)
                            if t >= 1:
                                pe.wait_ge(at_ready, 2 * TPB * b + 2 * t + u - 1)
                            for n, w in enumerate((kvbd, ksbd)):
                                for c in range(4):
                                    last = nc.tensor.matmul(psB[:, 2 * u + n, c * P:(c + 1) * P], w[:, 4 * u + c, :],
                                                            qfT[:, t % 2, (4 * u + c) * P:(4 * u + c + 1) * P], start=True, stop=True)
                            last.then_inc(nd_done, 1)
                    project(TPB - 1)
                    end_round(pe)

            @block.scalar
            def _(act):
                end_round(act)
                with act.Fori(0, BATCH) as b:
                    act.wait_ge(rounds, WORKERS * b + WORKERS)
                    both = "p a n -> p (a n)"

                    def q_features(t):
                        act.wait_ge(q_arg, TPB * b + t + 1)
                        nc.scalar.activation(qf[:, t, :], arg[:, t % 2, :], ACT.Exp).then_inc(q_exp, 1)

                    for t in range(TPB):
                        act.wait_ge(q_done, TPB * b + t + 1)
                        if t >= 1:
                            act.wait_ge(q_diag, TPB * b + t)
                        nc.scalar.activation(sq[:], psA[:].rearrange(both), ACT.Square).then_inc(q_squared, 1)
                        if t >= 1:
                            q_features(t - 1)
                    q_features(TPB - 1)

                    def k_features(t):
                        act.wait_ge(k_arg, TPB * b + t + 1)
                        if t >= 1:
                            act.wait_ge(kf_ready, TPB * b + t)
                        nc.scalar.activation(kfe[:], arg[:, t % 2, :], ACT.Exp, bias=ngmax[:]).then_inc(k_exp, 1)

                    for t in range(TPB):
                        for u in range(2):
                            act.wait_ge(v_done, 2 * TPB * b + 2 * t + u + 1)
                            if u == 0 and t >= 2:
                                act.wait_ge(kv_tile, TPB * b + t - 1)
                            nc.scalar.activation(v[:, t % 2, u * HALF:(u + 1) * HALF], psB[:, 2, :], ACT.Copy).then_inc(v_ready, 1)
                            if u == 0:
                                act.wait_ge(k_done, TPB * b + t + 1)
                                if t >= 1:
                                    act.wait_ge(k_diag, TPB * b + t)
                                else:
                                    act.wait_ge(q_diag, TPB * b + TPB)
                                nc.scalar.activation(sq[:], psA[:].rearrange(both), ACT.Square).then_inc(k_squared, 1)
                        if t >= 1:
                            k_features(t - 1)
                    k_features(TPB - 1)
                    for t in range(TPB):
                        for u in range(2):
                            act.wait_ge(qT_done, 2 * TPB * b + 2 * t + u + 1)
                            if t >= 2:
                                act.wait_ge(nd_done, 2 * TPB * b + 2 * t + u - 3)
                            nc.scalar.activation(qfT[:, t % 2, u * HALF:(u + 1) * HALF], psA[:, u, :], ACT.Identity,
                                                 bias=G.ratio_eps[:], scale=RATIO).then_inc(qfT_ready, 1)
                    end_round(act)

            @block.vector
            def _(dve):
                end_round(dve)
                with dve.Fori(0, BATCH) as b:
                    dve.wait_ge(rounds, WORKERS * b + WORKERS)
                    xnb = G.xn[:, bass.ds(b, 1), :, :].rearrange("p b t d -> p (b t) d")
                    both = "p a (h k) -> p (a h) k"
                    for t in range(TPB):
                        dve.wait_ge(q_squared, TPB * b + t + 1)
                        nc.vector.reduce_sum(diag[:], sq[:].rearrange(heads, k=DH), AX.X).then_inc(q_diag, 1)
                        dve.wait_ge(qd_done, TPB * b + t + 1)
                        dash = psB[:, 2 * (t % 2):2 * (t % 2) + 2, :].rearrange(both, k=MF)
                        nc.vector.reduce_max(qmax[:], dash, AX.X)
                        nc.vector.drain()
                        nc.vector.scalar_tensor_tensor(shift[:], diag[:], DN * DN / 2.0, qmax[:], ALU.mult, ALU.add)
                        nc.vector.drain()
                        if t >= 2:
                            dve.wait_ge(q_exp, TPB * b + t - 1)
                        nc.vector.tensor_tensor(arg[:, t % 2, :].rearrange(heads, k=MF), dash, bc(shift[:], MF),
                                                ALU.subtract).then_inc(q_arg, 1)

                    def k_features(t):
                        dve.wait_ge(k_exp, TPB * b + t + 1)
                        if t >= 2:
                            dve.wait_ge(kv_tile, TPB * b + t - 1)
                        nc.vector.tensor_scalar(kf[:, t % 2, :], kfe[:], EPS_KERNEL, RATIO, ALU.add, ALU.mult).then_inc(kf_ready, 1)

                    for t in range(TPB):
                        dve.wait_ge(k_squared, TPB * b + t + 1)
                        nc.vector.reduce_sum(diag[:], sq[:].rearrange(heads, k=DH), AX.X).then_inc(k_diag, 1)
                        nc.vector.drain()
                        nc.vector.tensor_scalar(shift[:], diag[:], DN * DN / 2.0, None, ALU.mult)
                        nc.vector.drain()
                        dve.wait_ge(kd_done, TPB * b + t + 1)
                        if t >= 2:
                            dve.wait_ge(k_exp, TPB * b + t - 1)
                        else:
                            dve.wait_ge(q_exp, TPB * b + TPB - 1 + t)
                        nc.vector.tensor_tensor(arg[:, t % 2, :].rearrange(heads, k=MF), psB[:, 0:2, :].rearrange(both, k=MF),
                                                bc(shift[:], MF), ALU.subtract).then_inc(k_arg, 1)
                        if t >= 1:
                            k_features(t - 1)
                    k_features(TPB - 1)
                    dve.wait_ge(kv_tile, TPB * b + TPB)
                    for h in range(2):
                        rows, cols = slice(h * DH, (h + 1) * DH), slice(h * DH, (h + 1) * DH)
                        nc.vector.tensor_copy(kvbd[rows, :, cols],
                                              psC[rows, :, :].rearrange("p a (c n) -> p (a c) n", n=P)[:, :, cols])
                        last = nc.vector.tensor_copy(ksbd[rows, :, cols], bc(psB[rows, 3, 0:PAIRS], DH))
                    last.then_inc(kv_out, 1)

                    def add_out(t):
                        dve.wait_ge(ao_done, TPB * b + t + 1)
                        nc.vector.tensor_tensor(xnb[:, t, :], xnb[:, t, :], psC[:, t % 2, 0:DM], ALU.add).then_inc(ao_taken, 1)

                    for t in range(TPB):
                        for u in range(2):
                            dve.wait_ge(nd_done, 2 * TPB * b + 2 * t + u + 1)
                            nc.vector.reciprocal(rden[:, u, :], psB[:, 2 * u + 1, :])
                            nc.vector.drain()
                            if t >= 2 and u == 0:
                                dve.wait_ge(ao_done, TPB * b + t - 1)
                            nc.vector.tensor_tensor(atT[:, t % 2, u * HALF:(u + 1) * HALF], psB[:, 2 * u, :], rden[:, u, :],
                                                    ALU.mult).then_inc(at_ready, 1)
                        if t >= 1:
                            add_out(t - 1)
                    add_out(TPB - 1)
                    end_round(dve)


def ffn_a(nc, G, W):
    with Memory(nc, "f") as m:
        w1 = m.sbuf("w1", [P, DFF])
        w2 = m.sbuf("w2", [P, FFC, DM])
        b1 = m.sbuf("b1", [P, FFC])
        g1, o1b, b2, g2, o2b = (m.sbuf(n, [P, DM]) for n in ("g1", "o1b", "b2", "g2", "o2b"))
        stats = m.sbuf("stats", [P, TPB, 6])
        mv = m.sbuf("mv", [P, TPB, 2])
        rstd, var, half = (m.sbuf(n, [P, TPB]) for n in ("rstd", "var", "half"))
        o = m.sbuf("o", [P, TPB, DM])
        oT = m.sbuf("oT", [P, 2, HALF])
        ex = m.sbuf("ex", [P, 2, FFC, HALF])
        hT = m.sbuf("hT", [P, 2, FFC, HALF])
        y = m.sbuf("y", [P, TPB, DM])
        psT = m.psum("psT", [P, 2, HALF])
        psH = m.psum("psH", [P, FFC, HALF])
        psY = m.psum("psY", [P, 2, HALF])
        landed, rounds = m.sem("landed"), m.sem("rounds")
        o_ready, turned, oT_ready, h_done, e_ready, h_taken, hT_ready, y_done = (m.sem(n) for n in (
            "o_ready", "turned", "oT_ready", "h_done", "e_ready", "h_taken", "hT_ready", "y_done"))
        block = m.block()
        WORKERS = 3
        LOADS = 8

        def end_round(eng):
            eng.drain()
            eng.sem_inc(rounds, 1)

        @block.sync
        def _(sp):
            sp.dma_start(w1[:], W["w1"]).then_inc(landed, 16)
            sp.dma_start(w2[:], W["w2"].rearrange("(c p) o -> p c o", p=P)).then_inc(landed, 16)
            sp.dma_start(b1[:], W["b1"]).then_inc(landed, 16)
            for dst, src in ((g1, W["ln1_g"]), (o1b, W["ln1_b"]), (b2, W["b2"]), (g2, W["ln2_g"]), (o2b, W["ln2_b"])):
                sp.dma_start(dst[:], src.unsqueeze(0).to_broadcast([P, DM])).then_inc(landed, 16)
            sp.wait_ge(landed, 16 * LOADS)

        @block.tensor
        def _(pe):
            end_round(pe)
            pe.wait_ge(landed, 16 * LOADS)
            with pe.Fori(0, BATCH) as b:
                pe.wait_ge(rounds, WORKERS * b + WORKERS)

                def up(u):
                    pe.wait_ge(oT_ready, 2 * b + u + 1)
                    for c in range(FFC):
                        if u == 1:
                            pe.wait_ge(h_taken, 2 * FFC * b + c + 1)
                        nc.tensor.matmul(psH[:, c, :], w1[:, c * P:(c + 1) * P], oT[:, u, :], start=True, stop=True).then_inc(h_done, 1)

                def down(u):
                    pe.wait_ge(hT_ready, 2 * b + u + 1)
                    for t in range(4):
                        for c in range(FFC):
                            last = nc.tensor.matmul(psY[:, u, t * DM:(t + 1) * DM], hT[:, u, c, t * P:(t + 1) * P], w2[:, c, :],
                                                    start=(c == 0), stop=(c == FFC - 1))
                    last.then_inc(y_done, 1)

                for u in range(2):
                    pe.wait_ge(o_ready, 2 * b + u + 1)
                    for t in range(4):
                        last = nc.tensor.transpose(psT[:, u, t * P:(t + 1) * P], o[:, 4 * u + t, :], G.ident[:])
                    last.then_inc(turned, 1)
                up(0)
                up(1)
                down(0)
                down(1)
                end_round(pe)

        @block.scalar
        def _(act):
            end_round(act)
            act.wait_ge(landed, 16 * LOADS)
            with act.Fori(0, BATCH) as b:
                act.wait_ge(rounds, WORKERS * b + WORKERS)
                for u in range(2):
                    act.wait_ge(turned, 2 * b + u + 1)
                    nc.scalar.activation(oT[:, u, :], psT[:, u, :], ACT.Copy).then_inc(oT_ready, 1)
                for u in range(2):
                    for c in range(FFC):
                        act.wait_ge(h_done, 2 * FFC * b + FFC * u + c + 1)
                        nc.scalar.activation(ex[:, u, c, :], psH[:, c, :], ACT.Exp, bias=b1[:, c:c + 1])
                        last = nc.scalar.activation(hT[:, u, c, :], psH[:, c, :], ACT.Relu, bias=b1[:, c:c + 1])
                        last.then_inc(h_taken, 1)
                end_round(act)

        @block.vector
        def _(dve):
            end_round(dve)
            dve.wait_ge(landed, 16 * LOADS)

            def normalize(rows, out, gain, offset, ready):
                for t in range(TPB):
                    nc.vector.bn_stats(stats[:, t, :], rows[:, t, :])
                nc.vector.drain()
                for t in range(TPB):
                    nc.vector.bn_aggr(mv[:, t, :], stats[:, t, :])
                nc.vector.drain()
                rsqrt(nc, rstd[:], mv[:, :, 1], EPS_LN_A, var[:], half[:])
                for t in range(TPB):
                    nc.vector.scalar_tensor_tensor(y[:, t, :], rows[:, t, :], mv[:, t, 0:1], gain[:], ALU.subtract, ALU.mult)
                nc.vector.drain()
                for t in range(TPB):
                    last = nc.vector.scalar_tensor_tensor(out[:, t, :], y[:, t, :], rstd[:, t:t + 1], offset[:], ALU.mult, ALU.add)
                    if ready is not None and t % 4 == 3:
                        last.then_inc(ready, 1)
                nc.vector.drain()

            with dve.Fori(0, BATCH) as b:
                dve.wait_ge(rounds, WORKERS * b + WORKERS)
                xb = G.x[:, bass.ds(b, 1), :, :].rearrange("p b t d -> p (b t) d")
                xnb = G.xn[:, bass.ds(b, 1), :, :].rearrange("p b t d -> p (b t) d")
                normalize(xnb, o, g1, o1b, o_ready)
                nc.vector.tensor_tensor(y[:], o[:], b2[:].unsqueeze(1).to_broadcast([P, TPB, DM]), ALU.add)
                for u in range(2):
                    dve.wait_ge(h_taken, 2 * FFC * b + FFC * u + FFC)
                    nc.vector.tensor_scalar(ex[:, u, :, :], ex[:, u, :, :], 1.0, -1.0, ALU.min, ALU.add)
                    nc.vector.drain()
                    nc.vector.tensor_tensor(hT[:, u, :, :], hT[:, u, :, :], ex[:, u, :, :], ALU.add).then_inc(hT_ready, 1)
                for u in range(2):
                    dve.wait_ge(y_done, 2 * b + u + 1)
                    nc.vector.tensor_tensor(o[:, 4 * u:4 * u + 4, :], y[:, 4 * u:4 * u + 4, :],
                                            psY[:, u, :].rearrange("p (t d) -> p t d", d=DM), ALU.add)
                nc.vector.drain()
                normalize(o, o, g2, o2b, None)
                nc.vector.tensor_tensor(xb, xb, o[:], ALU.add)
                end_round(dve)


def moe(nc, stage, G, W):
    with Memory(nc, stage) as m:
        L = Shared()
        L.w8 = m.sbuf("w8", [P, TILES, TOPK])
        L.place = m.sbuf("place", [P, TILES, TOPK], I32)
        L.wg = m.sbuf("wg", [P, EXPERTS, INTER])
        L.tile_expert = m.sbuf("tile_expert", [1, 4 * P], I32)
        L.wg_landed, L.shared_landed = m.sem("wg_landed"), m.sem("shared_landed")
        with Memory(nc, stage + "r") as r:
            normed(G, r)
            L.wgs = r.sbuf("wgs", [P, INTER])
            L.wds = r.sbuf("wds", [INTER, DM])
            L.picked = r.sbuf("picked", [P, TILES, EXPERTS], BF16)
            L.before = r.sbuf("before", [P, TILES + 1, EXPERTS], BF16)
            L.index = r.sbuf("index", [P, TILES, TOPK])
            L.earlier = r.sbuf("earlier", [P, P], BF16)
            L.ones_bf = r.sbuf("ones_bf", [P, P], BF16)
            L.base = r.sbuf("base", [P, EXPERTS])
            L.column = r.sbuf("column", [P, EXPERTS])
            layernorm(nc, stage + "0", G)
            router(nc, stage + "1", G, W, L)
            plan(nc, stage + "2", G, L)
            dispatch(nc, stage + "3", G, L)
        experts(nc, stage + "4", G, W, L)
        combine(nc, stage + "5", G, L)


def router(nc, stage, G, W, L):
    w8, picked, before, index = L.w8, L.picked, L.before, L.index
    with Memory(nc, stage) as m:
        wr = m.sbuf("wr", [P, EXPERTS])
        bias = m.sbuf("bias", [P, EXPERTS])
        xT = m.sbuf("xT", [P, SEQ])
        probs = m.sbuf("probs", [P, TPB, EXPERTS])
        marked = m.sbuf("marked", [P, TPB, EXPERTS])
        logits = m.sbuf("logits", [P, TPB, EXPERTS])
        top = m.sbuf("top", [P, TPB, TOPK])
        at = m.sbuf("at", [P, TPB, TOPK], mybir.dt.uint32)
        total, inverse = m.sbuf("total", [P, TPB]), m.sbuf("inverse", [P, TPB])
        scratch = m.sbuf("scratch", [P, 1])
        ps = m.psum("ps", [P, TPB // 2, 2, HALF // 2])
        landed, rounds, xT_ready, logits_done, logits_ready, probs_ready = (m.sem(n) for n in (
            "landed", "rounds", "xT_ready", "logits_done", "logits_ready", "probs_ready"))
        block = m.block()
        WORKERS = 3

        def end_round(eng):
            eng.drain()
            eng.sem_inc(rounds, 1)

        @block.sync
        def _(sp):
            sp.dma_start(wr[:], W["routerT"]).then_inc(landed, 16)
            sp.dma_start(bias[:], W["expert_bias"].unsqueeze(0).to_broadcast([P, EXPERTS])).then_inc(landed, 16)
            sp.dma_start(L.wgs[:], W["w_gate_sharedT"]).then_inc(L.shared_landed, 16)
            sp.dma_start(L.wds[:], W["w_down_sharedT"]).then_inc(L.shared_landed, 16)
            sp.dma_start(L.wg[:], W["w_gateT"]).then_inc(L.wg_landed, 16)
            sp.wait_ge(landed, 32)

        @block.gpsimd
        def _(pool):
            with pool.Fori(0, BATCH) as b:
                pool.wait_ge(rounds, WORKERS * b + WORKERS)
                nc.gpsimd.tensor_copy(xT[:], G.xnT[:, bass.ds(b, 1), :].rearrange("p b n -> p (b n)")).then_inc(xT_ready, 1)

        @block.tensor
        def _(pe):
            end_round(pe)
            pe.wait_ge(landed, 32)
            with pe.Fori(0, BATCH) as b:
                pe.wait_ge(xT_ready, b + 1)
                for t in range(TPB):
                    last = nc.tensor.matmul(ps[:, t // 2, t % 2, 0:EXPERTS], xT[:, t * P:(t + 1) * P], wr[:], start=True, stop=True)
                last.then_inc(logits_done, 1)
                end_round(pe)

        @block.scalar
        def _(act):
            end_round(act)
            with act.Fori(0, BATCH) as b:
                act.wait_ge(logits_ready, b + 1)
                nc.scalar.activation(probs[:], logits[:], ACT.Sigmoid).then_inc(probs_ready, 1)
                end_round(act)

        @block.vector
        def _(dve):
            nc.vector.memset(before[:, 0, :], 0.0)
            end_round(dve)
            dve.wait_ge(landed, 32)
            with dve.Fori(0, BATCH) as b:
                dve.wait_ge(rounds, WORKERS * b + WORKERS)
                dve.wait_ge(logits_done, b + 1)
                nc.vector.tensor_tensor(logits[:], ps[:, :, :, 0:EXPERTS].rearrange("p a b e -> p (a b) e"),
                                        bias[:].unsqueeze(1).to_broadcast([P, TPB, EXPERTS]), ALU.add).then_inc(logits_ready, 1)
                dve.wait_ge(probs_ready, b + 1)
                nc.vector.memset(scratch[:], 0.0)
                for t in range(TPB):
                    nc.vector.max(top[:, t, :], probs[:, t, :])
                nc.vector.drain()
                for t in range(TPB):
                    nc.vector.max_index(at[:, t, :], top[:, t, :], probs[:, t, :])
                nc.vector.drain()
                for t in range(TPB):
                    nc.vector.match_replace(marked[:, t, :], top[:, t, :], probs[:, t, :], -1.0)
                nc.vector.tensor_copy(index[:, bass.ds(b * TPB, TPB), :], at[:])
                nc.vector.reduce_sum(total[:], top[:], AX.X)
                nc.vector.drain()
                nc.vector.tensor_scalar(total[:], total[:], 1e-9, None, ALU.add)
                nc.vector.tensor_scalar(picked[:, bass.ds(b * TPB, TPB), :], marked[:], 0.0, None, ALU.is_lt)
                nc.vector.drain()
                nc.vector.reciprocal(inverse[:], total[:])
                for t in range(TPB):
                    nc.vector.tensor_tensor(before[:, bass.ds(b * TPB + t + 1, 1), :], before[:, bass.ds(b * TPB + t, 1), :],
                                            picked[:, bass.ds(b * TPB + t, 1), :], ALU.add)
                    nc.vector.drain()
                nc.vector.scalar_tensor_tensor(w8[:, bass.ds(b * TPB, TPB), :], top[:], ROUTED_SCALE, bc(inverse[:], TOPK),
                                               ALU.mult, ALU.mult)
                end_round(dve)


def plan(nc, stage, G, L):
    before, base, ones_bf, earlier, column, tile_expert = L.before, L.base, L.ones_bf, L.earlier, L.column, L.tile_expert
    with Memory(nc, stage) as m:
        count = m.sbuf("count", [P, EXPERTS], I32)
        tiles = m.sbuf("tiles", [P, EXPERTS])
        ends = m.sbuf("ends", [P, 2, EXPERTS])
        junk = m.sbuf("junk", [P, EXPERTS])
        number = m.sbuf("number", [P, 4], I32)
        number_f = m.sbuf("number_f", [P, 4])
        owner = m.sbuf("owner", [P, 4])
        owner_i = m.sbuf("owner_i", [P, 4], I32)
        ps = m.psum("ps", [P, HALF])
        made, counted, owned, written, back = (m.sem(n) for n in ("made", "counted", "owned", "written", "back"))
        block = m.block()

        @block.gpsimd
        def _(pool):
            nc.gpsimd.iota(number[:], [[P, 4]], base=0, channel_multiplier=1)
            nc.gpsimd.iota(column[:], [[1, EXPERTS]], base=0, channel_multiplier=0, allow_small_or_imprecise_dtypes=True)
            nc.gpsimd.memset(ones_bf[:], 1.0).then_inc(made, 1)
            pool.wait_ge(made, 1)
            nc.gpsimd.affine_select(out=earlier[:], in_=ones_bf[:], compare_op=ALU.is_gt, fill=0.0, base=0,
                                    pattern=[[1, P]], channel_multiplier=-1).then_inc(made, 1)
            pool.wait_ge(made, 2)

        @block.tensor
        def _(pe):
            pe.wait_ge(made, 1)
            nc.tensor.matmul(ps[:, 0:EXPERTS], ones_bf[:], before[:, TILES, :], start=True, stop=True).then_inc(counted, 1)

        @block.vector
        def _(dve):
            dve.wait_ge(made, 2)
            nc.vector.tensor_copy(number_f[:], number[:])
            dve.wait_ge(counted, 1)
            nc.vector.tensor_scalar(count[:], ps[:, 0:EXPERTS], float(P - 1), None, ALU.add)
            nc.vector.drain()
            nc.vector.tensor_scalar(count[:], count[:], P.bit_length() - 1, None, ALU.arith_shift_right)
            nc.vector.drain()
            nc.vector.tensor_copy(tiles[:], count[:])
            nc.vector.tensor_copy(ends[:, 0, :], count[:])
            nc.vector.drain()
            step, now = 1, 0
            while step < EXPERTS:
                nc.vector.tensor_copy(ends[:, 1 - now, 0:step], ends[:, now, 0:step])
                nc.vector.tensor_tensor(ends[:, 1 - now, step:], ends[:, now, step:], ends[:, now, 0:EXPERTS - step], ALU.add)
                nc.vector.drain()
                step, now = 2 * step, 1 - now
            nc.vector.tensor_tensor(base[:], ends[:, now, :], tiles[:], ALU.subtract)
            nc.vector.drain()
            nc.vector.tensor_scalar(base[:], base[:], float(P), None, ALU.mult)
            for j in range(4):
                nc.vector.tensor_scalar(junk[:], ends[:, now, :], number_f[:, j:j + 1], 0.0, ALU.is_le, ALU.add,
                                        accum_out=owner[:, j:j + 1])
                nc.vector.drain()
            nc.vector.tensor_scalar(owner_i[:], owner[:], float(EXPERTS - 1), None, ALU.min).then_inc(owned, 1)

        @block.sync
        def _(sp):
            sp.wait_ge(owned, 1)
            for j in range(4):
                sp.dma_start(G.owner_dram[j * P:(j + 1) * P, :], owner_i[:, j:j + 1]).then_inc(written, 16)
            sp.wait_ge(written, 64)
            sp.dma_start(tile_expert[:], G.owner_dram.rearrange("t a -> a t")).then_inc(back, 16)
            sp.wait_ge(back, 16)


def dispatch(nc, stage, G, L):
    picked, before, base, index, column, place = L.picked, L.before, L.base, L.index, L.column, L.place
    earlier, ones_bf, wgs, wds = L.earlier, L.ones_bf, L.wgs, L.wds
    with Memory(nc, stage) as m:
        rank = m.sbuf("rank", [P, TPB, EXPERTS])
        junk = m.sbuf("junk", [P, TOPK, EXPERTS])
        slot = m.sbuf("slot", [P, TPB, TOPK])
        slot_i, low = m.sbuf("slot_i", [P, TPB, TOPK], I32), m.sbuf("low", [P, TPB, TOPK], I32)
        hs = m.sbuf("hs", [INTER, 2, HALF])
        ps = m.psum("ps", [P, TPB // 2, 2, HALF // 2])
        psh = m.psum("psh", [P, 2, HALF])
        pss = m.psum("pss", [P, 2, HALF])
        rounds, ranked, placed, scattered, up_done, hs_ready, shared_done = (m.sem(n) for n in (
            "rounds", "ranked", "placed", "scattered", "up_done", "hs_ready", "shared_done"))
        block = m.block()
        WORKERS = 3

        def end_round(eng):
            eng.drain()
            eng.sem_inc(rounds, 1)

        @block.tensor
        def _(pe):
            end_round(pe)
            pe.wait_ge(L.shared_landed, 32)
            with pe.Fori(0, BATCH) as b:
                pe.wait_ge(rounds, WORKERS * b + WORKERS)
                for t in range(TPB):
                    out = ps[:, t // 2, t % 2, 0:EXPERTS]
                    nc.tensor.matmul(out, earlier[:], picked[:, bass.ds(b * TPB + t, 1), :].rearrange("p a e -> p (a e)"),
                                     start=True, stop=False)
                    last = nc.tensor.matmul(out, ones_bf[:], before[:, bass.ds(b * TPB + t, 1), :].rearrange("p a e -> p (a e)"),
                                            start=False, stop=True)
                last.then_inc(ranked, 1)
                for u in range(2):
                    nc.tensor.matmul(psh[0:INTER, u, :], wgs[:],
                                     G.xnT[:, bass.ds(b, 1), u * HALF:(u + 1) * HALF].rearrange("p b n -> p (b n)"),
                                     start=True, stop=True).then_inc(up_done, 1)
                for u in range(2):
                    pe.wait_ge(hs_ready, 2 * b + u + 1)
                    for t in range(4):
                        last = nc.tensor.matmul(pss[:, u, t * DM:(t + 1) * DM], hs[:, u, t * P:(t + 1) * P], wds[:], start=True, stop=True)
                    last.then_inc(shared_done, 1)
                end_round(pe)

        @block.scalar
        def _(act):
            end_round(act)
            with act.Fori(0, BATCH) as b:
                for u in range(2):
                    act.wait_ge(up_done, 2 * b + u + 1)
                    nc.scalar.activation(hs[:, u, :], psh[0:INTER, u, :], ACT.Silu).then_inc(hs_ready, 1)
                end_round(act)

        @block.vector
        def _(dve):
            end_round(dve)
            with dve.Fori(0, BATCH) as b:
                dve.wait_ge(rounds, WORKERS * b + WORKERS)
                dve.wait_ge(ranked, b + 1)
                nc.vector.tensor_tensor(rank[:], ps[:, :, :, 0:EXPERTS].rearrange("p a b e -> p (a b) e"),
                                        base[:].unsqueeze(1).to_broadcast([P, TPB, EXPERTS]), ALU.add)
                nc.vector.drain()
                ib = index[:, bass.ds(b * TPB, TPB), :]
                for t in range(TPB):
                    for k in range(TOPK):
                        nc.vector.scalar_tensor_tensor(junk[:, k, :], column[:], ib[:, t, k:k + 1], rank[:, t, :],
                                                       ALU.is_equal, ALU.mult, accum_out=slot[:, t, k:k + 1])
                    nc.vector.drain()
                nc.vector.tensor_copy(slot_i[:], slot[:])
                nc.vector.drain()
                pb = place[:, bass.ds(b * TPB, TPB), :]
                nc.vector.tensor_scalar(low[:], slot_i[:], P - 1, 2, ALU.bitwise_and, ALU.logical_shift_left)
                nc.vector.tensor_scalar(pb, slot_i[:], 7, 3, ALU.logical_shift_right, ALU.bitwise_and)
                nc.vector.drain()
                nc.vector.tensor_scalar(slot_i[:], slot_i[:], ~(GROUP * P - 1), None, ALU.bitwise_and)
                nc.vector.tensor_tensor(pb, pb, low[:], ALU.bitwise_or)
                nc.vector.drain()
                nc.vector.tensor_tensor(pb, pb, slot_i[:], ALU.bitwise_or).then_inc(placed, 1)
                xb = G.x[:, bass.ds(b, 1), :, :].rearrange("p b t d -> p (b t) d")
                for u in range(2):
                    dve.wait_ge(shared_done, 2 * b + u + 1)
                    nc.vector.tensor_tensor(xb[:, 4 * u:4 * u + 4, :], xb[:, 4 * u:4 * u + 4, :],
                                            pss[:, u, :].rearrange("p (t d) -> p t d", d=DM), ALU.add)
                end_round(dve)

        @block.gpsimd
        def _(pool):
            pool.wait_ge(G.slots_zeroed, 16 * ZERO_FILLS)
            for t in range(TILES):
                if t % TPB == 0:
                    pool.wait_ge(placed, t // TPB + 1)
                for k in range(TOPK):
                    nc.gpsimd.indirect_dma_start(G.slots_in, bass.IndirectOffsetOnAxis(place[:, t, k:k + 1], 0),
                                                 G.xn[:, t // TPB, t % TPB, :], None).then_inc(scattered, 16)
            pool.wait_ge(scattered, 16 * TILES * TOPK)


def experts(nc, stage, G, W, L):
    tile_expert = L.tile_expert
    DEEP = 4
    PEEL = 3
    assert (GROUPS - 1 - PEEL) % DEEP == 0
    with Memory(nc, stage) as m:
        wd = m.sbuf("wd", [INTER, EXPERTS, DM])
        wg2, wd2 = L.wg[:].rearrange("p e i -> p (e i)"), wd[:].rearrange("p e d -> p (e d)")
        wd_landed = m.sem("wd_landed")
        rows = m.sbuf("rows", [P, DEEP, GROUP, DM])
        xT = m.sbuf("xT", [P, 2, HALF])
        h = m.sbuf("h", [P, 2, GROUP, INTER])
        hT = m.sbuf("hT", [INTER, 2, HALF])
        y = m.sbuf("y", [P, DEEP, GROUP, DM])
        psX = m.psum("psX", [P, 2, HALF])
        psH = m.psum("psH", [P, 2, HALF])
        psT = m.psum("psT", [P, 2, HALF])
        psY = m.psum("psY", [P, 2, HALF])
        rows_landed = [m.sem(f"rows_landed{i}") for i in range(DEEP)]
        stored = [m.sem(f"stored{i}") for i in range(DEEP)]
        x_turned, xT_ready, up_done, h_ready, h_turned, hT_ready, down_done, y_ready = (m.sem(n) for n in (
            "x_turned", "xT_ready", "up_done", "h_ready", "h_turned", "hT_ready", "down_done", "y_ready"))
        AHEAD = 2
        block = m.block()
        src = G.slots_in.rearrange("(g p j) d -> g p (j d)", p=P, j=GROUP)
        dst = G.slots_out.rearrange("(g p j) d -> g p (j d)", p=P, j=GROUP)
        flat = "p j d -> p (j d)"

        def done(g):
            return g + 1 + AHEAD

        def group_loop(eng, step):
            for g in range(PEEL):
                step(g, g)
            with eng.Fori(0, (GROUPS - 1 - PEEL) // DEEP) as i:
                for u in range(DEEP):
                    step(i * DEEP + PEEL + u, PEEL + u)
            step(GROUPS - 1, GROUPS - 1)

        @block.sync
        def _(sp):
            def load(g, u):
                sp.dma_start(rows[:, u % DEEP, :, :].rearrange(flat),
                             (src[g] if isinstance(g, int) else src[bass.ds(g, 1)].rearrange("g p n -> (g p) n"))
                             ).then_inc(rows_landed[u % DEEP], 16)

            def store(g, u):
                sp.wait_ge(y_ready, done(g))
                sp.dma_start((dst[g] if isinstance(g, int) else dst[bass.ds(g, 1)].rearrange("g p n -> (g p) n")),
                             y[:, u % DEEP, :, :].rearrange(flat)).then_inc(stored[u % DEEP], 16)

            for s in stored:
                sp.sem_inc(s, 16)
            for g in range(DEEP):
                load(g, g)
            sp.dma_start(wd[:], W["w_downT"]).then_inc(wd_landed, 16)
            with sp.Fori(0, GROUPS // DEEP - 1) as i:
                for u in range(DEEP):
                    sp.wait_ge(x_turned, done(i * DEEP + u))
                    load(i * DEEP + DEEP + u, u)
                    store(i * DEEP + u, u)
            for u in range(DEEP):
                store(GROUPS - DEEP + u, u)
            for s in stored:
                sp.wait_ge(s, 16 * (GROUPS // DEEP + 1))

        @block.tensor
        def _(pe):
            for s in (x_turned, up_done, h_turned, down_done):
                pe.sem_inc(s, AHEAD)
            pe.wait_ge(L.wg_landed, 16)

            def turn(g, u, landings):
                pe.wait_ge(rows_landed[u % DEEP], 16 * landings)
                pe.wait_ge(xT_ready, done(g - 2))
                for j in range(GROUP):
                    last = nc.tensor.transpose(psX[:, u % 2, j * P:(j + 1) * P], rows[:, u % DEEP, j, :], G.ident[:])
                last.then_inc(x_turned, 1)

            def up(g, u, e):
                pe.wait_ge(xT_ready, done(g))
                pe.wait_ge(h_ready, done(g - 2))
                for j in range(GROUP):
                    last = nc.tensor.matmul(psH[:, u % 2, j * INTER:(j + 1) * INTER], xT[:, u % 2, j * P:(j + 1) * P],
                                            wg2[:, bass.ds(e[j] * INTER, INTER)], start=True, stop=True)
                last.then_inc(up_done, 1)

            def turn_h(g, u):
                pe.wait_ge(L.wg_landed, 16)
                pe.wait_ge(h_ready, done(g))
                pe.wait_ge(hT_ready, done(g - 2))
                for j in range(GROUP):
                    last = nc.tensor.transpose(psT[0:INTER, u % 2, j * P:(j + 1) * P], h[:, u % 2, j, :], G.ident[:])
                last.then_inc(h_turned, 1)

            def down(g, u, e):
                pe.wait_ge(hT_ready, done(g))
                pe.wait_ge(y_ready, done(g - 2))
                for j in range(GROUP):
                    last = nc.tensor.matmul(psY[:, u % 2, j * DM:(j + 1) * DM], hT[:, u % 2, j * P:(j + 1) * P],
                                            wd2[:, bass.ds(e[j] * DM, DM)], start=True, stop=True)
                last.then_inc(down_done, 1)

            def owners(g):
                at = tile_expert[0:1, g * GROUP:(g + 1) * GROUP] if isinstance(g, int) else tile_expert[0:1, bass.ds(g * GROUP, GROUP)]
                _, e = nc.values_load_multi_w_load_instructions(
                    at, engines=PE_ENGINE, min_val=0, max_val=EXPERTS - 1,
                    skip_runtime_bounds_check_because="the plan clamps it to the last expert")
                return e

            turn(0, 0, 1)
            def step(g, u, landings):
                e = owners(g)
                up(g, u, e)
                if landings is not None:
                    turn(g + 1, u + 1, landings)
                if not (isinstance(g, int) and g == 0):
                    down(g - 1, u - 1, owners(g - 1))
                turn_h(g, u)

            for g in range(PEEL):
                if g == 1:
                    pe.wait_ge(wd_landed, 16)
                step(g, g, (g + 1) // DEEP + 1)
            with pe.Fori(0, (GROUPS - 1 - PEEL) // DEEP) as i:
                for u in range(DEEP):
                    step(i * DEEP + PEEL + u, PEEL + u, i + 2)
            step(GROUPS - 1, GROUPS - 1, None)
            down(GROUPS - 1, GROUPS - 1, owners(GROUPS - 1))

        @block.scalar
        def _(act):
            act.sem_inc(h_ready, AHEAD)
            act.sem_inc(hT_ready, AHEAD)

            def step(g, u):
                act.wait_ge(up_done, done(g))
                act.wait_ge(h_turned, done(g - 2))
                nc.scalar.activation(h[:, u % 2, :, :].rearrange("p j i -> p (j i)"), psH[:, u % 2, 0:GROUP * INTER],
                                     ACT.Silu).then_inc(h_ready, 1)
                act.wait_ge(h_turned, done(g))
                act.wait_ge(down_done, done(g - 2))
                nc.scalar.activation(hT[:, u % 2, :], psT[0:INTER, u % 2, :], ACT.Copy).then_inc(hT_ready, 1)

            group_loop(act, step)

        @block.vector
        def _(dve):
            dve.sem_inc(xT_ready, AHEAD)
            dve.sem_inc(y_ready, AHEAD)

            def take_y(g, u, stores):
                dve.wait_ge(down_done, done(g))
                if stores is not None:
                    dve.wait_ge(stored[u % DEEP], 16 * (stores + 1))
                nc.vector.tensor_copy(y[:, u % DEEP, :, :].rearrange(flat), psY[:, u % 2, :]).then_inc(y_ready, 1)

            def step(g, u, stores):
                dve.wait_ge(x_turned, done(g))
                dve.wait_ge(up_done, done(g - 2))
                nc.vector.tensor_copy(xT[:, u % 2, :], psX[:, u % 2, :]).then_inc(xT_ready, 1)
                if not (isinstance(g, int) and g < 2):
                    take_y(g - 2, u - 2, stores)

            for g in range(PEEL):
                step(g, g, None)
            with dve.Fori(0, (GROUPS - 1 - PEEL) // DEEP) as i:
                for u in range(DEEP):
                    step(i * DEEP + PEEL + u, PEEL + u, i + (1 + u) // DEEP)
            step(GROUPS - 1, GROUPS - 1, (GROUPS - 3) // DEEP)
            take_y(GROUPS - 2, GROUPS - 2, (GROUPS - 2) // DEEP)
            take_y(GROUPS - 1, GROUPS - 1, (GROUPS - 1) // DEEP)


def combine(nc, stage, G, L):
    w8, place = L.w8, L.place
    with Memory(nc, stage) as m:
        got = m.sbuf("got", [P, TPB, TOPK, DM])
        landed = [m.sem(f"landed{t}") for t in range(TPB)]
        added = m.sem("added")
        block = m.block()

        @block.gpsimd
        def _(pool):
            for t in range(TILES):
                if t >= TPB:
                    pool.wait_ge(added, t - TPB + 1)
                for k in range(TOPK):
                    nc.gpsimd.indirect_dma_start(got[:, t % TPB, k, :], None, G.slots_out,
                                                 bass.IndirectOffsetOnAxis(place[:, t, k:k + 1], 0)).then_inc(landed[t % TPB], 16)

        @block.vector
        def _(dve):
            with dve.Fori(0, BATCH) as b:
                xb = G.x[:, bass.ds(b, 1), :, :].rearrange("p b t d -> p (b t) d")
                wb = w8[:, bass.ds(b * TPB, TPB), :]
                for t in range(TPB):
                    dve.wait_ge(landed[t], 16 * TOPK * b + 16 * TOPK)
                    for k in range(TOPK):
                        last = nc.vector.scalar_tensor_tensor(xb[:, t, :], got[:, t, k, :], wb[:, t, k:k + 1], xb[:, t, :],
                                                              ALU.mult, ALU.add)
                        if k < TOPK - 1:
                            nc.vector.drain()
                    last.then_inc(added, 1)


def attn_b(nc, stage, G, W):
    with Memory(nc, stage) as m:
        L = Shared()
        L.v = m.sbuf("v", [P, TILES, HB, VW])
        L.wo = m.sbuf("wo", [P, DM])
        L.wo_landed = m.sem("wo_landed")
        with Memory(nc, stage + "n") as n:
            normed(G, n)
            layernorm(nc, stage + "0", G)
            project_b(nc, stage + "1", G, W, L)
        attend_b(nc, stage + "2", G, L)


def project_b(nc, stage, G, W, L):
    with Memory(nc, stage) as m:
        wq, wk, wv, bo = (m.sbuf(n, [P, DM]) for n in ("wq", "wk", "wv", "bo"))
        xT = m.sbuf("xT", [P, SEQ])
        parts = m.sbuf("parts", [P, 2, 3, SEQ], BF16)
        rest = m.sbuf("rest", [P, 2, SEQ])
        ps = m.psum("ps", [P, 2, 2, HALF])
        psv = m.psum("psv", [P, 2, HALF])
        landed, rounds, cleared, v_room, xT_ready, high_ready, parts_ready, stacked = (m.sem(n) for n in (
            "landed", "rounds", "cleared", "v_room", "xT_ready", "high_ready", "parts_ready", "stacked"))
        qk_done, v_done = m.sem("qk_done"), m.sem("v_done")
        block = m.block()
        WORKERS = 3
        COPIES = 18

        def end_round(eng):
            eng.drain()
            eng.sem_inc(rounds, 1)

        @block.sync
        def _(sp):
            for dst, src in ((wq, W["bwqT"]), (wk, W["bwkT"]), (wv, W["bwvT"]), (bo, W["bo"].unsqueeze(0).to_broadcast([P, DM]))):
                sp.dma_start(dst[:], src).then_inc(landed, 16)
            sp.dma_start(L.wo[:], W["bwoT"]).then_inc(L.wo_landed, 16)
            with sp.Fori(0, BATCH) as b:
                for n, stack in enumerate((G.q_stack, G.k_stack)):
                    sp.wait_ge(parts_ready, 2 * b + n + 1)
                    for i in range(3):
                        for j in range(3):
                            row = (3 * i + j) * P
                            sp.dma_start(stack[row:row + P, bass.ds(b * SEQ, SEQ)], parts[:, n, j if n else i, :]).then_inc(stacked, 16)
            sp.wait_ge(stacked, 16 * COPIES * BATCH)

        @block.gpsimd
        def _(pool):
            nc.gpsimd.memset(L.v[:], 0.0).then_inc(cleared, 1)
            pool.wait_ge(cleared, 1)
            nc.gpsimd.memset(L.v[:, :, :, WB:WB + 1], 1.0).then_inc(v_room, 1)
            with pool.Fori(0, BATCH) as b:
                pool.wait_ge(rounds, WORKERS * b + WORKERS)
                nc.gpsimd.tensor_copy(xT[:], G.xnT[:, bass.ds(b, 1), :].rearrange("p b n -> p (b n)")).then_inc(xT_ready, 1)

        @block.tensor
        def _(pe):
            end_round(pe)
            pe.wait_ge(landed, 64)
            with pe.Fori(0, BATCH) as b:
                pe.wait_ge(xT_ready, b + 1)
                for n, w in enumerate((wq, wk)):
                    for u in range(2):
                        last = nc.tensor.matmul(ps[:, n, u, :], w[:], xT[:, u * HALF:(u + 1) * HALF], start=True, stop=True)
                    last.then_inc(qk_done, 1)
                for t in range(TPB):
                    last = nc.tensor.matmul(psv[:, t // 4, (t % 4) * DM:(t % 4 + 1) * DM], xT[:, t * P:(t + 1) * P], wv[:],
                                            start=True, stop=True)
                last.then_inc(v_done, 1)
                end_round(pe)

        @block.scalar
        def _(act):
            end_round(act)
            act.wait_ge(v_room, 1)
            with act.Fori(0, BATCH) as b:
                for n in range(2):
                    act.wait_ge(qk_done, 2 * b + n + 1)
                    nc.scalar.activation(parts[:, n, 0, :], ps[:, n, :, :].rearrange("p u n -> p (u n)"), ACT.Copy).then_inc(high_ready, 1)
                act.wait_ge(v_done, b + 1)
                nc.scalar.activation(L.v[:, bass.ds(b * TPB, TPB), :, 0:WB],
                                     psv[:].rearrange("p u (t h d) -> p (u t) h d", h=HB, d=WB), ACT.Copy)
                end_round(act)

        @block.vector
        def _(dve):
            end_round(dve)
            dve.wait_ge(landed, 64)
            with dve.Fori(0, BATCH) as b:
                dve.wait_ge(rounds, WORKERS * b + WORKERS)
                xb = G.x[:, bass.ds(b, 1), :, :].rearrange("p b t d -> p (b t) d")
                nc.vector.tensor_tensor(xb, xb, bo[:].unsqueeze(1).to_broadcast([P, TPB, DM]), ALU.add)
                for n in range(2):
                    dve.wait_ge(high_ready, 2 * b + n + 1)
                    nc.vector.tensor_tensor(rest[:, n, :], ps[:, n, :, :].rearrange("p u n -> p (u n)"), parts[:, n, 0, :], ALU.subtract)
                    nc.vector.drain()
                    nc.vector.tensor_copy(parts[:, n, 1, :], rest[:, n, :])
                    nc.vector.drain()
                    nc.vector.tensor_tensor(parts[:, n, 2, :], rest[:, n, :], parts[:, n, 1, :], ALU.subtract).then_inc(parts_ready, 1)
                dve.wait_ge(stacked, 16 * COPIES * b + 16 * COPIES)
                nc.vector.memset(rest[:, 0, 0:1], 0.0)
                end_round(dve)


def attend_b(nc, stage, G, L):
    SCALE = float(1.0 / np.sqrt(WB))
    HG = 4
    GB = HB // HG
    LAST = BATCH - 1
    QT = SEQ // P
    STEPS = [(1, kt, max(0, kt - 4) * P) for kt in range(8)] + [(0, kt, kt * P) for kt in range(4)]
    HALF1_STEPS = 8
    MAXIMA = [(h, qt, kh) for h in range(HG) for qt in range(QT) for kh in range(1 + (qt >= 4))]
    POINTS = 20
    MAX_TURN_STEP = 10
    NM = len(MAXIMA)
    SLOT = NM + 1 + 2
    FIRST_USES = NM + 1
    BATCH_USES = GB * SLOT + 4
    with Memory(nc, stage) as m:
        qS, kS = (m.sbuf(n, [P, GB, HG, SEQ], BF16) for n in ("qS", "kS"))
        ident_bf = m.sbuf("ident_bf", [P, P], BF16)
        mask_q, mask_k = m.sbuf("mask_q", [P, P], BF16), m.sbuf("mask_k", [P, P], BF16)
        vb = m.sbuf("vb", [P, QT, HB, VW])
        pT = m.sbuf("pT", [P, 2, HG, HALF])
        peak = m.sbuf("peak", [P, HG, QT])
        peak2 = m.sbuf("peak2", [P, HG, QT // 2, 2])
        negp = m.sbuf("negp", [HG * QT, 2, 3, P], BF16)
        negr = m.sbuf("negr", [HG * QT, P])
        ctxu = m.sbuf("ctxu", [P, 2, HALF])
        inv = m.sbuf("inv", [P, 4, HG])
        ctx = m.sbuf("ctx", [P, QT, HB, WB])
        ctxT = m.sbuf("ctxT", [P, SEQ])
        psE = m.psum("psE", [P, 2, 2, HALF])
        psM = m.psum("psM", [P, 2, HALF])
        psV = m.psum("psV", [P, 2, HALF])
        made, v_ready, slot_done = m.sem("made"), m.sem("v_ready"), m.sem("slot_done")
        stack_landed = [m.sem(f"stack_landed{g}") for g in range(GB)]
        peaks_landed = [m.sem(f"peaks_landed{g}") for g in range(GB)]
        m_done, m_taken, peak_ready, split_ready, e_done, e_taken, pv_done, ctx_taken, ctx_ready, ctxT_ready = (m.sem(n) for n in (
            "m_done", "m_taken", "peak_ready", "split_ready", "e_done", "e_taken", "pv_done", "ctx_taken", "ctx_ready", "ctxT_ready"))
        block = m.block()
        AHEAD = 2

        def batches(eng, batch):
            with eng.Fori(0, LAST) as b:
                batch(b, False)
            batch(LAST, True)

        def maxima_at(point):
            return range(point * NM // POINTS, (point + 1) * NM // POINTS) if point < POINTS else range(0)

        def uses(b, g):
            return FIRST_USES + b * BATCH_USES + g * SLOT

        @block.sync
        def _(sp):
            def load(b, g):
                cols = bass.ds(b * SEQ, SEQ)
                for dst, src in ((qS, G.q_stack), (kS, G.k_stack)):
                    sp.dma_start(dst[0:STACK, g, :, :], src.rearrange("(r h) n -> r h n", h=HB)[:, g * HG:(g + 1) * HG, cols]
                                 ).then_inc(stack_landed[g], 16)

            def peaks(n, g):
                sp.wait_ge(split_ready, n + 1)
                for i in range(3):
                    sp.dma_start(qS[STACK + i:STACK + i + 1, g, :, :].rearrange("a h (t q) -> a (h t) q", q=P),
                                 negp[:, g % 2, i, :]).then_inc(peaks_landed[g], 16)

            sp.wait_ge(made, 1)
            for g in range(GB):
                load(0, g)
            peaks(0, 0)

            def batch(b, last):
                for g in range(GB):
                    if not (last and g == GB - 1):
                        peaks(b * GB + g + 1, (g + 1) % GB)
                    if not last:
                        sp.wait_ge(slot_done, b * GB + g + 1)
                        load(b + 1, g)

            batches(sp, batch)

        @block.gpsimd
        def _(pool):
            def values(b, g):
                heads = slice(g * HG, (g + 1) * HG)
                nc.gpsimd.tensor_copy(vb[:, :, heads, :], L.v[:, bass.ds(b * QT, QT), heads, :]).then_inc(v_ready, 1)

            nc.gpsimd.memset(kS[64:96, :, :, :], 1.0).then_inc(made, 1)
            pool.wait_ge(made, 1)
            nc.gpsimd.memset(mask_q[:], 0.0)
            nc.gpsimd.memset(mask_k[:], 0.0)
            nc.gpsimd.tensor_copy(ident_bf[:], G.ident[:]).then_inc(made, 1)
            pool.wait_ge(made, 2)
            nc.gpsimd.affine_select(out=mask_q[:], in_=mask_q[:], compare_op=ALU.is_ge, fill=MASKED, base=0,
                                    pattern=[[-1, P]], channel_multiplier=1)
            nc.gpsimd.affine_select(out=mask_k[:], in_=mask_k[:], compare_op=ALU.is_ge, fill=MASKED, base=0,
                                    pattern=[[1, P]], channel_multiplier=-1).then_inc(made, 1)
            for g in range(GB):
                values(0, g)
            with pool.Fori(0, LAST) as b:
                for g in range(GB):
                    pool.wait_ge(slot_done, b * GB + g + 1)
                    values(b + 1, g)

        @block.tensor
        def _(pe):
            pe.wait_ge(made, 3)
            pe.wait_ge(L.wo_landed, 16)

            def use(c):
                pe.wait_ge(m_taken, c + 1)

            def maximum(c, parity, g, k):
                h, qt, kh = MAXIMA[k]
                n = min(HALF, (qt + 1) * P - kh * HALF)
                diagonal = (qt + 1) * P - kh * HALF <= HALF
                use(c)
                edge = n - P if diagonal else n
                if edge:
                    last = nc.tensor.matmul(psM[:, parity, 0:edge], qS[0:STACK, g, h, qt * P:(qt + 1) * P],
                                            kS[0:STACK, g, h, kh * HALF:kh * HALF + edge], start=True, stop=True)
                if diagonal:
                    nc.tensor.matmul(psM[:, parity, edge:n], qS[0:STACK, g, h, qt * P:(qt + 1) * P],
                                     kS[0:STACK, g, h, kh * HALF + edge:kh * HALF + n], start=True, stop=False)
                    last = nc.tensor.matmul(psM[:, parity, edge:n], ident_bf[:], mask_q[:], start=False, stop=True)
                last.then_inc(m_done, 1)

            def turn_maxima(c, parity, n):
                pe.wait_ge(peak_ready, n + 1)
                use(c)
                nc.tensor.transpose(psM[0:HG * QT, parity, 0:P], peak[:].rearrange("p h t -> p (h t)"), G.ident[:]).then_inc(m_done, 1)

            def scores(b, g, e, pair):
                half, kt, q0 = STEPS[e]
                pe.wait_ge(e_taken, (b * GB + g) * 24 + 2 * e + pair + 1)
                for i in range(2):
                    h = 2 * pair + i
                    keys = kS[0:STACK + 3, g, h, kt * P:(kt + 1) * P]
                    edge = q0
                    if kt >= 4 * half:
                        edge = q0 + P
                        nc.tensor.matmul(psE[:, pair, i, q0:edge], keys, qS[0:STACK + 3, g, h, half * HALF + q0:half * HALF + edge],
                                         start=True, stop=False)
                        last = nc.tensor.matmul(psE[:, pair, i, q0:edge], ident_bf[:], mask_k[:], start=False, stop=True)
                    if edge < HALF:
                        last = nc.tensor.matmul(psE[:, pair, i, edge:HALF], keys, qS[0:STACK + 3, g, h, half * HALF + edge:(half + 1) * HALF],
                                                start=True, stop=True)
                last.then_inc(e_done, 1)

            def weigh(b, g, e):
                half, kt, q0 = STEPS[e]
                pe.wait_ge(e_taken, (b * GB + g) * 24 + 2 * e + 2 + AHEAD)
                if kt == 0:
                    pe.wait_ge(ctx_taken, (b * GB + g) * 2 + 1 - half + AHEAD - 1)
                for h in range(HG):
                    last = nc.tensor.matmul(psV[32 * h:32 * h + 32, half, q0:HALF], vb[:, kt, g * HG + h, :], pT[:, e % 2, h, q0:HALF],
                                            start=(kt == 0), stop=True, skip_group_check=True)
                last.then_inc(pv_done, 1)

            def turn_context(b, g, half, c, parity):
                pe.wait_ge(ctx_taken, (b * GB + g) * 2 + 1 - half + 1 + AHEAD)
                use(c)
                for t in range(4):
                    last = nc.tensor.transpose(psM[:, parity, t * P:(t + 1) * P], ctxu[:, half, t * P:(t + 1) * P], G.ident[:])
                last.then_inc(m_done, 1)

            pe.wait_ge(stack_landed[0], 32)
            for k in range(NM):
                maximum(k, k % 2, 0, k)
            turn_maxima(NM, NM % 2, 0)

            def batch(b, last):
                for g in range(GB):
                    n = b * GB + g
                    more = not (last and g == GB - 1)
                    ahead = (g + 1) % GB
                    c, parity = uses(b, g), (FIRST_USES + g * SLOT) % 2
                    pe.wait_ge(peaks_landed[g], 48 * b + 48)
                    pe.wait_ge(v_ready, n + 1)
                    if more:
                        pe.wait_ge(stack_landed[ahead], 32 * (b + (g + 1) // GB) + 32)
                    for e in range(len(STEPS)):
                        for pair in range(2):
                            scores(b, g, e, pair)
                            for k in maxima_at(2 * e + pair) if more else ():
                                maximum(c, parity, ahead, k)
                                c, parity = c + 1, 1 - parity
                        if e == MAX_TURN_STEP and more:
                            turn_maxima(c, parity, n + 1)
                            c, parity = c + 1, 1 - parity
                        if e == MAX_TURN_STEP:
                            turn_context(b, g, 1, c, parity)
                            c, parity = c + 1, 1 - parity
                        if e >= 1:
                            weigh(b, g, e - 1)
                    weigh(b, g, len(STEPS) - 1)
                    turn_context(b, g, 0, c, parity)
                    c, parity = c + 1, 1 - parity
                    pe.wait_ge(m_done, c)
                    pe.sem_inc(slot_done, 1)
                pe.wait_ge(ctx_ready, 2 * GB * b + 2 * GB)
                for u in range(2):
                    use(c)
                    for t in range(4):
                        last = nc.tensor.transpose(psM[:, parity, t * P:(t + 1) * P],
                                                   ctx[:, 4 * u + t, :, :].rearrange("p h d -> p (h d)"), G.ident[:])
                    last.then_inc(m_done, 1)
                    c, parity = c + 1, 1 - parity
                for u in range(2):
                    pe.wait_ge(ctxT_ready, 2 * b + u + 1)
                    use(c)
                    for t in range(4):
                        last = nc.tensor.matmul(psM[:, parity, t * DM:(t + 1) * DM], ctxT[:, (4 * u + t) * P:(4 * u + t + 1) * P],
                                                L.wo[:], start=True, stop=True)
                    last.then_inc(m_done, 1)
                    c, parity = c + 1, 1 - parity

            batches(pe, batch)

        @block.scalar
        def _(act):
            act.sem_inc(e_taken, AHEAD)
            act.sem_inc(ctx_taken, AHEAD)

            def batch(b, last):
                for g in range(GB):
                    n = b * GB + g
                    for e, (half, kt, q0) in enumerate(STEPS):
                        for pair in range(2):
                            act.wait_ge(e_done, n * 24 + 2 * e + pair + 1)
                            if e >= 2:
                                act.wait_ge(pv_done, n * 12 + e - 1)
                            heads = slice(2 * pair, 2 * pair + 2)
                            nc.scalar.activation(pT[:, e % 2, heads, q0:HALF], psE[:, pair, :, q0:HALF], ACT.Exp,
                                                 scale=SCALE).then_inc(e_taken, 1)
                        if e == HALF1_STEPS:
                            act.wait_ge(pv_done, n * 12 + HALF1_STEPS)
                            nc.scalar.activation(ctxu[:, 1, :], psV[:, 1, :], ACT.Copy).then_inc(ctx_taken, 1)
                    act.wait_ge(pv_done, n * 12 + 12)
                    nc.scalar.activation(ctxu[:, 0, :], psV[:, 0, :], ACT.Copy).then_inc(ctx_taken, 1)

            batches(act, batch)

        @block.vector
        def _(dve):
            dve.sem_inc(m_taken, AHEAD)

            def maximum(c, parity, k):
                h, qt, kh = MAXIMA[k]
                size = min(HALF, (qt + 1) * P - kh * HALF)
                to = peak[:, h, qt:qt + 1] if qt < 4 else peak2[:, h, qt - 4, kh:kh + 1]
                dve.wait_ge(m_done, c + 1)
                nc.vector.reduce_max(to, psM[:, parity, 0:size], AX.X).then_inc(m_taken, 1)

            def peaks():
                nc.vector.drain()
                nc.vector.reduce_max(peak[:, :, 4:8], peak2[:], AX.X).then_inc(peak_ready, 1)

            def split(c, parity, g):
                dve.wait_ge(m_done, c + 1)
                turned = psM[0:HG * QT, parity, 0:P]
                high, mid, low = (negp[:, g % 2, i, :] for i in range(3))
                nc.vector.tensor_scalar(high, turned, -1.0, None, ALU.mult)
                nc.vector.drain()
                nc.vector.scalar_tensor_tensor(negr[:], turned, -1.0, high, ALU.mult, ALU.subtract).then_inc(m_taken, 1)
                nc.vector.drain()
                nc.vector.tensor_copy(mid, negr[:])
                nc.vector.drain()
                nc.vector.tensor_tensor(low, negr[:], mid, ALU.subtract).then_inc(split_ready, 1)

            def context(c, parity, g, half):
                dve.wait_ge(m_done, c + 1)
                turned = psM[:, parity, :].rearrange("p (t h w) -> p t h w", t=4, h=HG)
                nc.vector.reciprocal(inv[:], turned[:, :, :, WB])
                nc.vector.drain()
                nc.vector.tensor_tensor(ctx[:, 4 * half:4 * half + 4, g * HG:(g + 1) * HG, :], turned[:, :, :, 0:WB],
                                        inv[:].unsqueeze(3).to_broadcast([P, 4, HG, WB]), ALU.mult).then_inc(m_taken, 1)
                nc.vector.drain()
                dve.sem_inc(ctx_ready, 1)

            for k in range(NM):
                maximum(k, k % 2, k)
            peaks()
            split(NM, NM % 2, 0)

            def batch(b, last):
                xb = G.x[:, bass.ds(b, 1), :, :].rearrange("p b t d -> p (b t) d")
                for g in range(GB):
                    more = not (last and g == GB - 1)
                    c, parity = uses(b, g), (FIRST_USES + g * SLOT) % 2
                    for k in range(NM) if more else ():
                        maximum(c, parity, k)
                        c, parity = c + 1, 1 - parity
                    if more:
                        peaks()
                        split(c, parity, (g + 1) % GB)
                        c, parity = c + 1, 1 - parity
                    for half in (1, 0):
                        context(c, parity, g, half)
                        c, parity = c + 1, 1 - parity
                for u in range(2):
                    dve.wait_ge(m_done, c + 1)
                    nc.vector.tensor_copy(ctxT[:, u * HALF:(u + 1) * HALF], psM[:, parity, :]).then_inc(m_taken, 1)
                    nc.vector.drain()
                    dve.sem_inc(ctxT_ready, 1)
                    c, parity = c + 1, 1 - parity
                for u in range(2):
                    dve.wait_ge(m_done, c + 1)
                    nc.vector.tensor_tensor(xb[:, 4 * u:4 * u + 4, :], xb[:, 4 * u:4 * u + 4, :],
                                            psM[:, parity, :].rearrange("p (t d) -> p t d", d=DM), ALU.add).then_inc(m_taken, 1)
                    c, parity = c + 1, 1 - parity

            batches(dve, batch)


def build(nc, A, out):
    G, W = Shared(), A
    with Memory(nc, "g") as m:
        G.x = m.sbuf("x", [P, BATCH, TPB, DM])
        G.ident = m.sbuf("ident", [P, P])
        G.ones = m.sbuf("ones", [P, P])
        G.ratio_eps = m.sbuf("ratio_eps", [P, 1])
        G.slots_in = nc.dram_tensor("slots_in", [SLOTS, DM], F32, kind="Internal").ap()
        G.slots_out = nc.dram_tensor("slots_out", [SLOTS, DM], F32, kind="Internal").ap()
        G.owner_dram = nc.dram_tensor("owner", [4 * P, 1], I32, kind="Internal").ap()
        G.q_stack, G.k_stack = (nc.dram_tensor(n, [STACK * HB, TOKENS], BF16, kind="Internal").ap() for n in ("q_stack", "k_stack"))
        G.slots_zeroed = m.sem("slots_zeroed")
        setup(nc, A["x"], G)
        with Memory(nc, "a0") as a:
            normed(G, a)
            layernorm(nc, "a0", G)
            attn_a(nc, G, W)
            ffn_a(nc, G, W)
        moe(nc, "m", G, W)
        attn_b(nc, "b", G, W)
        moe(nc, "n", G, W)
        finish(nc, G.x, out)


def normed(G, m):
    G.xn = m.sbuf("xn", [P, BATCH, TPB, DM])
    G.xnT = m.sbuf("xnT", [P, BATCH, SEQ])


def finish(nc, x, out):
    with Memory(nc, "end") as e:
        stored = e.sem("stored")
        block = e.block()

        @block.sync
        def _(sp):
            sp.dma_start(out.rearrange("b (t p) d -> p b t d", p=P), x[:]).then_inc(stored, 16)
            sp.wait_ge(stored, 16)


def kernel(**inputs):
    import concourse.bacc as bacc
    from concourse.bass_utils import run_bass_kernel_spmd

    a = {n: np.ascontiguousarray(v) for n, v in inputs.items()}
    wq, wk = a["L0_attn_a_Wq"], a["L0_attn_a_Wk"]
    arrays = {
        "x": a["L0_attn_a_x"],
        "wq": wq, "wk": wk, "wv": a["L0_attn_a_Wv"], "wo": a["L0_attn_a_Wo"],
        "wqT": wq.reshape(DM, HD).T, "wkT": wk.reshape(DM, HD).T, "projT": a["L0_attn_a_proj"].T,
        **{n: a["L0_attn_a_" + o] for n, o in (("w1", "W1"), ("b1", "b1"), ("w2", "W2"), ("b2", "b2"), ("ln1_g", "ln1_g"),
                                               ("ln1_b", "ln1_b"), ("ln2_g", "ln2_g"), ("ln2_b", "ln2_b"))},
        "routerT": a["L0_ffn_router_w"].T, "expert_bias": a["L0_ffn_expert_bias"],
        "w_gateT": a["L0_ffn_w_gate"].transpose(2, 0, 1), "w_downT": a["L0_ffn_w_down"].transpose(2, 0, 1),
        "bwqT": a["L0_attn_b_Wq"].reshape(HB, WB, DM).transpose(2, 1, 0).reshape(DM, DM),
        "bwkT": a["L0_attn_b_Wk"].reshape(HB, WB, DM).transpose(2, 1, 0).reshape(DM, DM),
        "bwvT": a["L0_attn_b_Wv"].T, "bwoT": a["L0_attn_b_Wo"].T, "bo": a["L0_attn_b_bo"],
        "w_gate_sharedT": a["L0_ffn_w_gate_shared"].T, "w_down_sharedT": a["L0_ffn_w_down_shared"].T,
    }
    arrays["b1"] = arrays["b1"].reshape(FFC, P).T
    arrays = {n: np.ascontiguousarray(v) for n, v in arrays.items()}
    nc = bacc.Bacc("TRN2", target_bir_lowering=False, num_devices=1)
    A = {n: nc.dram_tensor(f"in_{n}", v.shape, mybir.dt.from_np(v.dtype), kind="ExternalInput").ap() for n, v in arrays.items()}
    out = nc.dram_tensor("out_x", (BATCH, SEQ, DM), F32, kind="ExternalOutput").ap()
    build(nc, A, out)
    r = run_bass_kernel_spmd(nc, [{f"in_{n}": v for n, v in arrays.items()}], core_ids=[0])
    return r.results[0]["out_x"]
```

```python
from contextlib import ExitStack

import concourse.bass as bass
import numpy as np
from concourse import mybir

F32 = mybir.dt.float32
BF16 = mybir.dt.bfloat16
I32 = mybir.dt.int32
ALU = mybir.AluOpType
ACT = mybir.ActivationFunctionType
AX = mybir.AxisListType

P = 128
BATCH, SEQ, DM = 4, 1024, 128
TOKENS = BATCH * SEQ
TILES = TOKENS // P
TPB = SEQ // P
HALF = 512

HA, DH, MF = 16, 64, 64
PAIRS = HA // 2
HD = HA * DH
DFF = 512
FFC = DFF // P
EPS_KERNEL = 1e-6
EPS_LN_A = 1e-6
EPS_LN = 1e-5
DN = float(np.float32(1.0) / np.sqrt(np.sqrt(np.float32(DH))))
RATIO = float(np.float32(1.0) / np.sqrt(np.float32(MF)))

HB, WB = 16, 8
VW = 32
STACK = 9 * WB
MASKED = -1e30

EXPERTS, TOPK, INTER = 160, 8, 64
ROUTED_SCALE = 2.5
HALVES = 2
GROUP = 4
HALF_TILES = TOKENS // HALVES * TOPK // P + EXPERTS
HALF_GROUPS = HALF_TILES // GROUP
GROUPS = HALVES * HALF_GROUPS
GROUP_SLOTS = GROUP * P
HALF_SLOTS = HALF_GROUPS * GROUP_SLOTS
OWNER_COLUMNS = -(-HALF_TILES // P)
TPH = TILES // HALVES
ZERO_FILLS = 18
assert HALF_TILES % GROUP == 0 and HALF_SLOTS % (ZERO_FILLS * P) == 0


class Shared:
    pass


class Memory:

    def __init__(self, nc, stage):
        self.nc, self.stage, self.ctx, self.sems = nc, stage, ExitStack(), []

    def __enter__(self):
        return self

    def __exit__(self, *a):
        self.ctx.__exit__(*a)
        self.nc.clear_and_free_semaphores(self.sems)
        self.nc.all_engine_barrier()

    def sbuf(self, name, shape, dtype=F32):
        return self.ctx.enter_context(self.nc.sbuf_tensor(f"{self.stage}_{name}", shape, dtype))

    def psum(self, name, shape, dtype=F32):
        return self.ctx.enter_context(self.nc.psum_tensor(f"{self.stage}_{name}", shape, dtype))

    def sem(self, name):
        self.sems.append(self.nc.alloc_semaphore(name=f"{self.stage}_{name}"))
        return self.sems[-1]

    def block(self):
        return self.ctx.enter_context(self.nc.Block())


def bc(ap, n):
    return ap.unsqueeze(2).to_broadcast([ap.shape[0], ap.shape[1], n])


def rsqrt(nc, out, var, eps, guess, half):
    dve = nc.vector
    dve.tensor_scalar(half, var, eps, None, ALU.add)
    dve.drain()
    dve.tensor_scalar(out.bitcast(I32), half.bitcast(I32), -0.5, float(0x5F3759DF), ALU.mult, ALU.add)
    dve.tensor_scalar(half, half, -0.5, None, ALU.mult)
    for _ in range(4):
        dve.drain()
        dve.tensor_tensor(guess, out, out, ALU.mult)
        dve.drain()
        dve.tensor_tensor(guess, guess, half, ALU.mult)
        dve.drain()
        dve.scalar_tensor_tensor(out, guess, 1.5, out, ALU.add, ALU.mult)
    dve.drain()


def setup(nc, x, G):
    with Memory(nc, "setup") as m:
        zeros_made = m.sem("zeros_made")
        zeroed, made = m.sem("zeroed"), m.sem("made")
        x_landed = m.sem("x_landed")
        block = m.block()

        @block.sync
        def _(sp):
            sp.dma_start(G.x[:], x.rearrange("b (t p) d -> p b t d", p=P)).then_inc(x_landed, 16)
            sp.wait_ge(x_landed, 16)

        @block.vector
        def _(dve):
            nc.vector.memset(G.zeros[:], 0.0).then_inc(zeros_made, 1)
            dve.wait_ge(zeros_made, 1)

        @block.gpsimd
        def _(pool):
            pool.memset(G.ident[:], 0.0).then_inc(zeroed, 1)
            pool.memset(G.ones[:], 1.0)
            pool.wait_ge(zeroed, 1)
            pool.affine_select(out=G.ident[:], in_=G.ident[:], compare_op=ALU.not_equal, fill=1.0, base=0,
                               pattern=[[-1, P]], channel_multiplier=1).then_inc(made, 1)
            pool.wait_ge(made, 1)


def layernorm(nc, stage, G):
    with Memory(nc, stage) as m:
        stats = m.sbuf("stats", [P, TPB, 6])
        mv = m.sbuf("mv", [P, TPB, 2])
        moments = m.sbuf("moments", [P, TILES, 2])
        var, half, rstd = (m.sbuf(n, [P, TILES]) for n in ("var", "half", "rstd"))
        ps = m.psum("ps", [P, 4, HALF])
        xn_ready, turned, bank_free = m.sem("xn_ready"), m.sem("turned"), m.sem("bank_free")
        block = m.block()
        x, xn = (t[:].rearrange("p b t d -> p (b t) d") for t in (G.x, G.xn))

        @block.vector
        def _(dve):
            with dve.Fori(0, BATCH) as b:
                for t in range(TPB):
                    nc.vector.bn_stats(stats[:, t, :], x[:, bass.ds(b * TPB + t, 1), :].rearrange("p a d -> p (a d)"))
                nc.vector.drain()
                for t in range(TPB):
                    nc.vector.bn_aggr(mv[:, t, :], stats[:, t, :])
                nc.vector.drain()
                nc.vector.tensor_copy(moments[:, bass.ds(b * TPB, TPB), :], mv[:])
            nc.vector.drain()
            rsqrt(nc, rstd[:], moments[:, :, 1], EPS_LN, var[:], half[:])
            for t in range(TILES):
                last = nc.vector.tensor_scalar(xn[:, t, :], x[:, t, :], moments[:, t, 0:1], rstd[:, t:t + 1], ALU.subtract, ALU.mult)
                if t % 4 == 3:
                    last.then_inc(xn_ready, 1)

        @block.tensor
        def _(pe):
            for u in range(TILES // 4):
                pe.wait_ge(xn_ready, u + 1)
                if u >= 4:
                    pe.wait_ge(bank_free, u - 3)
                for t in range(4):
                    last = nc.tensor.transpose(ps[:, u % 4, t * P:(t + 1) * P], xn[:, 4 * u + t, :], G.ident[:])
                last.then_inc(turned, 1)

        @block.scalar
        def _(act):
            xnT = G.xnT[:].rearrange("p b n -> p (b n)")
            for u in range(TILES // 4):
                act.wait_ge(turned, u + 1)
                nc.scalar.activation(xnT[:, u * HALF:(u + 1) * HALF], ps[:, u % 4, :], ACT.Copy).then_inc(bank_free, 1)


def attn_a(nc, G, W):
    with Memory(nc, "a") as m:
        wq, wk, wv = (m.sbuf(n, [P, HD]) for n in ("wq", "wk", "wv"))
        wqT, wkT = (m.sbuf(n, [P, PAIRS, DM]) for n in ("wqT", "wkT"))
        wqp, wkp = (m.sbuf(n, [P, PAIRS, P]) for n in ("wqp", "wkp"))
        proj2 = m.sbuf("proj2", [P, P])
        wo = m.sbuf("wo", [DH, HA, DM])
        ngmax = m.sbuf("ngmax", [P, 1])
        zero_fills = m.sem("zero_fills")

        with Memory(nc, "a1") as m1:
            pmax = m1.sbuf("pmax", [P, TOKENS // HALF, PAIRS])
            rowmax = m1.sbuf("rowmax", [P, 1])
            allmax = m1.sbuf("allmax", [1, 1])
            ps = m1.psum("ps", [P, 4, HALF])
            psw = m1.psum("psw", [P, 4, HALF])
            zeroed, landed = m1.sem("zeroed"), m1.sem("landed")
            proj_landed, fold_done, folded = m1.sem("proj_landed"), m1.sem("fold_done"), m1.sem("folded")
            feats, taken = m1.sem("feats"), m1.sem("taken")
            row_ready, turned, one_ready, spread = m1.sem("row_ready"), m1.sem("turned"), m1.sem("one"), m1.sem("spread")
            neg_ready = m1.sem("neg_ready")
            block = m1.block()

            @block.sync
            def _(sp):
                sp.dma_start(wkT[:], W["wkT"].rearrange("(c p) d -> p c d", p=P)).then_inc(landed, 16)
                sp.dma_start(wqT[:], W["wqT"].rearrange("(c p) d -> p c d", p=P)).then_inc(landed, 16)
                sp.wait_ge(zeroed, 1)
                for h in range(2):
                    sp.dma_start(proj2[h * DH:(h + 1) * DH, h * MF:(h + 1) * MF], W["projT"]).then_inc(proj_landed, 16)
                for dst, src in ((wq, W["wq"]), (wk, W["wk"]), (wv, W["wv"])):
                    sp.dma_start(dst[:], src.rearrange("d h k -> d (h k)")).then_inc(landed, 16)
                sp.dma_start(wo[:], W["wo"].rearrange("h k o -> k h o")).then_inc(landed, 16)
                for slots in G.slots_in:
                    fill = slots.rearrange("(n p j) d -> n p (j d)", n=ZERO_FILLS, p=P)
                    for n in range(ZERO_FILLS):
                        sp.dma_start(fill[n], G.zeros[:]).then_inc(zero_fills, 16)
                sp.wait_ge(landed, 96)

            @block.gpsimd
            def _(pool):
                pool.memset(proj2[:], 0.0).then_inc(zeroed, 1)

            @block.tensor
            def _(pe):
                pe.wait_ge(landed, 32)
                pe.wait_ge(proj_landed, 32)
                for n, w in enumerate((wkT, wqT)):
                    for c in range(PAIRS):
                        last = nc.tensor.matmul(psw[:, 2 * n + c // 4, (c % 4) * P:(c % 4 + 1) * P], w[:, c, :], proj2[:],
                                                start=True, stop=True)
                    last.then_inc(fold_done, 1)
                pe.wait_ge(folded, 1)
                with pe.Fori(0, TOKENS // HALF) as g:
                    xg = G.xnT[:].rearrange("p b n -> p (b n)")[:, bass.ds(g * HALF, HALF)]
                    for c in range(PAIRS):
                        pe.wait_ge(taken, PAIRS * g + c + 1)
                        nc.tensor.matmul(ps[:, c % 4, :], wkp[:, c, :], xg, start=True, stop=True).then_inc(feats, 1)
                pe.wait_ge(row_ready, 1)
                nc.tensor.transpose(ps[0:1, 0, 0:P], rowmax[:], G.ident[:]).then_inc(turned, 1)
                pe.wait_ge(one_ready, 1)
                nc.tensor.matmul(ps[:, 1, 0:1], G.ones[0:1, :], allmax[:], start=True, stop=True).then_inc(spread, 1)

            @block.scalar
            def _(act):
                for n, w in enumerate((wkp, wqp)):
                    act.wait_ge(fold_done, n + 1)
                    nc.scalar.activation(w[:].rearrange("p c m -> p (c m)"),
                                         psw[:, 2 * n:2 * n + 2, :].rearrange("p a n -> p (a n)"), ACT.Copy,
                                         scale=DN).then_inc(folded, 1)
                act.wait_ge(folded, 2)

            @block.vector
            def _(dve):
                dve.sem_inc(taken, 4)
                with dve.Fori(0, TOKENS // HALF) as g:
                    for c in range(PAIRS):
                        dve.wait_ge(feats, PAIRS * g + c + 1)
                        nc.vector.reduce_max(pmax[:, bass.ds(g, 1), c:c + 1].rearrange("p a b -> p (a b)"),
                                             ps[:, c % 4, :], AX.X).then_inc(taken, 1)
                nc.vector.drain()
                nc.vector.reduce_max(rowmax[:], pmax[:].rearrange("p a b -> p (a b)"), AX.X).then_inc(row_ready, 1)
                dve.wait_ge(turned, 1)
                nc.vector.reduce_max(allmax[:], ps[0:1, 0, 0:P], AX.X).then_inc(one_ready, 1)
                dve.wait_ge(spread, 1)
                nc.vector.tensor_scalar(ngmax[:], ps[:, 1, 0:1], -1.0, None, ALU.mult).then_inc(neg_ready, 1)
                dve.wait_ge(neg_ready, 1)

        with Memory(nc, "a2") as m2:
            xT = m2.sbuf("xT", [P, SEQ])
            sq = m2.sbuf("sq", [P, HD])
            diag = m2.sbuf("diag", [P, HA])
            qmax = m2.sbuf("qmax", [P, HA])
            shift = m2.sbuf("shift", [P, HA])
            arg = m2.sbuf("arg", [P, 2, HD])
            qe = m2.sbuf("qe", [P, TPB, HD])
            kf = m2.sbuf("kf", [P, 2, HD])
            kfe = m2.sbuf("kfe", [P, HD])
            v = m2.sbuf("v", [P, 2, HA, DH + 1])
            vk = m2.sbuf("vk", [DH + 1, HD])
            vkwo = m2.sbuf("vkwo", [P, PAIRS, DM])
            ksum = m2.sbuf("ksum", [P, HD])
            prod = m2.sbuf("prod", [P, HD])
            den, inv = m2.sbuf("den", [P, HA]), m2.sbuf("inv", [P, HA])
            qs = m2.sbuf("qs", [P, 2, HD])
            qsT = m2.sbuf("qsT", [P, 2, HD])
            psA = m2.psum("psA", [P, 2, HALF])
            psB = m2.psum("psB", [P, 4, HALF])
            psC = m2.psum("psC", [P, 2, HALF])
            xT_ready = m2.sem("xT_ready")
            cleared = m2.sem("cleared")
            q_done, qd_done, q_squared, q_diag, q_arg, q_exp = (m2.sem(n) for n in (
                "q_done", "qd_done", "q_squared", "q_diag", "q_arg", "q_exp"))
            k_done, kd_done, v_done, k_squared, k_diag, k_arg, k_exp, kf_ready, v_ready, kv_tile, kv_out = (
                m2.sem(n) for n in ("k_done", "kd_done", "v_done", "k_squared", "k_diag", "k_arg", "k_exp", "kf_ready",
                                    "v_ready", "kv_tile", "kv_out"))
            sums_spread, ksum_ready, vkwo_done, vkwo_ready, qs_ready, qT_done, qsT_ready, ao_done, ao_taken = (m2.sem(n) for n in (
                "sums_spread", "ksum_ready", "vkwo_done", "vkwo_ready", "qs_ready", "qT_done", "qsT_ready", "ao_done", "ao_taken"))
            block = m2.block()
            heads = "p (h k) -> p h k"

            @block.sync
            def _(sp):
                sp.wait_ge(zero_fills, 16 * HALVES * ZERO_FILLS)

            @block.gpsimd
            def _(pool):
                def bring(b):
                    nc.gpsimd.tensor_copy(xT[:], G.xnT[:, bass.ds(b, 1), :].rearrange("p b n -> p (b n)")).then_inc(xT_ready, 1)

                nc.gpsimd.memset(v[:, :, :, DH:], 1.0).then_inc(cleared, 1)
                bring(0)
                with pool.Fori(0, BATCH - 1) as b:
                    pool.wait_ge(kd_done, TPB * b + TPB)
                    bring(b + 1)

            @block.tensor
            def _(pe):
                pe.wait_ge(cleared, 1)
                with pe.Fori(0, BATCH) as b:
                    pe.wait_ge(xT_ready, b + 1)
                    for t in range(TPB):
                        xt = xT[:, t * P:(t + 1) * P]
                        if t >= 1:
                            pe.wait_ge(q_squared, TPB * b + t)
                        for u in range(2):
                            last = nc.tensor.matmul(psA[:, u, :], xt, wq[:, u * HALF:(u + 1) * HALF], start=True, stop=True)
                        last.then_inc(q_done, 1)
                        if t >= 2:
                            pe.wait_ge(q_arg, TPB * b + t - 1)
                        for u in range(2):
                            last = nc.tensor.matmul(psB[:, 2 * (t % 2) + u, :], xt,
                                                    wqp[:, 4 * u:4 * u + 4, :].rearrange("p c m -> p (c m)"), start=True, stop=True)
                        last.then_inc(qd_done, 1)
                    pe.wait_ge(q_squared, TPB * b + TPB)
                    pe.wait_ge(q_arg, TPB * b + TPB)

                    def add_kv(t):
                        pe.wait_ge(kf_ready, TPB * b + t + 1)
                        pe.wait_ge(v_ready, 2 * TPB * b + 2 * t + 2)
                        if t == 0:
                            pe.wait_ge(ao_taken, TPB * b + 1)
                        for h in range(HA):
                            last = nc.tensor.matmul(psC[0:DH + 1, h // 8, (h % 8) * MF:(h % 8 + 1) * MF], v[:, t % 2, h, :],
                                                    kf[:, t % 2, h * MF:(h + 1) * MF], start=(t == 0 and h % 8 == 0),
                                                    stop=(t == TPB - 1), skip_group_check=True)
                        last.then_inc(kv_tile, 1)

                    for t in range(TPB):
                        xt = xT[:, t * P:(t + 1) * P]
                        for u in range(2):
                            if t + u >= 1:
                                pe.wait_ge(v_ready, 2 * TPB * b + 2 * t + u)
                            nc.tensor.matmul(psB[:, 2, :], xt, wv[:, u * HALF:(u + 1) * HALF], start=True, stop=True).then_inc(v_done, 1)
                            if u == 0:
                                if t >= 1:
                                    pe.wait_ge(k_squared, TPB * b + t)
                                for w in range(2):
                                    last = nc.tensor.matmul(psA[:, w, :], xt, wk[:, w * HALF:(w + 1) * HALF], start=True, stop=True)
                                last.then_inc(k_done, 1)
                        if t >= 1:
                            pe.wait_ge(k_arg, TPB * b + t)
                        for u in range(2):
                            last = nc.tensor.matmul(psB[:, u, :], xt, wkp[:, 4 * u:4 * u + 4, :].rearrange("p c m -> p (c m)"),
                                                    start=True, stop=True)
                        last.then_inc(kd_done, 1)
                        if t >= 1:
                            add_kv(t - 1)
                    add_kv(TPB - 1)

                    pe.wait_ge(kv_out, b + 1)
                    for u in range(2):
                        last = nc.tensor.matmul(psB[:, u, :], G.ones[DH:DH + 1, :], vk[DH:DH + 1, u * HALF:(u + 1) * HALF], start=True, stop=True)
                    last.then_inc(sums_spread, 1)
                    pe.wait_ge(cleared, 1)
                    pe.wait_ge(k_squared, TPB * b + TPB)
                    for h in range(HA):
                        c, rows = h // 2, slice(h % 2 * MF, (h % 2 + 1) * MF)
                        last = nc.tensor.matmul(psA[rows, c // 4, (c % 4) * DM:(c % 4 + 1) * DM], vk[0:DH, h * MF:(h + 1) * MF], wo[:, h, :],
                                                start=True, stop=True)
                    last.then_inc(vkwo_done, 1)

                    def project(t):
                        pe.wait_ge(qsT_ready, 2 * TPB * b + 2 * t + 2)
                        if t >= 2:
                            pe.wait_ge(ao_taken, TPB * b + t)
                        for c in range(PAIRS):
                            last = nc.tensor.matmul(psC[:, t % 2, 0:DM], qsT[:, t % 2, c * P:(c + 1) * P], vkwo[:, c, :],
                                                    start=(c == 0), stop=(c == PAIRS - 1))
                        last.then_inc(ao_done, 1)

                    pe.wait_ge(vkwo_ready, b + 1)
                    for t in range(TPB):
                        pe.wait_ge(qs_ready, TPB * b + t + 1)
                        for u in range(2):
                            if t >= 1:
                                pe.wait_ge(qsT_ready, 2 * TPB * b + 2 * t + u - 1)
                            for c in range(4):
                                last = nc.tensor.transpose(psA[:, u, c * P:(c + 1) * P], qs[:, t % 2, (4 * u + c) * P:(4 * u + c + 1) * P],
                                                           G.ident[:])
                            last.then_inc(qT_done, 1)
                        if t >= 1:
                            project(t - 1)
                    project(TPB - 1)

            @block.scalar
            def _(act):
                with act.Fori(0, BATCH) as b:
                    both = "p a n -> p (a n)"

                    def q_features(t):
                        act.wait_ge(q_arg, TPB * b + t + 1)
                        nc.scalar.activation(qe[:, t, :], arg[:, t % 2, :], ACT.Exp).then_inc(q_exp, 1)

                    for t in range(TPB):
                        act.wait_ge(q_done, TPB * b + t + 1)
                        if t >= 1:
                            act.wait_ge(q_diag, TPB * b + t)
                        nc.scalar.activation(sq[:], psA[:].rearrange(both), ACT.Square).then_inc(q_squared, 1)
                        if t >= 1:
                            q_features(t - 1)
                    q_features(TPB - 1)

                    def k_features(t):
                        act.wait_ge(k_arg, TPB * b + t + 1)
                        if t >= 1:
                            act.wait_ge(kf_ready, TPB * b + t)
                        nc.scalar.activation(kfe[:], arg[:, t % 2, :], ACT.Exp, bias=ngmax[:]).then_inc(k_exp, 1)

                    for t in range(TPB):
                        for u in range(2):
                            act.wait_ge(v_done, 2 * TPB * b + 2 * t + u + 1)
                            if u == 0 and t >= 2:
                                act.wait_ge(kv_tile, TPB * b + t - 1)
                            nc.scalar.activation(v[:, t % 2, 8 * u:8 * u + 8, 0:DH], psB[:, 2, :].rearrange(heads, k=DH), ACT.Copy).then_inc(v_ready, 1)
                            if u == 0:
                                act.wait_ge(k_done, TPB * b + t + 1)
                                if t >= 1:
                                    act.wait_ge(k_diag, TPB * b + t)
                                else:
                                    act.wait_ge(q_diag, TPB * b + TPB)
                                nc.scalar.activation(sq[:], psA[:].rearrange(both), ACT.Square).then_inc(k_squared, 1)
                        if t >= 1:
                            k_features(t - 1)
                    k_features(TPB - 1)
                    act.wait_ge(sums_spread, b + 1)
                    nc.scalar.activation(ksum[:], psB[:, 0:2, :].rearrange(both), ACT.Copy).then_inc(ksum_ready, 1)
                    act.wait_ge(vkwo_done, b + 1)
                    nc.scalar.activation(vkwo[:].rearrange("p c o -> p (c o)"), psA[:].rearrange(both), ACT.Copy).then_inc(vkwo_ready, 1)
                    for t in range(TPB):
                        for u in range(2):
                            act.wait_ge(qT_done, 2 * TPB * b + 2 * t + u + 1)
                            if t >= 2:
                                act.wait_ge(ao_done, TPB * b + t - 1)
                            nc.scalar.activation(qsT[:, t % 2, u * HALF:(u + 1) * HALF], psA[:, u, :], ACT.Copy).then_inc(qsT_ready, 1)

            @block.vector
            def _(dve):
                dve.sem_inc(ao_taken, 1)
                with dve.Fori(0, BATCH) as b:
                    xnb = G.xn[:, bass.ds(b, 1), :, :].rearrange("p b t d -> p (b t) d")
                    both = "p a (h k) -> p (a h) k"
                    for t in range(TPB):
                        dve.wait_ge(q_squared, TPB * b + t + 1)
                        nc.vector.reduce_sum(diag[:], sq[:].rearrange(heads, k=DH), AX.X).then_inc(q_diag, 1)
                        dve.wait_ge(qd_done, TPB * b + t + 1)
                        dash = psB[:, 2 * (t % 2):2 * (t % 2) + 2, :].rearrange(both, k=MF)
                        nc.vector.reduce_max(qmax[:], dash, AX.X)
                        nc.vector.drain()
                        nc.vector.scalar_tensor_tensor(shift[:], diag[:], DN * DN / 2.0, qmax[:], ALU.mult, ALU.add)
                        nc.vector.drain()
                        if t >= 2:
                            dve.wait_ge(q_exp, TPB * b + t - 1)
                        nc.vector.tensor_tensor(arg[:, t % 2, :].rearrange(heads, k=MF), dash, bc(shift[:], MF),
                                                ALU.subtract).then_inc(q_arg, 1)

                    def k_features(t):
                        dve.wait_ge(k_exp, TPB * b + t + 1)
                        if t >= 2:
                            dve.wait_ge(kv_tile, TPB * b + t - 1)
                        nc.vector.tensor_scalar(kf[:, t % 2, :], kfe[:], EPS_KERNEL, RATIO, ALU.add, ALU.mult).then_inc(kf_ready, 1)

                    for t in range(TPB):
                        dve.wait_ge(k_squared, TPB * b + t + 1)
                        nc.vector.reduce_sum(diag[:], sq[:].rearrange(heads, k=DH), AX.X).then_inc(k_diag, 1)
                        nc.vector.drain()
                        nc.vector.tensor_scalar(shift[:], diag[:], DN * DN / 2.0, None, ALU.mult)
                        nc.vector.drain()
                        dve.wait_ge(kd_done, TPB * b + t + 1)
                        if t >= 2:
                            dve.wait_ge(k_exp, TPB * b + t - 1)
                        else:
                            dve.wait_ge(q_exp, TPB * b + TPB - 1 + t)
                        nc.vector.tensor_tensor(arg[:, t % 2, :].rearrange(heads, k=MF), psB[:, 0:2, :].rearrange(both, k=MF),
                                                bc(shift[:], MF), ALU.subtract).then_inc(k_arg, 1)
                        if t >= 1:
                            k_features(t - 1)
                    k_features(TPB - 1)
                    dve.wait_ge(kv_tile, TPB * b + TPB)
                    nc.vector.tensor_copy(vk[:], psC[0:DH + 1, :, :].rearrange("p a n -> p (a n)")).then_inc(kv_out, 1)

                    def add_out(t):
                        dve.wait_ge(ao_done, TPB * b + t + 1)
                        nc.vector.tensor_tensor(xnb[:, t, :], xnb[:, t, :], psC[:, t % 2, 0:DM], ALU.add).then_inc(ao_taken, 1)

                    dve.wait_ge(ksum_ready, b + 1)
                    for t in range(TPB):
                        nc.vector.scalar_tensor_tensor(prod[:], qe[:, t, :], EPS_KERNEL, ksum[:], ALU.add, ALU.mult)
                        nc.vector.drain()
                        nc.vector.reduce_sum(den[:], prod[:].rearrange(heads, k=MF), AX.X)
                        nc.vector.drain()
                        nc.vector.reciprocal(inv[:], den[:])
                        nc.vector.drain()
                        if t >= 2:
                            dve.wait_ge(qT_done, 2 * TPB * b + 2 * t - 2)
                        nc.vector.scalar_tensor_tensor(qs[:, t % 2, :].rearrange(heads, k=MF), qe[:, t, :].rearrange(heads, k=MF), EPS_KERNEL,
                                                       bc(inv[:], MF), ALU.add, ALU.mult).then_inc(qs_ready, 1)
                        if t >= 2:
                            add_out(t - 2)
                    add_out(TPB - 2)
                    add_out(TPB - 1)


def ffn_a(nc, G, W):
    with Memory(nc, "f") as m:
        w1 = m.sbuf("w1", [P, DFF])
        w2 = m.sbuf("w2", [P, FFC, DM])
        b1 = m.sbuf("b1", [P, FFC])
        g1, o1b, b2, g2, o2b = (m.sbuf(n, [P, DM]) for n in ("g1", "o1b", "b2", "g2", "o2b"))
        stats = m.sbuf("stats", [P, TPB, 6])
        mv = m.sbuf("mv", [P, TPB, 2])
        rstd, var, half = (m.sbuf(n, [P, TPB]) for n in ("rstd", "var", "half"))
        o = m.sbuf("o", [P, 2, TPB, DM])
        oT = m.sbuf("oT", [P, 2, HALF])
        ex = m.sbuf("ex", [P, 2, FFC, HALF])
        hT = m.sbuf("hT", [P, 2, FFC, HALF])
        y = m.sbuf("y", [P, TPB, DM])
        psT = m.psum("psT", [P, 2, HALF])
        psH = m.psum("psH", [P, FFC, HALF])
        psY = m.psum("psY", [P, 2, HALF])
        landed = m.sem("landed")
        o_ready, turned, oT_ready, h_done, h_taken, hT_ready, y_done, y_taken = (m.sem(n) for n in (
            "o_ready", "turned", "oT_ready", "h_done", "h_taken", "hT_ready", "y_done", "y_taken"))
        block = m.block()
        LOADS = 8
        HALVES_AHEAD = 2

        def pairs(eng, batch):
            with eng.Fori(0, BATCH // 2) as i:
                for w in range(2):
                    batch(2 * i + w, w)

        @block.sync
        def _(sp):
            sp.dma_start(w1[:], W["w1"]).then_inc(landed, 16)
            sp.dma_start(w2[:], W["w2"].rearrange("(c p) o -> p c o", p=P)).then_inc(landed, 16)
            sp.dma_start(b1[:], W["b1"]).then_inc(landed, 16)
            for dst, src in ((g1, W["ln1_g"]), (o1b, W["ln1_b"]), (b2, W["b2"]), (g2, W["ln2_g"]), (o2b, W["ln2_b"])):
                sp.dma_start(dst[:], src.unsqueeze(0).to_broadcast([P, DM])).then_inc(landed, 16)
            sp.wait_ge(landed, 16 * LOADS)

        @block.tensor
        def _(pe):
            pe.wait_ge(landed, 16 * LOADS)
            pe.sem_inc(y_done, HALVES_AHEAD)
            pe.sem_inc(h_done, 2 * FFC)

            def products(b, w):
                def up(u):
                    pe.wait_ge(oT_ready, 2 * b + u + 1 + HALVES_AHEAD)
                    for c in range(FFC):
                        pe.wait_ge(h_taken, FFC * (2 * b + u) + c + 1)
                        nc.tensor.matmul(psH[:, c, :], w1[:, c * P:(c + 1) * P], oT[:, u, :], start=True, stop=True).then_inc(h_done, 1)

                def down(u):
                    pe.wait_ge(hT_ready, 2 * b + u + 1)
                    pe.wait_ge(y_taken, 2 * b + u + 1)
                    for t in range(4):
                        for c in range(FFC):
                            last = nc.tensor.matmul(psY[:, u, t * DM:(t + 1) * DM], hT[:, u, c, t * P:(t + 1) * P], w2[:, c, :],
                                                    start=(c == 0), stop=(c == FFC - 1))
                    last.then_inc(y_done, 1)

                for u in range(2):
                    pe.wait_ge(o_ready, 2 * b + u + 1)
                    pe.wait_ge(oT_ready, 2 * b + u + 1)
                    for t in range(4):
                        last = nc.tensor.transpose(psT[:, u, t * P:(t + 1) * P], o[:, w, 4 * u + t, :], G.ident[:])
                    last.then_inc(turned, 1)
                up(0)
                up(1)
                down(0)
                down(1)

            pairs(pe, products)

        @block.scalar
        def _(act):
            act.wait_ge(landed, 16 * LOADS)
            act.sem_inc(oT_ready, HALVES_AHEAD)
            act.sem_inc(h_taken, FFC)

            def exponentials(b, w):
                for u in range(2):
                    act.wait_ge(turned, 2 * b + u + 1)
                    act.wait_ge(h_done, FFC * (2 * b + u) + FFC)
                    nc.scalar.activation(oT[:, u, :], psT[:, u, :], ACT.Copy).then_inc(oT_ready, 1)
                for u in range(2):
                    for c in range(FFC):
                        act.wait_ge(h_done, FFC * (2 * b + u) + c + 1 + 2 * FFC)
                        if c == 0:
                            act.wait_ge(y_done, 2 * b + u + 1)
                        nc.scalar.activation(ex[:, u, c, :], psH[:, c, :], ACT.Exp, bias=b1[:, c:c + 1])
                        last = nc.scalar.activation(hT[:, u, c, :], psH[:, c, :], ACT.Relu, bias=b1[:, c:c + 1])
                        last.then_inc(h_taken, 1)

            pairs(act, exponentials)

        @block.vector
        def _(dve):
            dve.wait_ge(landed, 16 * LOADS)
            dve.sem_inc(y_taken, HALVES_AHEAD)

            def normalize(rows, out, gain, offset, ready):
                for t in range(TPB):
                    nc.vector.bn_stats(stats[:, t, :], rows[:, t, :])
                nc.vector.drain()
                for t in range(TPB):
                    nc.vector.bn_aggr(mv[:, t, :], stats[:, t, :])
                nc.vector.drain()
                rsqrt(nc, rstd[:], mv[:, :, 1], EPS_LN_A, var[:], half[:])
                for t in range(TPB):
                    nc.vector.scalar_tensor_tensor(y[:, t, :], rows[:, t, :], mv[:, t, 0:1], gain[:], ALU.subtract, ALU.mult)
                nc.vector.drain()
                for t in range(TPB):
                    last = nc.vector.scalar_tensor_tensor(out[:, t, :], y[:, t, :], rstd[:, t:t + 1], offset[:], ALU.mult, ALU.add)
                    if ready is not None and t % 4 == 3:
                        last.then_inc(ready, 1)
                nc.vector.drain()

            def batch_of(tensor, b):
                return tensor[:, b:b + 1, :, :] if isinstance(b, int) else tensor[:, bass.ds(b, 1), :, :]

            flat = "p b t d -> p (b t) d"

            def first_norm(b, w):
                normalize(batch_of(G.xn, b).rearrange(flat), batch_of(o, w).rearrange(flat), g1, o1b, o_ready)

            def elu(b):
                for u in range(2):
                    dve.wait_ge(h_taken, FFC * (2 * b + u) + 2 * FFC)
                    nc.vector.tensor_scalar(ex[:, u, :, :], ex[:, u, :, :], 1.0, -1.0, ALU.min, ALU.add)
                    nc.vector.drain()
                    nc.vector.tensor_tensor(hT[:, u, :, :], hT[:, u, :, :], ex[:, u, :, :], ALU.add).then_inc(hT_ready, 1)

            def second_norm(b, w):
                ow, xb = batch_of(o, w).rearrange(flat), batch_of(G.x, b).rearrange(flat)
                nc.vector.tensor_tensor(y[:], ow, b2[:].unsqueeze(1).to_broadcast([P, TPB, DM]), ALU.add)
                nc.vector.drain()
                for u in range(2):
                    dve.wait_ge(y_done, 2 * b + u + 1 + HALVES_AHEAD)
                    nc.vector.tensor_tensor(ow[:, 4 * u:4 * u + 4, :], y[:, 4 * u:4 * u + 4, :],
                                            psY[:, u, :].rearrange("p (t d) -> p t d", d=DM), ALU.add).then_inc(y_taken, 1)
                nc.vector.drain()
                normalize(ow, ow, g2, o2b, None)
                nc.vector.tensor_tensor(xb, xb, ow, ALU.add)

            first_norm(0, 0)
            with dve.Fori(0, BATCH - 1) as b:
                elu(b)
                first_norm(b + 1, (b + 1) % 2)
                second_norm(b, b % 2)
            elu(BATCH - 1)
            second_norm(BATCH - 1, (BATCH - 1) % 2)


def moe(nc, stage, G, W):
    with Memory(nc, stage) as m:
        L = Shared()
        L.w8 = m.sbuf("w8", [P, TILES, TOPK])
        L.place = m.sbuf("place", [P, TILES, TOPK], I32)
        L.wg = m.sbuf("wg", [P, EXPERTS, INTER])
        L.tile_expert = m.sbuf("tile_expert", [1, HALVES * HALF_TILES], I32)
        G.xn = m.sbuf("xn", [P, BATCH, TPB, DM])
        L.wg_landed, L.shared_landed, L.owners_landed = m.sem("wg_landed"), m.sem("shared_landed"), m.sem("owners_landed")
        L.scattered = [m.sem(f"scattered{i}") for i in range(HALVES)]
        with Memory(nc, stage + "r") as r:
            G.xnT = r.sbuf("xnT", [P, BATCH, SEQ])
            L.wgs = r.sbuf("wgs", [P, INTER])
            L.wds = r.sbuf("wds", [INTER, DM])
            L.picked = r.sbuf("picked", [P, TILES, EXPERTS], BF16)
            L.before = r.sbuf("before", [P, TILES + 1, EXPERTS], BF16)
            L.index = r.sbuf("index", [P, TILES, TOPK])
            L.earlier = r.sbuf("earlier", [P, P], BF16)
            L.ones_bf = r.sbuf("ones_bf", [P, P], BF16)
            L.base = r.sbuf("base", [P, BATCH, EXPERTS])
            L.column = r.sbuf("column", [P, EXPERTS])
            L.owner = r.sbuf("owner", [P, HALVES, OWNER_COLUMNS], I32)
            layernorm(nc, stage + "0", G)
            router(nc, stage + "1", G, W, L)
            plan(nc, stage + "2", G, L)
            dispatch(nc, stage + "3", G, L)
        experts(nc, stage + "4", G, W, L)


def router(nc, stage, G, W, L):
    w8, picked, before, index = L.w8, L.picked, L.before, L.index
    with Memory(nc, stage) as m:
        wr = m.sbuf("wr", [P, EXPERTS])
        bias = m.sbuf("bias", [P, EXPERTS])
        xT = m.sbuf("xT", [P, 2, SEQ])
        probs = m.sbuf("probs", [P, 2, TPB, EXPERTS])
        logits = m.sbuf("logits", [P, 2, TPB, EXPERTS])
        top = m.sbuf("top", [P, TPB, TOPK])
        at = m.sbuf("at", [P, TPB, TOPK], mybir.dt.uint32)
        total, inverse = m.sbuf("total", [P, TPB]), m.sbuf("inverse", [P, TPB])
        scratch = m.sbuf("scratch", [P, 1])
        ps = m.psum("ps", [P, 2, TPB // 2, 2, HALF // 2])
        landed, xT_ready, logits_done, logits_ready, probs_ready = (m.sem(n) for n in (
            "landed", "xT_ready", "logits_done", "logits_ready", "probs_ready"))
        block = m.block()
        AHEAD = 2

        def pairs(eng, batch):
            with eng.Fori(0, BATCH // 2) as i:
                for w in range(2):
                    batch(2 * i + w, w)

        @block.sync
        def _(sp):
            sp.dma_start(wr[:], W["routerT"]).then_inc(landed, 16)
            sp.dma_start(bias[:], W["expert_bias"].unsqueeze(0).to_broadcast([P, EXPERTS])).then_inc(landed, 16)
            sp.dma_start(L.wgs[:], W["w_gate_sharedT"]).then_inc(L.shared_landed, 16)
            sp.dma_start(L.wds[:], W["w_down_sharedT"]).then_inc(L.shared_landed, 16)
            sp.dma_start(L.wg[:], W["w_gateT"]).then_inc(L.wg_landed, 16)
            sp.wait_ge(landed, 32)

        @block.gpsimd
        def _(pool):
            def bring(b, w):
                pool.wait_ge(logits_done, b - 2 + 1 + AHEAD)
                nc.gpsimd.tensor_copy(xT[:, w, :], G.xnT[:, bass.ds(b, 1), :].rearrange("p b n -> p (b n)")).then_inc(xT_ready, 1)

            pairs(pool, bring)

        @block.tensor
        def _(pe):
            pe.sem_inc(logits_done, AHEAD)
            pe.wait_ge(landed, 32)

            def multiply(b, w):
                pe.wait_ge(xT_ready, b + 1)
                pe.wait_ge(logits_ready, b - 2 + 1 + AHEAD)
                for t in range(TPB):
                    last = nc.tensor.matmul(ps[:, w, t // 2, t % 2, 0:EXPERTS], xT[:, w, t * P:(t + 1) * P], wr[:], start=True, stop=True)
                last.then_inc(logits_done, 1)

            pairs(pe, multiply)

        @block.scalar
        def _(act):
            def squash(b, w):
                act.wait_ge(logits_ready, b + 1 + AHEAD)
                nc.scalar.activation(probs[:, w, :, :], logits[:, w, :, :], ACT.Sigmoid).then_inc(probs_ready, 1)

            pairs(act, squash)

        @block.vector
        def _(dve):
            nc.vector.memset(before[:, 0, :], 0.0)
            dve.sem_inc(logits_ready, AHEAD)
            dve.wait_ge(landed, 32)

            def add_bias(b, w):
                dve.wait_ge(logits_done, b + 1 + AHEAD)
                nc.vector.tensor_tensor(logits[:, w, :, :], ps[:, w, :, :, 0:EXPERTS].rearrange("p a b e -> p (a b) e"),
                                        bias[:].unsqueeze(1).to_broadcast([P, TPB, EXPERTS]), ALU.add).then_inc(logits_ready, 1)

            def choose(b, w):
                tiles = bass.ds(b * TPB, TPB)
                dve.wait_ge(probs_ready, b + 1)
                nc.vector.memset(scratch[:], 0.0)
                for t in range(TPB):
                    nc.vector.max(top[:, t, :], probs[:, w, t, :])
                nc.vector.drain()
                for t in range(TPB):
                    nc.vector.max_index(at[:, t, :], top[:, t, :], probs[:, w, t, :])
                for t in range(TPB):
                    nc.vector.match_replace(logits[:, w, t, :], top[:, t, :], probs[:, w, t, :], -1.0)
                nc.vector.reduce_sum(total[:], top[:], AX.X)
                nc.vector.drain()
                nc.vector.tensor_copy(index[:, tiles, :], at[:])
                nc.vector.tensor_scalar(total[:], total[:], 1e-9, None, ALU.add)
                nc.vector.tensor_scalar(picked[:, tiles, :], logits[:, w, :, :], 0.0, None, ALU.is_lt)
                nc.vector.drain()
                nc.vector.reciprocal(inverse[:], total[:])
                for t in range(TPB):
                    nc.vector.tensor_tensor(before[:, bass.ds(b * TPB + t + 1, 1), :], before[:, bass.ds(b * TPB + t, 1), :],
                                            picked[:, bass.ds(b * TPB + t, 1), :], ALU.add)
                    nc.vector.drain()
                nc.vector.scalar_tensor_tensor(w8[:, tiles, :], top[:], ROUTED_SCALE, bc(inverse[:], TOPK), ALU.mult, ALU.mult)
                nc.vector.drain()

            with dve.Fori(0, BATCH // 2) as i:
                for w in range(2):
                    add_bias(2 * i + w, w)
                for w in range(2):
                    choose(2 * i + w, w)


def plan(nc, stage, G, L):
    before, base, ones_bf, earlier, column = L.before, L.base, L.ones_bf, L.earlier, L.column
    with Memory(nc, stage) as m:
        count = m.sbuf("count", [P, HALVES, EXPERTS], I32)
        first = m.sbuf("first", [P, EXPERTS])
        tiles = m.sbuf("tiles", [P, HALVES, EXPERTS])
        ends = m.sbuf("ends", [P, 2, HALVES, EXPERTS])
        junk = m.sbuf("junk", [P, EXPERTS])
        number = m.sbuf("number", [P, OWNER_COLUMNS], I32)
        number_f = m.sbuf("number_f", [P, OWNER_COLUMNS])
        owner = m.sbuf("owner", [P, HALVES, OWNER_COLUMNS])
        ps = m.psum("ps", [P, HALVES, HALF])
        made, counted = m.sem("made"), m.sem("counted")
        block = m.block()

        @block.gpsimd
        def _(pool):
            nc.gpsimd.iota(number[:], [[P, OWNER_COLUMNS]], base=0, channel_multiplier=1)
            nc.gpsimd.iota(column[:], [[1, EXPERTS]], base=0, channel_multiplier=0, allow_small_or_imprecise_dtypes=True)
            nc.gpsimd.memset(ones_bf[:], 1.0).then_inc(made, 1)
            pool.wait_ge(made, 1)
            nc.gpsimd.affine_select(out=earlier[:], in_=ones_bf[:], compare_op=ALU.is_gt, fill=0.0, base=0,
                                    pattern=[[1, P]], channel_multiplier=-1).then_inc(made, 1)
            pool.wait_ge(made, 2)

        @block.tensor
        def _(pe):
            pe.wait_ge(made, 1)
            for half in range(HALVES):
                last = nc.tensor.matmul(ps[:, half, 0:EXPERTS], ones_bf[:], before[:, TPH * (half + 1), :], start=True, stop=True)
            last.then_inc(counted, 1)

        @block.vector
        def _(dve):
            dve.wait_ge(made, 2)
            nc.vector.tensor_copy(number_f[:], number[:])
            dve.wait_ge(counted, 1)
            nc.vector.tensor_copy(first[:], ps[:, 0, 0:EXPERTS])
            nc.vector.drain()
            nc.vector.tensor_scalar(count[:, 0, :], first[:], float(P - 1), None, ALU.add)
            nc.vector.scalar_tensor_tensor(count[:, 1, :], ps[:, 1, 0:EXPERTS], float(P - 1), first[:], ALU.add, ALU.subtract)
            nc.vector.drain()
            nc.vector.tensor_scalar(count[:], count[:], P.bit_length() - 1, None, ALU.arith_shift_right)
            nc.vector.drain()
            nc.vector.tensor_copy(tiles[:], count[:])
            nc.vector.tensor_copy(ends[:, 0, :, :], count[:])
            nc.vector.drain()
            step, now = 1, 0
            while step < EXPERTS:
                nc.vector.tensor_copy(ends[:, 1 - now, :, 0:step], ends[:, now, :, 0:step])
                nc.vector.tensor_tensor(ends[:, 1 - now, :, step:], ends[:, now, :, step:], ends[:, now, :, 0:EXPERTS - step], ALU.add)
                nc.vector.drain()
                step, now = 2 * step, 1 - now
            nc.vector.tensor_tensor(tiles[:], ends[:, now, :, :], tiles[:], ALU.subtract)
            nc.vector.drain()
            nc.vector.tensor_scalar(base[:, 0, :], tiles[:, 0, :], float(P), None, ALU.mult)
            nc.vector.tensor_scalar(base[:, 1, :], tiles[:, 0, :], float(P), None, ALU.mult)
            for b in (2, 3):
                nc.vector.scalar_tensor_tensor(base[:, b, :], tiles[:, 1, :], float(P), first[:], ALU.mult, ALU.subtract)
            for half in range(HALVES):
                for j in range(OWNER_COLUMNS):
                    nc.vector.tensor_scalar(junk[:], ends[:, now, half, :], number_f[:, j:j + 1], 0.0, ALU.is_le, ALU.add,
                                            accum_out=owner[:, half, j:j + 1])
                    nc.vector.drain()
            nc.vector.tensor_scalar(L.owner[:], owner[:], float(EXPERTS - 1), None, ALU.min)


EARLY_TILES = 12


def scatter(nc, G, L, t):
    for k in range(TOPK):
        nc.gpsimd.indirect_dma_start(G.slots_in[t // TPH], bass.IndirectOffsetOnAxis(L.place[:, t, k:k + 1], 0),
                                     G.xn[:, t // TPB, t % TPB, :], None).then_inc(L.scattered[t // TPH], 16)


def dispatch(nc, stage, G, L):
    picked, before, base, index, column, place = L.picked, L.before, L.base, L.index, L.column, L.place
    earlier, ones_bf, wgs, wds = L.earlier, L.ones_bf, L.wgs, L.wds
    CHUNK = 2
    with Memory(nc, stage) as m:
        rank = m.sbuf("rank", [P, TPB, EXPERTS])
        junk = m.sbuf("junk", [P, TOPK, EXPERTS])
        slot = m.sbuf("slot", [P, CHUNK, TOPK])
        slot_i, low = m.sbuf("slot_i", [P, CHUNK, TOPK], I32), m.sbuf("low", [P, CHUNK, TOPK], I32)
        hs = m.sbuf("hs", [INTER, 2, HALF])
        ps = m.psum("ps", [P, TPB // 2, 2, HALF // 2])
        psh = m.psum("psh", [P, 2, HALF])
        pss = m.psum("pss", [P, 2, HALF])
        rounds, ranked, placed, up_done, hs_ready, shared_done = (m.sem(n) for n in (
            "rounds", "ranked", "placed", "up_done", "hs_ready", "shared_done"))
        block = m.block()
        written = m.sem("written")
        WORKERS = 3

        def end_round(eng):
            eng.drain()
            eng.sem_inc(rounds, 1)

        @block.sync
        def _(sp):
            for half in range(HALVES):
                for j in range(OWNER_COLUMNS):
                    n = min(P, HALF_TILES - j * P)
                    at = half * HALF_TILES + j * P
                    sp.dma_start(G.owner_dram[at:at + n, :], L.owner[0:n, half, j:j + 1]).then_inc(written, 16)
            sp.wait_ge(written, 16 * HALVES * OWNER_COLUMNS)
            sp.dma_start(L.tile_expert[:], G.owner_dram.rearrange("t a -> a t")).then_inc(L.owners_landed, 16)

        @block.tensor
        def _(pe):
            end_round(pe)
            pe.wait_ge(L.shared_landed, 32)
            with pe.Fori(0, BATCH) as b:
                pe.wait_ge(rounds, WORKERS * b + WORKERS)
                for t in range(TPB):
                    out = ps[:, t // 2, t % 2, 0:EXPERTS]
                    nc.tensor.matmul(out, earlier[:], picked[:, bass.ds(b * TPB + t, 1), :].rearrange("p a e -> p (a e)"),
                                     start=True, stop=False)
                    last = nc.tensor.matmul(out, ones_bf[:], before[:, bass.ds(b * TPB + t, 1), :].rearrange("p a e -> p (a e)"),
                                            start=False, stop=True)
                last.then_inc(ranked, 1)
                for u in range(2):
                    nc.tensor.matmul(psh[0:INTER, u, :], wgs[:],
                                     G.xnT[:, bass.ds(b, 1), u * HALF:(u + 1) * HALF].rearrange("p b n -> p (b n)"),
                                     start=True, stop=True).then_inc(up_done, 1)
                for u in range(2):
                    pe.wait_ge(hs_ready, 2 * b + u + 1)
                    for t in range(4):
                        last = nc.tensor.matmul(pss[:, u, t * DM:(t + 1) * DM], hs[:, u, t * P:(t + 1) * P], wds[:], start=True, stop=True)
                    last.then_inc(shared_done, 1)
                end_round(pe)

        @block.scalar
        def _(act):
            end_round(act)
            with act.Fori(0, BATCH) as b:
                for u in range(2):
                    act.wait_ge(up_done, 2 * b + u + 1)
                    nc.scalar.activation(hs[:, u, :], psh[0:INTER, u, :], ACT.Silu).then_inc(hs_ready, 1)
                end_round(act)

        @block.vector
        def _(dve):
            end_round(dve)
            with dve.Fori(0, BATCH) as b:
                dve.wait_ge(rounds, WORKERS * b + WORKERS)
                dve.wait_ge(ranked, b + 1)
                nc.vector.tensor_tensor(rank[:], ps[:, :, :, 0:EXPERTS].rearrange("p a b e -> p (a b) e"),
                                        base[:, bass.ds(b, 1), :].to_broadcast([P, TPB, EXPERTS]), ALU.add)
                nc.vector.drain()
                ib = index[:, bass.ds(b * TPB, TPB), :]
                for t0 in range(0, TPB, CHUNK):
                    for t in range(CHUNK):
                        for k in range(TOPK):
                            nc.vector.scalar_tensor_tensor(junk[:, k, :], column[:], ib[:, t0 + t, k:k + 1], rank[:, t0 + t, :],
                                                           ALU.is_equal, ALU.mult, accum_out=slot[:, t, k:k + 1])
                        nc.vector.drain()
                    nc.vector.tensor_copy(slot_i[:], slot[:])
                    nc.vector.drain()
                    at = place[:, bass.ds(b * TPB + t0, CHUNK), :]
                    nc.vector.tensor_scalar(low[:], slot_i[:], P - 1, 2, ALU.bitwise_and, ALU.logical_shift_left)
                    nc.vector.tensor_scalar(at, slot_i[:], 7, 3, ALU.logical_shift_right, ALU.bitwise_and)
                    nc.vector.drain()
                    nc.vector.tensor_scalar(slot_i[:], slot_i[:], ~(GROUP_SLOTS - 1), None, ALU.bitwise_and)
                    nc.vector.tensor_tensor(at, at, low[:], ALU.bitwise_or)
                    nc.vector.drain()
                    nc.vector.tensor_tensor(at, at, slot_i[:], ALU.bitwise_or).then_inc(placed, 1)
                    nc.vector.drain()
                xb = G.x[:, bass.ds(b, 1), :, :].rearrange("p b t d -> p (b t) d")
                for u in range(2):
                    dve.wait_ge(shared_done, 2 * b + u + 1)
                    nc.vector.tensor_tensor(xb[:, 4 * u:4 * u + 4, :], xb[:, 4 * u:4 * u + 4, :],
                                            pss[:, u, :].rearrange("p (t d) -> p t d", d=DM), ALU.add)
                end_round(dve)

        @block.gpsimd
        def _(pool):
            for t in range(EARLY_TILES):
                if t % CHUNK == 0:
                    pool.wait_ge(placed, t // CHUNK + 1)
                scatter(nc, G, L, t)


def experts(nc, stage, G, W, L):
    tile_expert, place, w8 = L.tile_expert, L.place, L.w8
    DEEP = 4
    PEEL = 3
    FIRST_STAGES = GROUPS - TPH * DEEP
    RING = BATCH
    PE, DVE = mybir.EngineType.PE, mybir.EngineType.DVE
    assert FIRST_STAGES >= HALF_GROUPS and (GROUPS - 1 - PEEL) % DEEP == 0 and HALF_GROUPS % DEEP == 0 and TPB == TOPK
    with Memory(nc, stage) as m:
        wd = m.sbuf("wd", [INTER, EXPERTS, DM])
        wg2, wd2 = L.wg[:].rearrange("p e i -> p (e i)"), wd[:].rearrange("p e d -> p (e d)")
        wd_landed = m.sem("wd_landed")
        rows = m.sbuf("rows", [P, DEEP, GROUP, DM])
        xT = m.sbuf("xT", [P, 2, HALF])
        up_w = m.sbuf("up_w", [P, DEEP, GROUP, INTER])
        hT = m.sbuf("hT", [INTER, 2, GROUP, P])
        y = m.sbuf("y", [P, DEEP, GROUP, DM])
        sum8 = m.sbuf("sum8", [P, DM])
        got = G.xn
        psX = m.psum("psX", [P, 2, HALF])
        psH = m.psum("psH", [INTER, 2, GROUP, P])
        psY = m.psum("psY", [P, 2, HALF])
        rows_landed = [m.sem(f"rows_landed{i}") for i in range(DEEP)]
        stored = [m.sem(f"stored{i}") for i in range(DEEP)]
        x_turned, xT_ready, staged, up_done, hT_ready, down_done, y_ready = (m.sem(n) for n in (
            "x_turned", "xT_ready", "staged", "up_done", "hT_ready", "down_done", "y_ready"))
        AHEAD = DEEP
        gathered = [m.sem(f"gathered{i}") for i in range(RING)]
        added = m.sem("added")
        block = m.block()
        src, dst = ([s.rearrange("(g p j) d -> g p (j d)", p=P, j=GROUP) for s in slots] for slots in (G.slots_in, G.slots_out))
        flat = "p j d -> p (j d)"

        def done(g):
            return g + 1 + AHEAD

        def owners(g, engine):
            at = tile_expert[0:1, g * GROUP:(g + 1) * GROUP] if isinstance(g, int) else tile_expert[0:1, bass.ds(g * GROUP, GROUP)]
            _, e = nc.values_load_multi_w_load_instructions(
                at, engines=[engine], min_val=0, max_val=EXPERTS - 1,
                skip_runtime_bounds_check_because="the plan clamps it to the last expert")
            return e

        def stores(half):
            return 16 * ((half + 1) * HALF_GROUPS // DEEP + 1)

        @block.sync
        def _(sp):
            def rows_of(slots, g):
                return slots[g] if isinstance(g, int) else slots[bass.ds(g, 1)].rearrange("g p n -> (g p) n")

            def load(half, g, u):
                sp.dma_start(rows[:, u % DEEP, :, :].rearrange(flat), rows_of(src[half], g)).then_inc(rows_landed[u % DEEP], 16)

            def store(half, g, u):
                sp.wait_ge(y_ready, done(half * HALF_GROUPS + g))
                sp.dma_start(rows_of(dst[half], g), y[:, u % DEEP, :, :].rearrange(flat)).then_inc(stored[u % DEEP], 16)

            for s in stored:
                sp.sem_inc(s, 16)
            sp.dma_start(wd[:], W["w_downT"]).then_inc(wd_landed, 16)
            sp.wait_ge(L.scattered[0], 16 * TPH * TOPK)
            for u in range(DEEP):
                load(0, u, u)
            for half in range(HALVES):
                with sp.Fori(0, HALF_GROUPS // DEEP - 1) as i:
                    for u in range(DEEP):
                        sp.wait_ge(x_turned, done(i * DEEP + half * HALF_GROUPS + u))
                        load(half, i * DEEP + DEEP + u, u)
                        store(half, i * DEEP + u, u)
                if half + 1 < HALVES:
                    sp.wait_ge(L.scattered[half + 1], 16 * TPH * TOPK)
                for u in range(DEEP):
                    if half + 1 < HALVES:
                        sp.wait_ge(x_turned, done((half + 1) * HALF_GROUPS - DEEP + u))
                        load(half + 1, u, u)
                    store(half, HALF_GROUPS - DEEP + u, u)
            for s in stored:
                sp.wait_ge(s, stores(HALVES - 1))

        @block.gpsimd
        def _(pool):
            for t in range(EARLY_TILES, TILES):
                scatter(nc, G, L, t)
            pool.wait_ge(L.scattered[1], 16 * TPH * TOPK)
            for t in range(TILES):
                if t % TPH == 0:
                    for s in stored:
                        pool.wait_ge(s, stores(t // TPH))
                if t >= RING:
                    pool.wait_ge(added, t - RING + 1)
                for k in range(TOPK):
                    nc.gpsimd.indirect_dma_start(got[:, t % RING, k, :], None, G.slots_out[t // TPH],
                                                 bass.IndirectOffsetOnAxis(place[:, t, k:k + 1], 0)).then_inc(gathered[t % RING], 16)

        @block.tensor
        def _(pe):
            for s in (x_turned, up_done, down_done):
                pe.sem_inc(s, AHEAD)
            pe.wait_ge(L.wg_landed, 16)
            pe.wait_ge(L.owners_landed, 16)

            def turn(g, u, landings):
                pe.wait_ge(rows_landed[u % DEEP], 16 * landings)
                pe.wait_ge(xT_ready, done(g - 2))
                for j in range(GROUP):
                    last = nc.tensor.transpose(psX[:, u % 2, j * P:(j + 1) * P], rows[:, u % DEEP, j, :], G.ident[:])
                last.then_inc(x_turned, 1)

            def up(g, u):
                pe.wait_ge(L.wg_landed, 16)
                pe.wait_ge(xT_ready, done(g))
                pe.wait_ge(staged, done(g))
                pe.wait_ge(hT_ready, done(g - 2))
                for j in range(GROUP):
                    last = nc.tensor.matmul(psH[:, u % 2, j, :], up_w[:, u % DEEP, j, :], xT[:, u % 2, j * P:(j + 1) * P],
                                            start=True, stop=True)
                last.then_inc(up_done, 1)

            def down(g, u, e):
                pe.wait_ge(hT_ready, done(g))
                pe.wait_ge(y_ready, done(g - 2))
                for j in range(GROUP):
                    last = nc.tensor.matmul(psY[:, u % 2, j * DM:(j + 1) * DM], hT[:, u % 2, j, :],
                                            wd2[:, bass.ds(e[j] * DM, DM)], start=True, stop=True)
                last.then_inc(down_done, 1)

            turn(0, 0, 1)
            def step(g, u, landings):
                up(g, u)
                if landings is not None:
                    turn(g + 1, u + 1, landings)
                if not (isinstance(g, int) and g == 0):
                    down(g - 1, u - 1, owners(g - 1, PE))

            for g in range(PEEL):
                if g == 1:
                    pe.wait_ge(wd_landed, 16)
                step(g, g, (g + 1) // DEEP + 1)
            with pe.Fori(0, (GROUPS - 1 - PEEL) // DEEP) as i:
                for u in range(DEEP):
                    step(i * DEEP + PEEL + u, PEEL + u, i + 2)
            step(GROUPS - 1, GROUPS - 1, None)
            down(GROUPS - 1, GROUPS - 1, owners(GROUPS - 1, PE))

        @block.scalar
        def _(act):
            for s in (xT_ready, hT_ready, y_ready):
                act.sem_inc(s, AHEAD)

            def take_xT(g, u):
                act.wait_ge(x_turned, done(g))
                act.wait_ge(up_done, done(g - 2))
                nc.scalar.activation(xT[:, u % 2, :], psX[:, u % 2, :], ACT.Copy).then_inc(xT_ready, 1)

            def take_y(g, u, left):
                act.wait_ge(down_done, done(g))
                act.wait_ge(stored[u % DEEP], 16 * (left + 1))
                nc.scalar.activation(y[:, u % DEEP, :, :].rearrange(flat), psY[:, u % 2, :], ACT.Copy).then_inc(y_ready, 1)

            def step(g, u, left, more=True):
                act.wait_ge(up_done, done(g))
                act.wait_ge(down_done, done(g - 2))
                nc.scalar.activation(hT[:, u % 2, :, :], psH[:, u % 2, :, :], ACT.Silu).then_inc(hT_ready, 1)
                if more:
                    take_xT(g + 1, u + 1)
                if not (isinstance(g, int) and g == 0):
                    take_y(g - 1, u - 1, left)

            take_xT(0, 0)
            for g in range(PEEL):
                step(g, g, 0)
            with act.Fori(0, (GROUPS - 1 - PEEL) // DEEP) as i:
                for u in range(DEEP):
                    step(i * DEEP + PEEL + u, PEEL + u, i + (PEEL + u - 1) // DEEP)
            step(GROUPS - 1, GROUPS - 1, (GROUPS - 2) // DEEP, more=False)
            take_y(GROUPS - 1, GROUPS - 1, (GROUPS - 1) // DEEP)

        @block.vector
        def _(dve):
            x = G.x[:].rearrange("p b t d -> p (b t) d")
            dve.sem_inc(staged, AHEAD)
            dve.wait_ge(L.owners_landed, 16)
            dve.wait_ge(L.wg_landed, 16)

            def stage(g, u):
                e = owners(g, DVE)
                dve.wait_ge(L.wg_landed, 16)
                dve.wait_ge(up_done, done(g - DEEP))
                for j in range(GROUP):
                    last = nc.vector.tensor_copy(up_w[:, u % DEEP, j, :], wg2[:, bass.ds(e[j] * INTER, INTER)])
                last.then_inc(staged, 1)

            def combine(i, ring):
                dve.wait_ge(gathered[ring], 16 * TOPK * i + 16 * TOPK)
                t = bass.ds(i * RING + ring, 1)
                xt, wt = x[:, t, :].rearrange("p a d -> p (a d)"), w8[:, t, :].rearrange("p a k -> p (a k)")
                rows8 = got[:, ring, :, :]
                nc.vector.tensor_tensor(rows8, rows8, bc(wt, DM), ALU.mult)
                nc.vector.drain()
                nc.vector.reduce_sum(sum8[:], rows8.rearrange("p k d -> p d k"), AX.X)
                nc.vector.drain()
                nc.vector.tensor_tensor(xt, xt, sum8[:], ALU.add).then_inc(added, 1)

            with dve.Fori(0, FIRST_STAGES // DEEP) as i:
                for u in range(DEEP):
                    stage(i * DEEP + u, u)
            with dve.Fori(0, TPH // RING) as i:
                for ring in range(RING):
                    for u in range(DEEP):
                        stage(i * (RING * DEEP) + FIRST_STAGES + ring * DEEP + u, u)
                    combine(i, ring)
            with dve.Fori(TPH // RING, TILES // RING) as i:
                for ring in range(RING):
                    combine(i, ring)


def attn_b(nc, stage, G, W):
    with Memory(nc, stage) as m:
        L = Shared()
        L.v = m.sbuf("v", [P, TILES, HB, VW])
        L.wo = m.sbuf("wo", [P, DM])
        L.wo_landed = m.sem("wo_landed")
        with Memory(nc, stage + "n") as n:
            normed(G, n)
            layernorm(nc, stage + "0", G)
            project_b(nc, stage + "1", G, W, L)
        attend_b(nc, stage + "2", G, L)


def project_b(nc, stage, G, W, L):
    with Memory(nc, stage) as m:
        wq, wk, wv, bo = (m.sbuf(n, [P, DM]) for n in ("wq", "wk", "wv", "bo"))
        xT = m.sbuf("xT", [P, 2, SEQ])
        parts = m.sbuf("parts", [P, 2, 2, 3, SEQ], BF16)
        rest = m.sbuf("rest", [P, 2, SEQ])
        ps = m.psum("ps", [P, 2, 2, HALF])
        psv = m.psum("psv", [P, 2, HALF])
        landed, cleared, v_room, xT_ready, qk_done, qk_taken, v_done, v_taken, high_ready, parts_ready = (m.sem(n) for n in (
            "landed", "cleared", "v_room", "xT_ready", "qk_done", "qk_taken", "v_done", "v_taken", "high_ready", "parts_ready"))
        stacked = [m.sem(f"stacked{w}") for w in range(2)]
        block = m.block()
        COPIES = 6
        AHEAD = 2

        def pairs(eng, batch):
            with eng.Fori(0, BATCH // 2) as i:
                for w in range(2):
                    batch(2 * i + w, w, i)

        @block.sync
        def _(sp):
            for dst, src in ((wq, W["bwqT"]), (wk, W["bwkT"]), (wv, W["bwvT"]), (bo, W["bo"].unsqueeze(0).to_broadcast([P, DM]))):
                sp.dma_start(dst[:], src).then_inc(landed, 16)
            sp.dma_start(L.wo[:], W["bwoT"]).then_inc(L.wo_landed, 16)
            for s in stacked:
                sp.sem_inc(s, 16)

            def stack(b, w, i):
                for n, rows in enumerate((G.q_stack.rearrange("(i j p) n -> i p j n", i=3, j=3),
                                          G.k_stack.rearrange("(i j p) n -> j p i n", i=3, j=3))):
                    sp.wait_ge(parts_ready, 2 * b + n + 1)
                    for part in range(3):
                        sp.dma_start(rows[part][:, :, bass.ds(b * SEQ, SEQ)],
                                     parts[:, w, n, part, :].unsqueeze(1).to_broadcast([P, 3, SEQ])).then_inc(stacked[w], 16)

            pairs(sp, stack)
            for s in stacked:
                sp.wait_ge(s, 16 * COPIES * (BATCH // 2) + 16)

        @block.gpsimd
        def _(pool):
            def bring(b, w, i):
                pool.wait_ge(v_done, b - 2 + 1 + AHEAD)
                nc.gpsimd.tensor_copy(xT[:, w, :], G.xnT[:, bass.ds(b, 1), :].rearrange("p b n -> p (b n)")).then_inc(xT_ready, 1)

            pairs(pool, bring)

        @block.tensor
        def _(pe):
            pe.wait_ge(landed, 64)
            pe.sem_inc(v_done, AHEAD)

            def multiply(b, w, i):
                pe.wait_ge(xT_ready, b + 1)
                for n, wqk in enumerate((wq, wk)):
                    pe.wait_ge(qk_taken, 2 * (b - 1) + n + 1 + AHEAD)
                    for u in range(2):
                        last = nc.tensor.matmul(ps[:, n, u, :], wqk[:], xT[:, w, u * HALF:(u + 1) * HALF], start=True, stop=True)
                    last.then_inc(qk_done, 1)
                pe.wait_ge(v_taken, b - 1 + 1 + AHEAD)
                for t in range(TPB):
                    last = nc.tensor.matmul(psv[:, t // 4, (t % 4) * DM:(t % 4 + 1) * DM], xT[:, w, t * P:(t + 1) * P], wv[:],
                                            start=True, stop=True)
                last.then_inc(v_done, 1)

            pairs(pe, multiply)

        @block.scalar
        def _(act):
            act.sem_inc(v_taken, AHEAD)
            act.wait_ge(v_room, 1)

            def take(b, w, i):
                for n in range(2):
                    act.wait_ge(qk_done, 2 * b + n + 1)
                    if n == 0:
                        act.wait_ge(stacked[w], 16 * COPIES * i + 16)
                    nc.scalar.activation(parts[:, w, n, 0, :], ps[:, n, :, :].rearrange("p u n -> p (u n)"), ACT.Copy).then_inc(high_ready, 1)
                act.wait_ge(v_done, b + 1 + AHEAD)
                nc.scalar.activation(L.v[:, bass.ds(b * TPB, TPB), :, 0:WB],
                                     psv[:].rearrange("p u (t h d) -> p (u t) h d", h=HB, d=WB), ACT.Copy).then_inc(v_taken, 1)

            pairs(act, take)

        @block.vector
        def _(dve):
            nc.vector.memset(L.v[:], 0.0).then_inc(cleared, 1)
            dve.wait_ge(cleared, 1)
            nc.vector.memset(L.v[:, :, :, WB:WB + 1], 1.0).then_inc(v_room, 1)
            dve.sem_inc(qk_taken, AHEAD)
            dve.wait_ge(landed, 64)

            def cut(b, w, i):
                for n in range(2):
                    dve.wait_ge(high_ready, 2 * b + n + 1)
                    nc.vector.tensor_tensor(rest[:, n, :], ps[:, n, :, :].rearrange("p u n -> p (u n)"), parts[:, w, n, 0, :],
                                            ALU.subtract).then_inc(qk_taken, 1)
                    nc.vector.drain()
                    nc.vector.tensor_copy(parts[:, w, n, 1, :], rest[:, n, :])
                    nc.vector.drain()
                    nc.vector.tensor_tensor(parts[:, w, n, 2, :], rest[:, n, :], parts[:, w, n, 1, :], ALU.subtract).then_inc(parts_ready, 1)
                xb = G.x[:, bass.ds(b, 1), :, :].rearrange("p b t d -> p (b t) d")
                nc.vector.tensor_tensor(xb, xb, bo[:].unsqueeze(1).to_broadcast([P, TPB, DM]), ALU.add)

            pairs(dve, cut)


def attend_b(nc, stage, G, L):
    SCALE = float(1.0 / np.sqrt(WB))
    HG = 4
    GB = HB // HG
    LAST = BATCH - 1
    QT = SEQ // P
    STEPS = [(1, kt, max(0, kt - 4) * P) for kt in range(8)] + [(0, kt, kt * P) for kt in range(4)]
    HALF1_STEPS = 8
    MAXIMA = [(h, qt, kh) for h in range(HG) for qt in range(QT) for kh in range(1 + (qt >= 4))]
    SPREAD_STEPS = 9
    TURN_STEP = SPREAD_STEPS
    PARTS = 4
    NM = len(MAXIMA)
    SLOT = NM + 1 + 2
    FIRST_USES = NM + 1
    BATCH_USES = GB * SLOT + 4
    with Memory(nc, stage) as m:
        qS, kS = (m.sbuf(n, [P, GB, HG, SEQ], BF16) for n in ("qS", "kS"))
        ident_bf = m.sbuf("ident_bf", [P, P], BF16)
        mask_q, mask_k = m.sbuf("mask_q", [P, P], BF16), m.sbuf("mask_k", [P, P], BF16)
        vb = m.sbuf("vb", [P, QT, HB, VW])
        pT = m.sbuf("pT", [P, 2, HG, HALF])
        peak = m.sbuf("peak", [P, HG, QT])
        peak2 = m.sbuf("peak2", [P, HG, QT // 2, 2])
        negp = m.sbuf("negp", [HG * QT, 2, 3, P], BF16)
        negr = m.sbuf("negr", [HG * QT, P])
        ctxu = m.sbuf("ctxu", [P, 2, HALF])
        inv = m.sbuf("inv", [P, 4, HG])
        ctx = m.sbuf("ctx", [P, QT, HB, WB])
        ctxT = m.sbuf("ctxT", [P, SEQ])
        psE = m.psum("psE", [P, 2, 2, HALF])
        psM = m.psum("psM", [P, 2, HALF])
        psV = m.psum("psV", [P, 2, HALF])
        made, v_ready, slot_done = m.sem("made"), m.sem("v_ready"), m.sem("slot_done")
        stack_landed = [m.sem(f"stack_landed{g}") for g in range(GB)]
        peaks_landed = [m.sem(f"peaks_landed{g}") for g in range(GB)]
        m_done, m_taken, peak_ready, split_ready, e_done, e_taken, pv_done, ctx_taken, ctx_ready, ctxT_ready = (m.sem(n) for n in (
            "m_done", "m_taken", "peak_ready", "split_ready", "e_done", "e_taken", "pv_done", "ctx_taken", "ctx_ready", "ctxT_ready"))
        block = m.block()
        AHEAD = 2

        def batches(eng, batch):
            with eng.Fori(0, LAST) as b:
                batch(b, False)
            batch(LAST, True)

        def maxima_at(e, part):
            share = [HALF - q0 for _, _, q0 in STEPS[:SPREAD_STEPS] for _ in range(PARTS)]
            at = e * PARTS + part
            return range(NM * sum(share[:at]) // sum(share), NM * sum(share[:at + 1]) // sum(share))

        def uses(b, g):
            return FIRST_USES + b * BATCH_USES + g * SLOT - (g > 0)

        @block.sync
        def _(sp):
            def load(b, g):
                cols = bass.ds(b * SEQ, SEQ)
                for dst, src in ((qS, G.q_stack), (kS, G.k_stack)):
                    sp.dma_start(dst[0:STACK, g, :, :], src.rearrange("(r h) n -> r h n", h=HB)[:, g * HG:(g + 1) * HG, cols]
                                 ).then_inc(stack_landed[g], 16)

            def peaks(n, g):
                sp.wait_ge(split_ready, n + 1)
                for i in range(3):
                    sp.dma_start(qS[STACK + i:STACK + i + 1, g, :, :].rearrange("a h (t q) -> a (h t) q", q=P),
                                 negp[:, g % 2, i, :]).then_inc(peaks_landed[g], 16)

            sp.wait_ge(made, 1)
            for g in range(GB):
                load(0, g)
            peaks(0, 0)

            def batch(b, last):
                for g in range(GB):
                    if not (last and g == GB - 1):
                        peaks(b * GB + g + 1, (g + 1) % GB)
                    if not last:
                        sp.wait_ge(slot_done, b * GB + g + 1)
                        load(b + 1, g)

            batches(sp, batch)

        @block.gpsimd
        def _(pool):
            def values(b, g):
                heads = slice(g * HG, (g + 1) * HG)
                nc.gpsimd.tensor_copy(vb[:, :, heads, :], L.v[:, bass.ds(b * QT, QT), heads, :]).then_inc(v_ready, 1)

            nc.gpsimd.memset(kS[64:96, :, :, :], 1.0).then_inc(made, 1)
            pool.wait_ge(made, 1)
            nc.gpsimd.memset(mask_q[:], 0.0)
            nc.gpsimd.memset(mask_k[:], 0.0)
            nc.gpsimd.tensor_copy(ident_bf[:], G.ident[:]).then_inc(made, 1)
            pool.wait_ge(made, 2)
            nc.gpsimd.affine_select(out=mask_q[:], in_=mask_q[:], compare_op=ALU.is_ge, fill=MASKED, base=0,
                                    pattern=[[-1, P]], channel_multiplier=1)
            nc.gpsimd.affine_select(out=mask_k[:], in_=mask_k[:], compare_op=ALU.is_ge, fill=MASKED, base=0,
                                    pattern=[[1, P]], channel_multiplier=-1).then_inc(made, 1)
            for g in range(GB):
                values(0, g)
            with pool.Fori(0, LAST) as b:
                for g in range(GB):
                    pool.wait_ge(slot_done, b * GB + g + 1)
                    values(b + 1, g)

        @block.tensor
        def _(pe):
            pe.wait_ge(made, 3)
            pe.wait_ge(L.wo_landed, 16)

            def use(c):
                pe.wait_ge(m_taken, c + 1)

            def maximum(c, parity, g, k):
                h, qt, kh = MAXIMA[k]
                n = min(HALF, (qt + 1) * P - kh * HALF)
                diagonal = (qt + 1) * P - kh * HALF <= HALF
                use(c)
                edge = n - P if diagonal else n
                if edge:
                    last = nc.tensor.matmul(psM[:, parity, 0:edge], qS[0:STACK, g, h, qt * P:(qt + 1) * P],
                                            kS[0:STACK, g, h, kh * HALF:kh * HALF + edge], start=True, stop=True)
                if diagonal:
                    nc.tensor.matmul(psM[:, parity, edge:n], qS[0:STACK, g, h, qt * P:(qt + 1) * P],
                                     kS[0:STACK, g, h, kh * HALF + edge:kh * HALF + n], start=True, stop=False)
                    last = nc.tensor.matmul(psM[:, parity, edge:n], ident_bf[:], mask_q[:], start=False, stop=True)
                last.then_inc(m_done, 1)

            def turn_maxima(c, parity, n):
                pe.wait_ge(peak_ready, n + 1)
                use(c)
                nc.tensor.transpose(psM[0:HG * QT, parity, 0:P], peak[:].rearrange("p h t -> p (h t)"), G.ident[:]).then_inc(m_done, 1)

            def scores(b, g, e, pair):
                half, kt, q0 = STEPS[e]
                pe.wait_ge(e_taken, (b * GB + g) * 24 + 2 * e + pair + 1)
                for i in range(2):
                    h = 2 * pair + i
                    keys = kS[0:STACK + 3, g, h, kt * P:(kt + 1) * P]
                    edge = q0
                    if kt >= 4 * half:
                        edge = q0 + P
                        nc.tensor.matmul(psE[:, pair, i, q0:edge], keys, qS[0:STACK + 3, g, h, half * HALF + q0:half * HALF + edge],
                                         start=True, stop=False)
                        last = nc.tensor.matmul(psE[:, pair, i, q0:edge], ident_bf[:], mask_k[:], start=False, stop=True)
                    if edge < HALF:
                        last = nc.tensor.matmul(psE[:, pair, i, edge:HALF], keys, qS[0:STACK + 3, g, h, half * HALF + edge:(half + 1) * HALF],
                                                start=True, stop=True)
                last.then_inc(e_done, 1)

            def weigh(b, g, e, pair):
                half, kt, q0 = STEPS[e]
                if pair == 0:
                    pe.wait_ge(e_taken, (b * GB + g) * 24 + 2 * e + 2 + AHEAD)
                    if kt == 0:
                        pe.wait_ge(ctx_taken, (b * GB + g) * 2 + 1 - half + AHEAD - 1)
                for h in (2 * pair, 2 * pair + 1):
                    last = nc.tensor.matmul(psV[32 * h:32 * h + 32, half, q0:HALF], vb[:, kt, g * HG + h, :], pT[:, e % 2, h, q0:HALF],
                                            start=(kt == 0), stop=True, skip_group_check=True)
                if pair == 1:
                    last.then_inc(pv_done, 1)

            def turn_context(b, g, half, c, parity):
                pe.wait_ge(ctx_taken, (b * GB + g) * 2 + 1 - half + 1 + AHEAD)
                use(c)
                for t in range(4):
                    last = nc.tensor.transpose(psM[:, parity, t * P:(t + 1) * P], ctxu[:, half, t * P:(t + 1) * P], G.ident[:])
                last.then_inc(m_done, 1)

            pe.wait_ge(stack_landed[0], 32)
            for k in range(NM):
                maximum(k, k % 2, 0, k)
            turn_maxima(NM, NM % 2, 0)

            def batch(b, last):
                for g in range(GB):
                    n = b * GB + g
                    more = not (last and g == GB - 1)
                    ahead = (g + 1) % GB
                    c, parity = uses(b, g), uses(0, g) % 2
                    pe.wait_ge(peaks_landed[g], 48 * b + 48)
                    pe.wait_ge(v_ready, n + 1)
                    if more:
                        pe.wait_ge(stack_landed[ahead], 32 * (b + (g + 1) // GB) + 32)
                    for e in range(len(STEPS)):
                        if e == TURN_STEP:
                            if more:
                                turn_maxima(c, parity, n + 1)
                                c, parity = c + 1, 1 - parity
                            turn_context(b, g, 1, c, parity)
                            c, parity = c + 1, 1 - parity
                        for part in range(PARTS):
                            if part < 2:
                                scores(b, g, e, part)
                            elif e >= 1:
                                weigh(b, g, e - 1, part - 2)
                            if part == 0 and e == 2 and g > 0:
                                turn_context(b, g - 1, 0, c, parity)
                                c, parity = c + 1, 1 - parity
                                pe.wait_ge(m_done, c)
                                pe.sem_inc(slot_done, 1)
                            if more and e < SPREAD_STEPS:
                                for k in maxima_at(e, part):
                                    maximum(c, parity, ahead, k)
                                    c, parity = c + 1, 1 - parity
                    for pair in range(2):
                        weigh(b, g, len(STEPS) - 1, pair)
                turn_context(b, GB - 1, 0, c, parity)
                c, parity = c + 1, 1 - parity
                pe.wait_ge(m_done, c)
                pe.sem_inc(slot_done, 1)
                pe.wait_ge(ctx_ready, 2 * GB * b + 2 * GB)
                for u in range(2):
                    use(c)
                    for t in range(4):
                        last = nc.tensor.transpose(psM[:, parity, t * P:(t + 1) * P],
                                                   ctx[:, 4 * u + t, :, :].rearrange("p h d -> p (h d)"), G.ident[:])
                    last.then_inc(m_done, 1)
                    c, parity = c + 1, 1 - parity
                for u in range(2):
                    pe.wait_ge(ctxT_ready, 2 * b + u + 1)
                    use(c)
                    for t in range(4):
                        last = nc.tensor.matmul(psM[:, parity, t * DM:(t + 1) * DM], ctxT[:, (4 * u + t) * P:(4 * u + t + 1) * P],
                                                L.wo[:], start=True, stop=True)
                    last.then_inc(m_done, 1)
                    c, parity = c + 1, 1 - parity

            batches(pe, batch)

        @block.scalar
        def _(act):
            act.sem_inc(e_taken, AHEAD)
            act.sem_inc(ctx_taken, AHEAD)

            def batch(b, last):
                for g in range(GB):
                    n = b * GB + g
                    for e, (half, kt, q0) in enumerate(STEPS):
                        for pair in range(2):
                            act.wait_ge(e_done, n * 24 + 2 * e + pair + 1)
                            if e >= 2:
                                act.wait_ge(pv_done, n * 12 + e - 1)
                            heads = slice(2 * pair, 2 * pair + 2)
                            nc.scalar.activation(pT[:, e % 2, heads, q0:HALF], psE[:, pair, :, q0:HALF], ACT.Exp,
                                                 scale=SCALE).then_inc(e_taken, 1)
                        if e == HALF1_STEPS:
                            act.wait_ge(pv_done, n * 12 + HALF1_STEPS)
                            nc.scalar.activation(ctxu[:, 1, :], psV[:, 1, :], ACT.Copy).then_inc(ctx_taken, 1)
                    act.wait_ge(pv_done, n * 12 + 12)
                    nc.scalar.activation(ctxu[:, 0, :], psV[:, 0, :], ACT.Copy).then_inc(ctx_taken, 1)

            batches(act, batch)

        @block.vector
        def _(dve):
            dve.sem_inc(m_taken, AHEAD)

            def maximum(c, parity, k):
                h, qt, kh = MAXIMA[k]
                size = min(HALF, (qt + 1) * P - kh * HALF)
                to = peak[:, h, qt:qt + 1] if qt < 4 else peak2[:, h, qt - 4, kh:kh + 1]
                dve.wait_ge(m_done, c + 1)
                nc.vector.reduce_max(to, psM[:, parity, 0:size], AX.X).then_inc(m_taken, 1)

            def peaks():
                nc.vector.drain()
                nc.vector.reduce_max(peak[:, :, 4:8], peak2[:], AX.X).then_inc(peak_ready, 1)

            def split(c, parity, g):
                dve.wait_ge(m_done, c + 1)
                turned = psM[0:HG * QT, parity, 0:P]
                high, mid, low = (negp[:, g % 2, i, :] for i in range(3))
                nc.vector.tensor_scalar(high, turned, -1.0, None, ALU.mult)
                nc.vector.drain()
                nc.vector.scalar_tensor_tensor(negr[:], turned, -1.0, high, ALU.mult, ALU.subtract).then_inc(m_taken, 1)
                nc.vector.drain()
                nc.vector.tensor_copy(mid, negr[:])
                nc.vector.drain()
                nc.vector.tensor_tensor(low, negr[:], mid, ALU.subtract).then_inc(split_ready, 1)

            def context(c, parity, g, half):
                dve.wait_ge(m_done, c + 1)
                turned = psM[:, parity, :].rearrange("p (t h w) -> p t h w", t=4, h=HG)
                nc.vector.reciprocal(inv[:], turned[:, :, :, WB])
                nc.vector.drain()
                nc.vector.tensor_tensor(ctx[:, 4 * half:4 * half + 4, g * HG:(g + 1) * HG, :], turned[:, :, :, 0:WB],
                                        inv[:].unsqueeze(3).to_broadcast([P, 4, HG, WB]), ALU.mult).then_inc(m_taken, 1)
                nc.vector.drain()
                dve.sem_inc(ctx_ready, 1)

            for k in range(NM):
                maximum(k, k % 2, k)
            peaks()
            split(NM, NM % 2, 0)

            def batch(b, last):
                xb = G.x[:, bass.ds(b, 1), :, :].rearrange("p b t d -> p (b t) d")
                for g in range(GB):
                    more = not (last and g == GB - 1)
                    c, parity = uses(b, g), uses(0, g) % 2
                    for e in range(TURN_STEP):
                        for part in range(PARTS):
                            if part == 0 and e == 2 and g > 0:
                                context(c, parity, g - 1, 0)
                                c, parity = c + 1, 1 - parity
                            if more:
                                for k in maxima_at(e, part):
                                    maximum(c, parity, k)
                                    c, parity = c + 1, 1 - parity
                    if more:
                        peaks()
                        split(c, parity, (g + 1) % GB)
                        c, parity = c + 1, 1 - parity
                    context(c, parity, g, 1)
                    c, parity = c + 1, 1 - parity
                context(c, parity, GB - 1, 0)
                c, parity = c + 1, 1 - parity
                for u in range(2):
                    dve.wait_ge(m_done, c + 1)
                    nc.vector.tensor_copy(ctxT[:, u * HALF:(u + 1) * HALF], psM[:, parity, :]).then_inc(m_taken, 1)
                    nc.vector.drain()
                    dve.sem_inc(ctxT_ready, 1)
                    c, parity = c + 1, 1 - parity
                for u in range(2):
                    dve.wait_ge(m_done, c + 1)
                    nc.vector.tensor_tensor(xb[:, 4 * u:4 * u + 4, :], xb[:, 4 * u:4 * u + 4, :],
                                            psM[:, parity, :].rearrange("p (t d) -> p t d", d=DM), ALU.add).then_inc(m_taken, 1)
                    c, parity = c + 1, 1 - parity

            batches(dve, batch)


def build(nc, A, out):
    G, W = Shared(), A
    with Memory(nc, "g") as m:
        G.x = m.sbuf("x", [P, BATCH, TPB, DM])
        G.ident = m.sbuf("ident", [P, P])
        G.ones = m.sbuf("ones", [P, P])
        G.slots_in, G.slots_out = ([nc.dram_tensor(f"{n}{i}", [HALF_SLOTS, DM], F32, kind="Internal").ap() for i in range(HALVES)]
                                   for n in ("slots_in", "slots_out"))
        G.owner_dram = nc.dram_tensor("owner", [HALVES * HALF_TILES, 1], I32, kind="Internal").ap()
        G.q_stack, G.k_stack = (nc.dram_tensor(n, [STACK * HB, TOKENS], BF16, kind="Internal").ap() for n in ("q_stack", "k_stack"))
        with Memory(nc, "a0") as a:
            normed(G, a)
            G.zeros = a.sbuf("zeros", [P, HALF_SLOTS // ZERO_FILLS // P * DM])
            setup(nc, A["x"], G)
            layernorm(nc, "a0", G)
            attn_a(nc, G, W)
            ffn_a(nc, G, W)
        moe(nc, "m", G, W)
        attn_b(nc, "b", G, W)
        moe(nc, "n", G, W)
        finish(nc, G.x, out)


def normed(G, m):
    G.xn = m.sbuf("xn", [P, BATCH, TPB, DM])
    G.xnT = m.sbuf("xnT", [P, BATCH, SEQ])


def finish(nc, x, out):
    with Memory(nc, "end") as e:
        stored = e.sem("stored")
        block = e.block()

        @block.sync
        def _(sp):
            sp.dma_start(out.rearrange("b (t p) d -> p b t d", p=P), x[:]).then_inc(stored, 16)
            sp.wait_ge(stored, 16)


def kernel(**inputs):
    import concourse.bacc as bacc
    from concourse.bass_utils import run_bass_kernel_spmd

    a = {n: np.ascontiguousarray(v) for n, v in inputs.items()}
    wq, wk = a["L0_attn_a_Wq"], a["L0_attn_a_Wk"]
    arrays = {
        "x": a["L0_attn_a_x"],
        "wq": wq, "wk": wk, "wv": a["L0_attn_a_Wv"], "wo": a["L0_attn_a_Wo"],
        "wqT": wq.reshape(DM, HD).T, "wkT": wk.reshape(DM, HD).T, "projT": a["L0_attn_a_proj"].T,
        **{n: a["L0_attn_a_" + o] for n, o in (("w1", "W1"), ("b1", "b1"), ("w2", "W2"), ("b2", "b2"), ("ln1_g", "ln1_g"),
                                               ("ln1_b", "ln1_b"), ("ln2_g", "ln2_g"), ("ln2_b", "ln2_b"))},
        "routerT": a["L0_ffn_router_w"].T, "expert_bias": a["L0_ffn_expert_bias"],
        "w_gateT": a["L0_ffn_w_gate"].transpose(2, 0, 1), "w_downT": a["L0_ffn_w_down"].transpose(2, 0, 1),
        "bwqT": a["L0_attn_b_Wq"].reshape(HB, WB, DM).transpose(2, 1, 0).reshape(DM, DM),
        "bwkT": a["L0_attn_b_Wk"].reshape(HB, WB, DM).transpose(2, 1, 0).reshape(DM, DM),
        "bwvT": a["L0_attn_b_Wv"].T, "bwoT": a["L0_attn_b_Wo"].T, "bo": a["L0_attn_b_bo"],
        "w_gate_sharedT": a["L0_ffn_w_gate_shared"].T, "w_down_sharedT": a["L0_ffn_w_down_shared"].T,
    }
    arrays["b1"] = arrays["b1"].reshape(FFC, P).T
    arrays = {n: np.ascontiguousarray(v) for n, v in arrays.items()}
    nc = bacc.Bacc("TRN2", target_bir_lowering=False, num_devices=1)
    A = {n: nc.dram_tensor(f"in_{n}", v.shape, mybir.dt.from_np(v.dtype), kind="ExternalInput").ap() for n, v in arrays.items()}
    out = nc.dram_tensor("out_x", (BATCH, SEQ, DM), F32, kind="ExternalOutput").ap()
    build(nc, A, out)
    r = run_bass_kernel_spmd(nc, [{f"in_{n}": v for n, v in arrays.items()}], core_ids=[0])
    return r.results[0]["out_x"]
```

```python
from contextlib import ExitStack

import concourse.bass as bass
import numpy as np
from concourse import mybir

F32 = mybir.dt.float32
BF16 = mybir.dt.bfloat16
I32 = mybir.dt.int32
ALU = mybir.AluOpType
ACT = mybir.ActivationFunctionType
AX = mybir.AxisListType

P = 128
BATCH, SEQ, DM = 4, 1024, 128
TOKENS = BATCH * SEQ
TILES = TOKENS // P
TPB = SEQ // P
HALF = 512

HA, DH, MF = 16, 64, 64
PAIRS = HA // 2
HD = HA * DH
DFF = 512
FFC = DFF // P
EPS_KERNEL = 1e-6
EPS_LN_A = 1e-6
EPS_LN = 1e-5
DN = float(np.float32(1.0) / np.sqrt(np.sqrt(np.float32(DH))))
RATIO = float(np.float32(1.0) / np.sqrt(np.float32(MF)))

HB, WB = 16, 8
VW = 32
STACK = 9 * WB
STORES = 3
LOADS = 6
MASKED = -1e30

EXPERTS, TOPK, INTER = 160, 8, 64
ROUTED_SCALE = 2.5
HALVES = 2
GROUP = 4
HALF_TILES = TOKENS // HALVES * TOPK // P + EXPERTS
HALF_GROUPS = HALF_TILES // GROUP
GROUPS = HALVES * HALF_GROUPS
GROUP_SLOTS = GROUP * P
HALF_SLOTS = HALF_GROUPS * GROUP_SLOTS
OWNER_COLUMNS = -(-HALF_TILES // P)
TPH = TILES // HALVES
ZERO_FILLS = 18
assert HALF_TILES % GROUP == 0 and HALF_SLOTS % (ZERO_FILLS * P) == 0


class Shared:
    pass


class Memory:

    def __init__(self, nc, stage):
        self.nc, self.stage, self.ctx, self.sems = nc, stage, ExitStack(), []

    def __enter__(self):
        return self

    def __exit__(self, *a):
        self.ctx.__exit__(*a)
        self.nc.clear_and_free_semaphores(self.sems)
        self.nc.all_engine_barrier()

    def sbuf(self, name, shape, dtype=F32):
        return self.ctx.enter_context(self.nc.sbuf_tensor(f"{self.stage}_{name}", shape, dtype))

    def psum(self, name, shape, dtype=F32):
        return self.ctx.enter_context(self.nc.psum_tensor(f"{self.stage}_{name}", shape, dtype))

    def sem(self, name):
        self.sems.append(self.nc.alloc_semaphore(name=f"{self.stage}_{name}"))
        return self.sems[-1]

    def block(self):
        return self.ctx.enter_context(self.nc.Block())


def bc(ap, n):
    return ap.unsqueeze(2).to_broadcast([ap.shape[0], ap.shape[1], n])


def rsqrt(nc, out, var, eps, guess, half):
    dve = nc.vector
    dve.tensor_scalar(half, var, eps, None, ALU.add)
    dve.drain()
    dve.tensor_scalar(out.bitcast(I32), half.bitcast(I32), -0.5, float(0x5F3759DF), ALU.mult, ALU.add)
    dve.tensor_scalar(half, half, -0.5, None, ALU.mult)
    for _ in range(4):
        dve.drain()
        dve.tensor_tensor(guess, out, out, ALU.mult)
        dve.drain()
        dve.tensor_tensor(guess, guess, half, ALU.mult)
        dve.drain()
        dve.scalar_tensor_tensor(out, guess, 1.5, out, ALU.add, ALU.mult)
    dve.drain()


def setup(nc, x, G):
    with Memory(nc, "setup") as m:
        zeros_made = m.sem("zeros_made")
        zeroed, made = m.sem("zeroed"), m.sem("made")
        x_landed = m.sem("x_landed")
        block = m.block()

        @block.sync
        def _(sp):
            sp.dma_start(G.x[:], x.rearrange("b (t p) d -> p b t d", p=P)).then_inc(x_landed, 16)
            sp.wait_ge(x_landed, 16)

        @block.vector
        def _(dve):
            nc.vector.memset(G.zeros[:], 0.0).then_inc(zeros_made, 1)
            dve.wait_ge(zeros_made, 1)

        @block.gpsimd
        def _(pool):
            pool.memset(G.ident[:], 0.0).then_inc(zeroed, 1)
            pool.memset(G.ones[:], 1.0)
            pool.wait_ge(zeroed, 1)
            pool.affine_select(out=G.ident[:], in_=G.ident[:], compare_op=ALU.not_equal, fill=1.0, base=0,
                               pattern=[[-1, P]], channel_multiplier=1).then_inc(made, 1)
            pool.wait_ge(made, 1)


def layernorm(nc, stage, G):
    with Memory(nc, stage) as m:
        stats = m.sbuf("stats", [P, TPB, 6])
        mv = m.sbuf("mv", [P, TPB, 2])
        moments = m.sbuf("moments", [P, TILES, 2])
        var, half, rstd = (m.sbuf(n, [P, TILES]) for n in ("var", "half", "rstd"))
        ps = m.psum("ps", [P, 4, HALF])
        xn_ready, turned, bank_free = m.sem("xn_ready"), m.sem("turned"), m.sem("bank_free")
        block = m.block()
        x, xn = (t[:].rearrange("p b t d -> p (b t) d") for t in (G.x, G.xn))

        @block.vector
        def _(dve):
            with dve.Fori(0, BATCH) as b:
                for t in range(TPB):
                    nc.vector.bn_stats(stats[:, t, :], x[:, bass.ds(b * TPB + t, 1), :].rearrange("p a d -> p (a d)"))
                nc.vector.drain()
                for t in range(TPB):
                    nc.vector.bn_aggr(mv[:, t, :], stats[:, t, :])
                nc.vector.drain()
                nc.vector.tensor_copy(moments[:, bass.ds(b * TPB, TPB), :], mv[:])
            nc.vector.drain()
            rsqrt(nc, rstd[:], moments[:, :, 1], EPS_LN, var[:], half[:])
            for t in range(TILES):
                last = nc.vector.tensor_scalar(xn[:, t, :], x[:, t, :], moments[:, t, 0:1], rstd[:, t:t + 1], ALU.subtract, ALU.mult)
                if t % 4 == 3:
                    last.then_inc(xn_ready, 1)

        @block.tensor
        def _(pe):
            for u in range(TILES // 4):
                pe.wait_ge(xn_ready, u + 1)
                if u >= 4:
                    pe.wait_ge(bank_free, u - 3)
                for t in range(4):
                    last = nc.tensor.transpose(ps[:, u % 4, t * P:(t + 1) * P], xn[:, 4 * u + t, :], G.ident[:])
                last.then_inc(turned, 1)

        @block.scalar
        def _(act):
            xnT = G.xnT[:].rearrange("p b n -> p (b n)")
            for u in range(TILES // 4):
                act.wait_ge(turned, u + 1)
                nc.scalar.activation(xnT[:, u * HALF:(u + 1) * HALF], ps[:, u % 4, :], ACT.Copy).then_inc(bank_free, 1)


def attn_a(nc, G, W):
    with Memory(nc, "a") as m:
        wq, wk, wv = (m.sbuf(n, [P, HD]) for n in ("wq", "wk", "wv"))
        wqp, wkp = (m.sbuf(n, [P, PAIRS, P]) for n in ("wqp", "wkp"))
        proj2 = m.sbuf("proj2", [P, P])
        wo = m.sbuf("wo", [DH, HA, DM])
        ngmax = m.sbuf("ngmax", [P, 1])
        zero_fills = m.sem("zero_fills")

        with Memory(nc, "a1") as m1:
            wqT, wkT = (m1.sbuf(n, [P, PAIRS, DM]) for n in ("wqT", "wkT"))
            pmax = m1.sbuf("pmax", [P, TOKENS // HALF, PAIRS])
            rowmax = m1.sbuf("rowmax", [P, 1])
            allmax = m1.sbuf("allmax", [1, 1])
            ps = m1.psum("ps", [P, 4, HALF])
            psw = m1.psum("psw", [P, 4, HALF])
            zeroed, landed = m1.sem("zeroed"), m1.sem("landed")
            proj_landed, fold_done, folded = m1.sem("proj_landed"), m1.sem("fold_done"), m1.sem("folded")
            feats, taken = m1.sem("feats"), m1.sem("taken")
            row_ready, turned, one_ready, spread = m1.sem("row_ready"), m1.sem("turned"), m1.sem("one"), m1.sem("spread")
            neg_ready = m1.sem("neg_ready")
            block = m1.block()

            @block.sync
            def _(sp):
                sp.dma_start(wkT[:], W["wkT"].rearrange("(c p) d -> p c d", p=P)).then_inc(landed, 16)
                sp.dma_start(wqT[:], W["wqT"].rearrange("(c p) d -> p c d", p=P)).then_inc(landed, 16)
                sp.wait_ge(zeroed, 1)
                for h in range(2):
                    sp.dma_start(proj2[h * DH:(h + 1) * DH, h * MF:(h + 1) * MF], W["projT"]).then_inc(proj_landed, 16)
                for dst, src in ((wq, W["wq"]), (wk, W["wk"]), (wv, W["wv"])):
                    sp.dma_start(dst[:], src.rearrange("d h k -> d (h k)")).then_inc(landed, 16)
                sp.dma_start(wo[:], W["wo"].rearrange("h k o -> k h o")).then_inc(landed, 16)
                for slots in G.slots_in:
                    fill = slots.rearrange("(n p j) d -> n p (j d)", n=ZERO_FILLS, p=P)
                    for n in range(ZERO_FILLS):
                        sp.dma_start(fill[n], G.zeros[:]).then_inc(zero_fills, 16)
                sp.wait_ge(landed, 96)

            @block.gpsimd
            def _(pool):
                pool.memset(proj2[:], 0.0).then_inc(zeroed, 1)

            @block.tensor
            def _(pe):
                pe.wait_ge(landed, 32)
                pe.wait_ge(proj_landed, 32)
                for n, w in enumerate((wkT, wqT)):
                    for c in range(PAIRS):
                        last = nc.tensor.matmul(psw[:, 2 * n + c // 4, (c % 4) * P:(c % 4 + 1) * P], w[:, c, :], proj2[:],
                                                start=True, stop=True)
                    last.then_inc(fold_done, 1)
                pe.wait_ge(folded, 1)
                with pe.Fori(0, TOKENS // HALF) as g:
                    xg = G.xnT[:].rearrange("p b n -> p (b n)")[:, bass.ds(g * HALF, HALF)]
                    for c in range(PAIRS):
                        pe.wait_ge(taken, PAIRS * g + c + 1)
                        nc.tensor.matmul(ps[:, c % 4, :], wkp[:, c, :], xg, start=True, stop=True).then_inc(feats, 1)
                pe.wait_ge(row_ready, 1)
                nc.tensor.transpose(ps[0:1, 0, 0:P], rowmax[:], G.ident[:]).then_inc(turned, 1)
                pe.wait_ge(one_ready, 1)
                nc.tensor.matmul(ps[:, 1, 0:1], G.ones[0:1, :], allmax[:], start=True, stop=True).then_inc(spread, 1)

            @block.scalar
            def _(act):
                for n, w in enumerate((wkp, wqp)):
                    act.wait_ge(fold_done, n + 1)
                    nc.scalar.activation(w[:].rearrange("p c m -> p (c m)"),
                                         psw[:, 2 * n:2 * n + 2, :].rearrange("p a n -> p (a n)"), ACT.Copy,
                                         scale=DN).then_inc(folded, 1)
                act.wait_ge(folded, 2)

            @block.vector
            def _(dve):
                dve.sem_inc(taken, 4)
                with dve.Fori(0, TOKENS // HALF) as g:
                    for c in range(PAIRS):
                        dve.wait_ge(feats, PAIRS * g + c + 1)
                        nc.vector.reduce_max(pmax[:, bass.ds(g, 1), c:c + 1].rearrange("p a b -> p (a b)"),
                                             ps[:, c % 4, :], AX.X).then_inc(taken, 1)
                nc.vector.drain()
                nc.vector.reduce_max(rowmax[:], pmax[:].rearrange("p a b -> p (a b)"), AX.X).then_inc(row_ready, 1)
                dve.wait_ge(turned, 1)
                nc.vector.reduce_max(allmax[:], ps[0:1, 0, 0:P], AX.X).then_inc(one_ready, 1)
                dve.wait_ge(spread, 1)
                nc.vector.tensor_scalar(ngmax[:], ps[:, 1, 0:1], -1.0, None, ALU.mult).then_inc(neg_ready, 1)
                dve.wait_ge(neg_ready, 1)

        with Memory(nc, "a2") as m2:
            xT = m2.sbuf("xT", [P, SEQ])
            sq = m2.sbuf("sq", [P, 2, HD])
            diag = m2.sbuf("diag", [P, HA])
            fold2 = m2.sbuf("fold2", [P, 2, HA, DH // 2])
            fold4 = m2.sbuf("fold4", [P, 2, HA, DH // 4])
            squares_seen, halved, q_folded = m2.sem("squares_seen"), m2.sem("halved"), m2.sem("q_folded")
            qmax = m2.sbuf("qmax", [P, HA])
            shift = m2.sbuf("shift", [P, HA])
            arg = m2.sbuf("arg", [P, 2, HD])
            qe = m2.sbuf("qe", [P, TPB, HD])
            kf = m2.sbuf("kf", [P, 2, HD])
            kfe = m2.sbuf("kfe", [P, HD])
            v = m2.sbuf("v", [P, 2, HA, DH + 1])
            vk = m2.sbuf("vk", [DH + 1, HD])
            vkwo = m2.sbuf("vkwo", [P, PAIRS, DM])
            ksum = m2.sbuf("ksum", [P, HD])
            prod = m2.sbuf("prod", [P, 2, HD])
            feature_sum = m2.sbuf("feature_sum", [P, HA])
            prod_ready, prod_taken, ksum_seen = m2.sem("prod_ready"), m2.sem("prod_taken"), m2.sem("ksum_seen")
            den, inv = m2.sbuf("den", [P, HA]), m2.sbuf("inv", [P, HA])
            qs = m2.sbuf("qs", [P, 2, HD])
            qsT = m2.sbuf("qsT", [P, 2, HD])
            psA = m2.psum("psA", [P, 2, HALF])
            psB = m2.psum("psB", [P, 4, HALF])
            psC = m2.psum("psC", [P, 2, HALF])
            xT_ready = m2.sem("xT_ready")
            cleared = m2.sem("cleared")
            q_done, qd_done, q_squared, q_diag, q_arg, q_exp = (m2.sem(n) for n in (
                "q_done", "qd_done", "q_squared", "q_diag", "q_arg", "q_exp"))
            k_done, kd_done, v_done, k_squared, k_diag, k_arg, k_exp, kf_ready, v_ready, kv_tile, kv_out = (
                m2.sem(n) for n in ("k_done", "kd_done", "v_done", "k_squared", "k_diag", "k_arg", "k_exp", "kf_ready",
                                    "v_ready", "kv_tile", "kv_out"))
            sums_spread, ksum_ready, vkwo_done, vkwo_ready, qs_ready, qT_done, qsT_ready, ao_done, ao_taken = (m2.sem(n) for n in (
                "sums_spread", "ksum_ready", "vkwo_done", "vkwo_ready", "qs_ready", "qT_done", "qsT_ready", "ao_done", "ao_taken"))
            block = m2.block()
            heads = "p (h k) -> p h k"

            @block.sync
            def _(sp):
                sp.wait_ge(zero_fills, 16 * HALVES * ZERO_FILLS)

            @block.gpsimd
            def _(pool):
                def bring(b):
                    nc.gpsimd.tensor_copy(xT[:], G.xnT[:, bass.ds(b, 1), :].rearrange("p b n -> p (b n)")).then_inc(xT_ready, 1)

                nc.gpsimd.memset(v[:, :, :, DH:], 1.0).then_inc(cleared, 1)
                bring(0)

                def weigh(b):
                    for t in range(TPB):
                        pool.wait_ge(ksum_ready, b + 1)
                        if t >= 2:
                            pool.wait_ge(prod_taken, TPB * b + t - 1)
                        pool.sem_inc(ksum_seen, 1)
                        nc.gpsimd.tensor_tensor(prod[:, t % 2, :], qe[:, t, :], ksum[:], ALU.mult).then_inc(prod_ready, 1)

                def fold_squares(b):
                    for t in range(TPB):
                        pool.wait_ge(q_squared, TPB * b + t + 1)
                        if t >= 2:
                            pool.wait_ge(q_folded, TPB * b + t - 1)
                        pool.sem_inc(squares_seen, 1)
                        squares = sq[:, t % 2, :].rearrange(heads, k=DH)
                        nc.gpsimd.tensor_tensor(fold2[:, t % 2, :, :], squares[:, :, 0:DH // 2], squares[:, :, DH // 2:], ALU.add).then_inc(halved, 1)
                        pool.wait_ge(halved, TPB * b + t + 1)
                        if t >= 2:
                            pool.wait_ge(q_diag, TPB * b + t - 1)
                        pool.sem_inc(squares_seen, 1)
                        nc.gpsimd.tensor_tensor(fold4[:, t % 2, :, :], fold2[:, t % 2, :, 0:DH // 4], fold2[:, t % 2, :, DH // 4:], ALU.add).then_inc(q_folded, 1)
                    pool.wait_ge(q_folded, TPB * b + TPB)
                    pool.sem_inc(squares_seen, 1)

                with pool.Fori(0, BATCH - 1) as b:
                    fold_squares(b)
                    pool.wait_ge(kd_done, TPB * b + TPB)
                    bring(b + 1)
                    weigh(b)
                fold_squares(BATCH - 1)
                weigh(BATCH - 1)

            @block.tensor
            def _(pe):
                pe.wait_ge(cleared, 1)
                with pe.Fori(0, BATCH) as b:
                    pe.wait_ge(xT_ready, b + 1)
                    for t in range(TPB):
                        xt = xT[:, t * P:(t + 1) * P]
                        if t >= 1:
                            pe.wait_ge(q_squared, TPB * b + t)
                        for u in range(2):
                            last = nc.tensor.matmul(psA[:, u, :], xt, wq[:, u * HALF:(u + 1) * HALF], start=True, stop=True)
                        last.then_inc(q_done, 1)
                        if t >= 2:
                            pe.wait_ge(q_arg, TPB * b + t - 1)
                        for u in range(2):
                            last = nc.tensor.matmul(psB[:, 2 * (t % 2) + u, :], xt,
                                                    wqp[:, 4 * u:4 * u + 4, :].rearrange("p c m -> p (c m)"), start=True, stop=True)
                        last.then_inc(qd_done, 1)
                    def add_kv(t):
                        pe.wait_ge(kf_ready, TPB * b + t + 1)
                        pe.wait_ge(v_ready, 2 * TPB * b + 2 * t + 2)
                        if t == 0:
                            pe.wait_ge(ao_taken, TPB * b + 1)
                        for h in range(HA):
                            last = nc.tensor.matmul(psC[0:DH + 1, h // 8, (h % 8) * MF:(h % 8 + 1) * MF], v[:, t % 2, h, :],
                                                    kf[:, t % 2, h * MF:(h + 1) * MF], start=(t == 0 and h % 8 == 0),
                                                    stop=(t == TPB - 1), skip_group_check=True)
                        last.then_inc(kv_tile, 1)

                    def values(t, u):
                        if t + u >= 1:
                            pe.wait_ge(v_ready, 2 * TPB * b + 2 * t + u)
                        else:
                            pe.wait_ge(q_arg, TPB * b + TPB)
                        nc.tensor.matmul(psB[:, 2, :], xT[:, t * P:(t + 1) * P], wv[:, u * HALF:(u + 1) * HALF],
                                         start=True, stop=True).then_inc(v_done, 1)

                    for t in range(TPB):
                        xt = xT[:, t * P:(t + 1) * P]
                        if t >= 1:
                            values(t, 0)
                            pe.wait_ge(k_squared, TPB * b + t)
                        else:
                            pe.wait_ge(q_squared, TPB * b + TPB)
                        for w in range(2):
                            last = nc.tensor.matmul(psA[:, w, :], xt, wk[:, w * HALF:(w + 1) * HALF], start=True, stop=True)
                        last.then_inc(k_done, 1)
                        if t >= 1:
                            values(t, 1)
                            pe.wait_ge(k_arg, TPB * b + t)
                        else:
                            pe.wait_ge(q_arg, TPB * b + TPB - 1)
                        for u in range(2):
                            last = nc.tensor.matmul(psB[:, u, :], xt, wkp[:, 4 * u:4 * u + 4, :].rearrange("p c m -> p (c m)"),
                                                    start=True, stop=True)
                        last.then_inc(kd_done, 1)
                        if t == 0:
                            values(t, 0)
                            values(t, 1)
                        else:
                            add_kv(t - 1)
                    add_kv(TPB - 1)

                    pe.wait_ge(kv_out, b + 1)
                    for u in range(2):
                        last = nc.tensor.matmul(psB[:, u, :], G.ones[DH:DH + 1, :], vk[DH:DH + 1, u * HALF:(u + 1) * HALF], start=True, stop=True)
                    last.then_inc(sums_spread, 1)
                    pe.wait_ge(cleared, 1)
                    pe.wait_ge(k_squared, TPB * b + TPB)
                    for h in range(HA):
                        c, rows = h // 2, slice(h % 2 * MF, (h % 2 + 1) * MF)
                        last = nc.tensor.matmul(psA[rows, c // 4, (c % 4) * DM:(c % 4 + 1) * DM], vk[0:DH, h * MF:(h + 1) * MF], wo[:, h, :],
                                                start=True, stop=True)
                    last.then_inc(vkwo_done, 1)

                    def project(t):
                        pe.wait_ge(qsT_ready, 2 * TPB * b + 2 * t + 2)
                        if t >= 2:
                            pe.wait_ge(ao_taken, TPB * b + t)
                        for c in range(PAIRS):
                            last = nc.tensor.matmul(psC[:, t % 2, 0:DM], qsT[:, t % 2, c * P:(c + 1) * P], vkwo[:, c, :],
                                                    start=(c == 0), stop=(c == PAIRS - 1))
                        last.then_inc(ao_done, 1)

                    pe.wait_ge(vkwo_ready, b + 1)
                    for t in range(TPB):
                        pe.wait_ge(qs_ready, TPB * b + t + 1)
                        for u in range(2):
                            if t >= 1:
                                pe.wait_ge(qsT_ready, 2 * TPB * b + 2 * t + u - 1)
                            for c in range(4):
                                last = nc.tensor.transpose(psA[:, u, c * P:(c + 1) * P], qs[:, t % 2, (4 * u + c) * P:(4 * u + c + 1) * P],
                                                           G.ident[:])
                            last.then_inc(qT_done, 1)
                        if t >= 1:
                            project(t - 1)
                    project(TPB - 1)

            @block.scalar
            def _(act):
                with act.Fori(0, BATCH) as b:
                    both = "p a n -> p (a n)"

                    def q_features(t):
                        act.wait_ge(q_arg, TPB * b + t + 1)
                        nc.scalar.activation(qe[:, t, :], arg[:, t % 2, :], ACT.Exp).then_inc(q_exp, 1)

                    for t in range(TPB):
                        act.wait_ge(q_done, TPB * b + t + 1)
                        if t >= 2:
                            act.wait_ge(halved, TPB * b + t - 1)
                        nc.scalar.activation(sq[:, t % 2, :], psA[:].rearrange(both), ACT.Square).then_inc(q_squared, 1)
                        if t >= 1:
                            q_features(t - 1)
                    q_features(TPB - 1)

                    def k_features(t):
                        act.wait_ge(k_arg, TPB * b + t + 1)
                        if t >= 1:
                            act.wait_ge(kf_ready, TPB * b + t)
                        nc.scalar.activation(kfe[:], arg[:, t % 2, :], ACT.Exp, bias=ngmax[:]).then_inc(k_exp, 1)

                    def take_values(t, u):
                        act.wait_ge(v_done, 2 * TPB * b + 2 * t + u + 1)
                        if u == 0 and t >= 2:
                            act.wait_ge(kv_tile, TPB * b + t - 1)
                        nc.scalar.activation(v[:, t % 2, 8 * u:8 * u + 8, 0:DH], psB[:, 2, :].rearrange(heads, k=DH), ACT.Copy).then_inc(v_ready, 1)

                    for t in range(TPB):
                        if t >= 1:
                            k_features(t - 1)
                            take_values(t, 0)
                        act.wait_ge(k_done, TPB * b + t + 1)
                        if t >= 2:
                            act.wait_ge(k_diag, TPB * b + t - 1)
                        else:
                            act.wait_ge(halved, TPB * b + TPB - 1 + t)
                        nc.scalar.activation(sq[:, t % 2, :], psA[:].rearrange(both), ACT.Square).then_inc(k_squared, 1)
                        if t == 0:
                            take_values(t, 0)
                        take_values(t, 1)
                    k_features(TPB - 1)
                    act.wait_ge(sums_spread, b + 1)
                    nc.scalar.activation(ksum[:], psB[:, 0:2, :].rearrange(both), ACT.Copy).then_inc(ksum_ready, 1)
                    act.wait_ge(vkwo_done, b + 1)
                    nc.scalar.activation(vkwo[:].rearrange("p c o -> p (c o)"), psA[:].rearrange(both), ACT.Copy).then_inc(vkwo_ready, 1)
                    for t in range(TPB):
                        for u in range(2):
                            act.wait_ge(qT_done, 2 * TPB * b + 2 * t + u + 1)
                            if t >= 2:
                                act.wait_ge(ao_done, TPB * b + t - 1)
                            nc.scalar.activation(qsT[:, t % 2, u * HALF:(u + 1) * HALF], psA[:, u, :], ACT.Copy).then_inc(qsT_ready, 1)

            @block.vector
            def _(dve):
                dve.sem_inc(ao_taken, 1)
                with dve.Fori(0, BATCH) as b:
                    xnb = G.xn[:, bass.ds(b, 1), :, :].rearrange("p b t d -> p (b t) d")
                    both = "p a (h k) -> p (a h) k"
                    for t in range(TPB):
                        dve.wait_ge(qd_done, TPB * b + t + 1)
                        dash = psB[:, 2 * (t % 2):2 * (t % 2) + 2, :].rearrange(both, k=MF)
                        nc.vector.reduce_max(qmax[:], dash, AX.X)
                        dve.wait_ge(q_folded, TPB * b + t + 1)
                        nc.vector.reduce_sum(diag[:], fold4[:, t % 2, :, :], AX.X).then_inc(q_diag, 1)
                        nc.vector.drain()
                        nc.vector.scalar_tensor_tensor(shift[:], diag[:], DN * DN / 2.0, qmax[:], ALU.mult, ALU.add)
                        nc.vector.drain()
                        if t >= 2:
                            dve.wait_ge(q_exp, TPB * b + t - 1)
                        nc.vector.tensor_tensor(arg[:, t % 2, :].rearrange(heads, k=MF), dash, bc(shift[:], MF),
                                                ALU.subtract).then_inc(q_arg, 1)

                    def k_features(t):
                        dve.wait_ge(k_exp, TPB * b + t + 1)
                        if t >= 2:
                            dve.wait_ge(kv_tile, TPB * b + t - 1)
                        nc.vector.tensor_scalar(kf[:, t % 2, :], kfe[:], EPS_KERNEL, RATIO, ALU.add, ALU.mult).then_inc(kf_ready, 1)

                    for t in range(TPB):
                        if t >= 1:
                            k_features(t - 1)
                        dve.wait_ge(k_squared, TPB * b + t + 1)
                        nc.vector.reduce_sum(diag[:], sq[:, t % 2, :].rearrange(heads, k=DH), AX.X).then_inc(k_diag, 1)
                        nc.vector.drain()
                        nc.vector.tensor_scalar(shift[:], diag[:], DN * DN / 2.0, None, ALU.mult)
                        nc.vector.drain()
                        dve.wait_ge(kd_done, TPB * b + t + 1)
                        if t >= 2:
                            dve.wait_ge(k_exp, TPB * b + t - 1)
                        else:
                            dve.wait_ge(q_exp, TPB * b + TPB - 1 + t)
                        nc.vector.tensor_tensor(arg[:, t % 2, :].rearrange(heads, k=MF), psB[:, 0:2, :].rearrange(both, k=MF),
                                                bc(shift[:], MF), ALU.subtract).then_inc(k_arg, 1)
                    k_features(TPB - 1)
                    dve.wait_ge(kv_tile, TPB * b + TPB)
                    nc.vector.tensor_copy(vk[:], psC[0:DH + 1, :, :].rearrange("p a n -> p (a n)")).then_inc(kv_out, 1)

                    def add_out(t):
                        dve.wait_ge(ao_done, TPB * b + t + 1)
                        nc.vector.tensor_tensor(xnb[:, t, :], xnb[:, t, :], psC[:, t % 2, 0:DM], ALU.add).then_inc(ao_taken, 1)

                    dve.wait_ge(ksum_ready, b + 1)
                    nc.vector.reduce_sum(feature_sum[:], ksum[:].rearrange(heads, k=MF), AX.X)
                    for t in range(TPB):
                        dve.wait_ge(prod_ready, TPB * b + t + 1)
                        nc.vector.reduce_sum(den[:], prod[:, t % 2, :].rearrange(heads, k=MF), AX.X).then_inc(prod_taken, 1)
                        nc.vector.drain()
                        nc.vector.scalar_tensor_tensor(den[:], feature_sum[:], EPS_KERNEL, den[:], ALU.mult, ALU.add)
                        nc.vector.drain()
                        nc.vector.reciprocal(inv[:], den[:])
                        nc.vector.drain()
                        if t >= 2:
                            dve.wait_ge(qT_done, 2 * TPB * b + 2 * t - 2)
                        nc.vector.scalar_tensor_tensor(qs[:, t % 2, :].rearrange(heads, k=MF), qe[:, t, :].rearrange(heads, k=MF), EPS_KERNEL,
                                                       bc(inv[:], MF), ALU.add, ALU.mult).then_inc(qs_ready, 1)
                        if t >= 2:
                            add_out(t - 2)
                    add_out(TPB - 2)
                    add_out(TPB - 1)


def ffn_a(nc, G, W):
    with Memory(nc, "f") as m:
        w1 = m.sbuf("w1", [P, DFF])
        w2 = m.sbuf("w2", [P, FFC, DM])
        b1 = m.sbuf("b1", [P, FFC])
        g1, o1b, b2, g2, o2b = (m.sbuf(n, [P, DM]) for n in ("g1", "o1b", "b2", "g2", "o2b"))
        stats = m.sbuf("stats", [P, TPB, 6])
        mv = m.sbuf("mv", [P, TPB, 2])
        rstd, var, half = (m.sbuf(n, [P, TPB]) for n in ("rstd", "var", "half"))
        o = m.sbuf("o", [P, 2, TPB, DM])
        oT = m.sbuf("oT", [P, 2, HALF])
        ex = m.sbuf("ex", [P, 2, FFC, HALF])
        hT = m.sbuf("hT", [P, 2, FFC, HALF])
        y = m.sbuf("y", [P, TPB, DM])
        ob2 = m.sbuf("ob2", [P, 2, TPB, DM])
        ex_ready, biased, o2_ready = (m.sem(n) for n in ("ex_ready", "biased", "o2_ready"))
        psT = m.psum("psT", [P, 2, HALF])
        psH = m.psum("psH", [P, FFC, HALF])
        psY = m.psum("psY", [P, 2, HALF])
        landed = m.sem("landed")
        o_ready, turned, oT_ready, h_done, h_taken, hT_ready, y_done, y_taken = (m.sem(n) for n in (
            "o_ready", "turned", "oT_ready", "h_done", "h_taken", "hT_ready", "y_done", "y_taken"))
        block = m.block()
        LOADS = 8
        HALVES_AHEAD = 2

        @block.sync
        def _(sp):
            sp.dma_start(w1[:], W["w1"]).then_inc(landed, 16)
            sp.dma_start(w2[:], W["w2"].rearrange("(c p) o -> p c o", p=P)).then_inc(landed, 16)
            sp.dma_start(b1[:], W["b1"]).then_inc(landed, 16)
            for dst, src in ((g1, W["ln1_g"]), (o1b, W["ln1_b"]), (b2, W["b2"]), (g2, W["ln2_g"]), (o2b, W["ln2_b"])):
                sp.dma_start(dst[:], src.unsqueeze(0).to_broadcast([P, DM])).then_inc(landed, 16)
            sp.wait_ge(landed, 16 * LOADS)

        @block.tensor
        def _(pe):
            pe.wait_ge(landed, 16 * LOADS)
            pe.sem_inc(y_done, HALVES_AHEAD)
            pe.sem_inc(h_done, 2 * FFC)

            def up(b, u):
                pe.wait_ge(oT_ready, 2 * b + u + 1 + HALVES_AHEAD)
                for c in range(FFC):
                    pe.wait_ge(h_taken, FFC * (2 * b + u) + c + 1)
                    nc.tensor.matmul(psH[:, c, :], w1[:, c * P:(c + 1) * P], oT[:, u, :], start=True, stop=True).then_inc(h_done, 1)

            def down(b, u):
                pe.wait_ge(hT_ready, 2 * b + u + 1)
                pe.wait_ge(y_taken, 2 * b + u + 1)
                for t in range(4):
                    for c in range(FFC):
                        last = nc.tensor.matmul(psY[:, u, t * DM:(t + 1) * DM], hT[:, u, c, t * P:(t + 1) * P], w2[:, c, :],
                                                start=(c == 0), stop=(c == FFC - 1))
                last.then_inc(y_done, 1)

            def products(b):
                for u in range(2):
                    pe.wait_ge(o_ready, 2 * b + u + 1)
                    pe.wait_ge(oT_ready, 2 * b + u + 1)
                    for t in range(4):
                        last = nc.tensor.transpose(psT[:, u, t * P:(t + 1) * P], o[:, b % 2, 4 * u + t, :], G.ident[:])
                    last.then_inc(turned, 1)
                up(b, 0)
                if b >= 1:
                    down(b - 1, 1)
                up(b, 1)
                down(b, 0)

            for b in range(BATCH):
                products(b)
            down(BATCH - 1, 1)

        @block.scalar
        def _(act):
            act.wait_ge(landed, 16 * LOADS)
            act.sem_inc(oT_ready, HALVES_AHEAD)
            act.sem_inc(h_taken, FFC)

            for b in range(BATCH):
                for u in range(2):
                    act.wait_ge(turned, 2 * b + u + 1)
                    act.wait_ge(h_done, FFC * (2 * b + u) + FFC)
                    nc.scalar.activation(oT[:, u, :], psT[:, u, :], ACT.Copy).then_inc(oT_ready, 1)
                for u in range(2):
                    for c in range(FFC):
                        act.wait_ge(h_done, FFC * (2 * b + u) + c + 1 + 2 * FFC)
                        if c == 0:
                            act.wait_ge(y_done, 2 * b + u + 1)
                        nc.scalar.activation(ex[:, u, c, :], psH[:, c, :], ACT.Exp, bias=b1[:, c:c + 1])
                        last = nc.scalar.activation(hT[:, u, c, :], psH[:, c, :], ACT.Relu, bias=b1[:, c:c + 1])
                        last.then_inc(h_taken, 1)


        @block.gpsimd
        def _(pool):
            pool.wait_ge(landed, 16 * LOADS)
            for b in range(BATCH):
                pool.wait_ge(o_ready, 2 * b + 2)
                if b >= 2:
                    pool.wait_ge(y_taken, 2 * (b - 2) + 2 + HALVES_AHEAD)
                nc.gpsimd.tensor_tensor(ob2[:, b % 2, :, :], o[:, b % 2, :, :], b2[:].unsqueeze(1).to_broadcast([P, TPB, DM]),
                                        ALU.add).then_inc(biased, 1)
                for u in range(2):
                    pool.wait_ge(ex_ready, 2 * b + u + 1)
                    nc.gpsimd.tensor_tensor(hT[:, u, :, :], hT[:, u, :, :], ex[:, u, :, :], ALU.add).then_inc(hT_ready, 1)
                if b >= 1:
                    pool.wait_ge(o2_ready, b)
                    nc.gpsimd.tensor_tensor(G.x[:, b - 1, :, :], G.x[:, b - 1, :, :], G.xn[:, b - 1, :, :], ALU.add)
            pool.wait_ge(o2_ready, BATCH)
            nc.gpsimd.tensor_tensor(G.x[:, BATCH - 1, :, :], G.x[:, BATCH - 1, :, :], G.xn[:, BATCH - 1, :, :], ALU.add)

        @block.vector
        def _(dve):
            dve.wait_ge(landed, 16 * LOADS)
            dve.sem_inc(y_taken, HALVES_AHEAD)

            def normalize(rows, out, gain, offset, ready):
                for t in range(TPB):
                    nc.vector.bn_stats(stats[:, t, :], rows[:, t, :])
                nc.vector.drain()
                for t in range(TPB):
                    nc.vector.bn_aggr(mv[:, t, :], stats[:, t, :])
                nc.vector.drain()
                rsqrt(nc, rstd[:], mv[:, :, 1], EPS_LN_A, var[:], half[:])
                for t in range(TPB):
                    nc.vector.scalar_tensor_tensor(y[:, t, :], rows[:, t, :], mv[:, t, 0:1], gain[:], ALU.subtract, ALU.mult)
                nc.vector.drain()
                for t in range(TPB):
                    last = nc.vector.scalar_tensor_tensor(out[:, t, :], y[:, t, :], rstd[:, t:t + 1], offset[:], ALU.mult, ALU.add)
                    if ready is not None and t % 4 == 3:
                        last.then_inc(ready, 1)
                nc.vector.drain()

            def first_norm(b):
                normalize(G.xn[:, b, :, :], o[:, b % 2, :, :], g1, o1b, o_ready)

            def elu(b):
                for u in range(2):
                    dve.wait_ge(h_taken, FFC * (2 * b + u) + 2 * FFC)
                    nc.vector.tensor_scalar(ex[:, u, :, :], ex[:, u, :, :], 1.0, -1.0, ALU.min, ALU.add).then_inc(ex_ready, 1)

            def second_norm(b):
                rows = G.xn[:, b, :, :]
                dve.wait_ge(biased, b + 1)
                for u in range(2):
                    dve.wait_ge(y_done, 2 * b + u + 1 + HALVES_AHEAD)
                    nc.vector.tensor_tensor(rows[:, 4 * u:4 * u + 4, :], ob2[:, b % 2, 4 * u:4 * u + 4, :],
                                            psY[:, u, :].rearrange("p (t d) -> p t d", d=DM), ALU.add).then_inc(y_taken, 1)
                nc.vector.drain()
                normalize(rows, rows, g2, o2b, None)
                dve.sem_inc(o2_ready, 1)

            first_norm(0)
            first_norm(1)
            for b in range(BATCH):
                elu(b)
                if b >= 1:
                    second_norm(b - 1)
                if b + 2 < BATCH:
                    dve.wait_ge(biased, b + 1)
                    first_norm(b + 2)
            second_norm(BATCH - 1)


def moe(nc, stage, G, W):
    with Memory(nc, stage) as m:
        L = Shared()
        L.w8 = m.sbuf("w8", [P, TILES, TOPK])
        L.place = m.sbuf("place", [P, TILES, TOPK], I32)
        L.wg = m.sbuf("wg", [P, EXPERTS, INTER])
        L.tile_expert = m.sbuf("tile_expert", [1, HALVES * HALF_TILES], I32)
        G.xn = m.sbuf("xn", [P, BATCH, TPB, DM])
        L.wg_landed, L.shared_landed, L.owners_landed = m.sem("wg_landed"), m.sem("shared_landed"), m.sem("owners_landed")
        L.scattered = [m.sem(f"scattered{i}") for i in range(HALVES)]
        with Memory(nc, stage + "r") as r:
            G.xnT = r.sbuf("xnT", [P, BATCH, SEQ])
            L.wgs = r.sbuf("wgs", [P, INTER])
            L.wds = r.sbuf("wds", [INTER, DM])
            L.picked = r.sbuf("picked", [P, TILES, EXPERTS], BF16)
            L.before = r.sbuf("before", [P, TILES + 1, EXPERTS], BF16)
            L.index = r.sbuf("index", [P, TILES, TOPK])
            L.earlier = r.sbuf("earlier", [P, P], BF16)
            L.ones_bf = r.sbuf("ones_bf", [P, P], BF16)
            L.base = r.sbuf("base", [P, BATCH, EXPERTS])
            L.column = r.sbuf("column", [P, EXPERTS])
            L.owner = r.sbuf("owner", [P, HALVES, OWNER_COLUMNS], I32)
            layernorm(nc, stage + "0", G)
            router(nc, stage + "1", G, W, L)
            plan(nc, stage + "2", G, L)
            dispatch(nc, stage + "3", G, L)
        experts(nc, stage + "4", G, W, L)


def router(nc, stage, G, W, L):
    w8, picked, before, index = L.w8, L.picked, L.before, L.index
    with Memory(nc, stage) as m:
        wr = m.sbuf("wr", [P, EXPERTS])
        bias = m.sbuf("bias", [P, EXPERTS])
        xT = m.sbuf("xT", [P, 2, SEQ])
        probs = m.sbuf("probs", [P, 2, TPB, EXPERTS])
        logits = m.sbuf("logits", [P, 2, TPB, EXPERTS])
        top = m.sbuf("top", [P, TPB, TOPK])
        at = m.sbuf("at", [P, TPB, TOPK], mybir.dt.uint32)
        total, inverse = m.sbuf("total", [P, TPB]), m.sbuf("inverse", [P, TPB])
        scratch = m.sbuf("scratch", [P, 1])
        ps = m.psum("ps", [P, 2, TPB // 2, 2, HALF // 2])
        landed, xT_ready, logits_done, logits_ready, probs_ready = (m.sem(n) for n in (
            "landed", "xT_ready", "logits_done", "logits_ready", "probs_ready"))
        block = m.block()
        AHEAD = 2

        def pairs(eng, batch):
            with eng.Fori(0, BATCH // 2) as i:
                for w in range(2):
                    batch(2 * i + w, w)

        @block.sync
        def _(sp):
            sp.dma_start(wr[:], W["routerT"]).then_inc(landed, 16)
            sp.dma_start(bias[:], W["expert_bias"].unsqueeze(0).to_broadcast([P, EXPERTS])).then_inc(landed, 16)
            sp.dma_start(L.wgs[:], W["w_gate_sharedT"]).then_inc(L.shared_landed, 16)
            sp.dma_start(L.wds[:], W["w_down_sharedT"]).then_inc(L.shared_landed, 16)
            sp.dma_start(L.wg[:], W["w_gateT"]).then_inc(L.wg_landed, 16)
            sp.wait_ge(landed, 32)

        @block.gpsimd
        def _(pool):
            def bring(b, w):
                pool.wait_ge(logits_done, b - 2 + 1 + AHEAD)
                nc.gpsimd.tensor_copy(xT[:, w, :], G.xnT[:, bass.ds(b, 1), :].rearrange("p b n -> p (b n)")).then_inc(xT_ready, 1)

            pairs(pool, bring)

        @block.tensor
        def _(pe):
            pe.sem_inc(logits_done, AHEAD)
            pe.wait_ge(landed, 32)

            def multiply(b, w):
                pe.wait_ge(xT_ready, b + 1)
                pe.wait_ge(logits_ready, b - 2 + 1 + AHEAD)
                for t in range(TPB):
                    last = nc.tensor.matmul(ps[:, w, t // 2, t % 2, 0:EXPERTS], xT[:, w, t * P:(t + 1) * P], wr[:], start=True, stop=True)
                last.then_inc(logits_done, 1)

            pairs(pe, multiply)

        @block.scalar
        def _(act):
            def squash(b, w):
                act.wait_ge(logits_ready, b + 1 + AHEAD)
                nc.scalar.activation(probs[:, w, :, :], logits[:, w, :, :], ACT.Sigmoid).then_inc(probs_ready, 1)

            pairs(act, squash)

        @block.vector
        def _(dve):
            nc.vector.memset(before[:, 0, :], 0.0)
            dve.sem_inc(logits_ready, AHEAD)
            dve.wait_ge(landed, 32)

            def add_bias(b, w):
                dve.wait_ge(logits_done, b + 1 + AHEAD)
                nc.vector.tensor_tensor(logits[:, w, :, :], ps[:, w, :, :, 0:EXPERTS].rearrange("p a b e -> p (a b) e"),
                                        bias[:].unsqueeze(1).to_broadcast([P, TPB, EXPERTS]), ALU.add).then_inc(logits_ready, 1)

            def choose(b, w):
                tiles = bass.ds(b * TPB, TPB)
                dve.wait_ge(probs_ready, b + 1)
                nc.vector.memset(scratch[:], 0.0)
                for t in range(TPB):
                    nc.vector.max(top[:, t, :], probs[:, w, t, :])
                nc.vector.drain()
                for t in range(TPB):
                    nc.vector.max_index(at[:, t, :], top[:, t, :], probs[:, w, t, :])
                for t in range(TPB):
                    nc.vector.match_replace(logits[:, w, t, :], top[:, t, :], probs[:, w, t, :], -1.0)
                nc.vector.reduce_sum(total[:], top[:], AX.X)
                nc.vector.drain()
                nc.vector.tensor_copy(index[:, tiles, :], at[:])
                nc.vector.tensor_scalar(total[:], total[:], 1e-9, None, ALU.add)
                nc.vector.tensor_scalar(picked[:, tiles, :], logits[:, w, :, :], 0.0, None, ALU.is_lt)
                nc.vector.drain()
                nc.vector.reciprocal(inverse[:], total[:])
                for t in range(TPB):
                    nc.vector.tensor_tensor(before[:, bass.ds(b * TPB + t + 1, 1), :], before[:, bass.ds(b * TPB + t, 1), :],
                                            picked[:, bass.ds(b * TPB + t, 1), :], ALU.add)
                    nc.vector.drain()
                nc.vector.scalar_tensor_tensor(w8[:, tiles, :], top[:], ROUTED_SCALE, bc(inverse[:], TOPK), ALU.mult, ALU.mult)
                nc.vector.drain()

            with dve.Fori(0, BATCH // 2) as i:
                for w in range(2):
                    add_bias(2 * i + w, w)
                for w in range(2):
                    choose(2 * i + w, w)


def plan(nc, stage, G, L):
    before, base, ones_bf, earlier, column = L.before, L.base, L.ones_bf, L.earlier, L.column
    with Memory(nc, stage) as m:
        count = m.sbuf("count", [P, HALVES, EXPERTS], I32)
        first = m.sbuf("first", [P, EXPERTS])
        tiles = m.sbuf("tiles", [P, HALVES, EXPERTS])
        ends = m.sbuf("ends", [P, 2, HALVES, EXPERTS])
        junk = m.sbuf("junk", [P, EXPERTS])
        number = m.sbuf("number", [P, OWNER_COLUMNS], I32)
        number_f = m.sbuf("number_f", [P, OWNER_COLUMNS])
        owner = m.sbuf("owner", [P, HALVES, OWNER_COLUMNS])
        ps = m.psum("ps", [P, HALVES, HALF])
        made, counted = m.sem("made"), m.sem("counted")
        block = m.block()

        @block.gpsimd
        def _(pool):
            nc.gpsimd.iota(number[:], [[P, OWNER_COLUMNS]], base=0, channel_multiplier=1)
            nc.gpsimd.iota(column[:], [[1, EXPERTS]], base=0, channel_multiplier=0, allow_small_or_imprecise_dtypes=True)
            nc.gpsimd.memset(ones_bf[:], 1.0).then_inc(made, 1)
            pool.wait_ge(made, 1)
            nc.gpsimd.affine_select(out=earlier[:], in_=ones_bf[:], compare_op=ALU.is_gt, fill=0.0, base=0,
                                    pattern=[[1, P]], channel_multiplier=-1).then_inc(made, 1)
            pool.wait_ge(made, 2)

        @block.tensor
        def _(pe):
            pe.wait_ge(made, 1)
            for half in range(HALVES):
                last = nc.tensor.matmul(ps[:, half, 0:EXPERTS], ones_bf[:], before[:, TPH * (half + 1), :], start=True, stop=True)
            last.then_inc(counted, 1)

        @block.vector
        def _(dve):
            dve.wait_ge(made, 2)
            nc.vector.tensor_copy(number_f[:], number[:])
            dve.wait_ge(counted, 1)
            nc.vector.tensor_copy(first[:], ps[:, 0, 0:EXPERTS])
            nc.vector.drain()
            nc.vector.tensor_scalar(count[:, 0, :], first[:], float(P - 1), None, ALU.add)
            nc.vector.scalar_tensor_tensor(count[:, 1, :], ps[:, 1, 0:EXPERTS], float(P - 1), first[:], ALU.add, ALU.subtract)
            nc.vector.drain()
            nc.vector.tensor_scalar(count[:], count[:], P.bit_length() - 1, None, ALU.arith_shift_right)
            nc.vector.drain()
            nc.vector.tensor_copy(tiles[:], count[:])
            nc.vector.tensor_copy(ends[:, 0, :, :], count[:])
            nc.vector.drain()
            step, now = 1, 0
            while step < EXPERTS:
                nc.vector.tensor_copy(ends[:, 1 - now, :, 0:step], ends[:, now, :, 0:step])
                nc.vector.tensor_tensor(ends[:, 1 - now, :, step:], ends[:, now, :, step:], ends[:, now, :, 0:EXPERTS - step], ALU.add)
                nc.vector.drain()
                step, now = 2 * step, 1 - now
            nc.vector.tensor_tensor(tiles[:], ends[:, now, :, :], tiles[:], ALU.subtract)
            nc.vector.drain()
            nc.vector.tensor_scalar(base[:, 0, :], tiles[:, 0, :], float(P), None, ALU.mult)
            nc.vector.tensor_scalar(base[:, 1, :], tiles[:, 0, :], float(P), None, ALU.mult)
            for b in (2, 3):
                nc.vector.scalar_tensor_tensor(base[:, b, :], tiles[:, 1, :], float(P), first[:], ALU.mult, ALU.subtract)
            for half in range(HALVES):
                for j in range(OWNER_COLUMNS):
                    nc.vector.tensor_scalar(junk[:], ends[:, now, half, :], number_f[:, j:j + 1], 0.0, ALU.is_le, ALU.add,
                                            accum_out=owner[:, half, j:j + 1])
                    nc.vector.drain()
            nc.vector.tensor_scalar(L.owner[:], owner[:], float(EXPERTS - 1), None, ALU.min)


EARLY_TILES = 12


def scatter(nc, G, L, t):
    for k in range(TOPK):
        nc.gpsimd.indirect_dma_start(G.slots_in[t // TPH], bass.IndirectOffsetOnAxis(L.place[:, t, k:k + 1], 0),
                                     G.xn[:, t // TPB, t % TPB, :], None).then_inc(L.scattered[t // TPH], 16)


def dispatch(nc, stage, G, L):
    picked, before, base, index, column, place = L.picked, L.before, L.base, L.index, L.column, L.place
    earlier, ones_bf, wgs, wds = L.earlier, L.ones_bf, L.wgs, L.wds
    CHUNK = 2
    with Memory(nc, stage) as m:
        rank = m.sbuf("rank", [P, TPB, EXPERTS])
        junk = m.sbuf("junk", [P, TOPK, EXPERTS])
        slot = m.sbuf("slot", [P, CHUNK, TOPK])
        slot_i, low = m.sbuf("slot_i", [P, CHUNK, TOPK], I32), m.sbuf("low", [P, CHUNK, TOPK], I32)
        hs = m.sbuf("hs", [INTER, 2, HALF])
        ps = m.psum("ps", [P, TPB // 2, 2, HALF // 2])
        psh = m.psum("psh", [P, 2, HALF])
        pss = m.psum("pss", [P, 2, HALF])
        rounds, ranked, placed, up_done, hs_ready, shared_done = (m.sem(n) for n in (
            "rounds", "ranked", "placed", "up_done", "hs_ready", "shared_done"))
        block = m.block()
        written = m.sem("written")
        WORKERS = 3

        def end_round(eng):
            eng.drain()
            eng.sem_inc(rounds, 1)

        @block.sync
        def _(sp):
            for half in range(HALVES):
                for j in range(OWNER_COLUMNS):
                    n = min(P, HALF_TILES - j * P)
                    at = half * HALF_TILES + j * P
                    sp.dma_start(G.owner_dram[at:at + n, :], L.owner[0:n, half, j:j + 1]).then_inc(written, 16)
            sp.wait_ge(written, 16 * HALVES * OWNER_COLUMNS)
            sp.dma_start(L.tile_expert[:], G.owner_dram.rearrange("t a -> a t")).then_inc(L.owners_landed, 16)

        @block.tensor
        def _(pe):
            end_round(pe)
            pe.wait_ge(L.shared_landed, 32)
            with pe.Fori(0, BATCH) as b:
                pe.wait_ge(rounds, WORKERS * b + WORKERS)
                for t in range(TPB):
                    out = ps[:, t // 2, t % 2, 0:EXPERTS]
                    nc.tensor.matmul(out, earlier[:], picked[:, bass.ds(b * TPB + t, 1), :].rearrange("p a e -> p (a e)"),
                                     start=True, stop=False)
                    last = nc.tensor.matmul(out, ones_bf[:], before[:, bass.ds(b * TPB + t, 1), :].rearrange("p a e -> p (a e)"),
                                            start=False, stop=True)
                last.then_inc(ranked, 1)
                for u in range(2):
                    nc.tensor.matmul(psh[0:INTER, u, :], wgs[:],
                                     G.xnT[:, bass.ds(b, 1), u * HALF:(u + 1) * HALF].rearrange("p b n -> p (b n)"),
                                     start=True, stop=True).then_inc(up_done, 1)
                for u in range(2):
                    pe.wait_ge(hs_ready, 2 * b + u + 1)
                    for t in range(4):
                        last = nc.tensor.matmul(pss[:, u, t * DM:(t + 1) * DM], hs[:, u, t * P:(t + 1) * P], wds[:], start=True, stop=True)
                    last.then_inc(shared_done, 1)
                end_round(pe)

        @block.scalar
        def _(act):
            end_round(act)
            with act.Fori(0, BATCH) as b:
                for u in range(2):
                    act.wait_ge(up_done, 2 * b + u + 1)
                    nc.scalar.activation(hs[:, u, :], psh[0:INTER, u, :], ACT.Silu).then_inc(hs_ready, 1)
                end_round(act)

        @block.vector
        def _(dve):
            end_round(dve)
            with dve.Fori(0, BATCH) as b:
                dve.wait_ge(rounds, WORKERS * b + WORKERS)
                dve.wait_ge(ranked, b + 1)
                nc.vector.tensor_tensor(rank[:], ps[:, :, :, 0:EXPERTS].rearrange("p a b e -> p (a b) e"),
                                        base[:, bass.ds(b, 1), :].to_broadcast([P, TPB, EXPERTS]), ALU.add)
                nc.vector.drain()
                ib = index[:, bass.ds(b * TPB, TPB), :]
                for t0 in range(0, TPB, CHUNK):
                    for t in range(CHUNK):
                        for k in range(TOPK):
                            nc.vector.scalar_tensor_tensor(junk[:, k, :], column[:], ib[:, t0 + t, k:k + 1], rank[:, t0 + t, :],
                                                           ALU.is_equal, ALU.mult, accum_out=slot[:, t, k:k + 1])
                        nc.vector.drain()
                    nc.vector.tensor_copy(slot_i[:], slot[:])
                    nc.vector.drain()
                    at = place[:, bass.ds(b * TPB + t0, CHUNK), :]
                    nc.vector.tensor_scalar(low[:], slot_i[:], P - 1, 2, ALU.bitwise_and, ALU.logical_shift_left)
                    nc.vector.tensor_scalar(at, slot_i[:], 7, 3, ALU.logical_shift_right, ALU.bitwise_and)
                    nc.vector.drain()
                    nc.vector.tensor_scalar(slot_i[:], slot_i[:], ~(GROUP_SLOTS - 1), None, ALU.bitwise_and)
                    nc.vector.tensor_tensor(at, at, low[:], ALU.bitwise_or)
                    nc.vector.drain()
                    nc.vector.tensor_tensor(at, at, slot_i[:], ALU.bitwise_or).then_inc(placed, 1)
                    nc.vector.drain()
                xb = G.x[:, bass.ds(b, 1), :, :].rearrange("p b t d -> p (b t) d")
                for u in range(2):
                    dve.wait_ge(shared_done, 2 * b + u + 1)
                    nc.vector.tensor_tensor(xb[:, 4 * u:4 * u + 4, :], xb[:, 4 * u:4 * u + 4, :],
                                            pss[:, u, :].rearrange("p (t d) -> p t d", d=DM), ALU.add)
                end_round(dve)

        @block.gpsimd
        def _(pool):
            for t in range(EARLY_TILES):
                if t % CHUNK == 0:
                    pool.wait_ge(placed, t // CHUNK + 1)
                scatter(nc, G, L, t)


def experts(nc, stage, G, W, L):
    tile_expert, place, w8 = L.tile_expert, L.place, L.w8
    DEEP = 4
    PEEL = 3
    FIRST_STAGES = GROUPS - TPH * DEEP
    RING = BATCH
    PE, DVE = mybir.EngineType.PE, mybir.EngineType.DVE
    assert FIRST_STAGES >= HALF_GROUPS and (GROUPS - 1 - PEEL) % DEEP == 0 and HALF_GROUPS % DEEP == 0 and TPB == TOPK
    with Memory(nc, stage) as m:
        wd = m.sbuf("wd", [INTER, EXPERTS, DM])
        wg2, wd2 = L.wg[:].rearrange("p e i -> p (e i)"), wd[:].rearrange("p e d -> p (e d)")
        wd_landed = m.sem("wd_landed")
        rows = m.sbuf("rows", [P, DEEP, GROUP, DM])
        xT = m.sbuf("xT", [P, 2, HALF])
        up_w = m.sbuf("up_w", [P, DEEP, GROUP, INTER])
        hT = m.sbuf("hT", [INTER, 2, GROUP, P])
        y = m.sbuf("y", [P, DEEP, GROUP, DM])
        sum8 = m.sbuf("sum8", [P, DM])
        got = G.xn
        psX = m.psum("psX", [P, 2, HALF])
        psH = m.psum("psH", [INTER, 2, GROUP, P])
        psY = m.psum("psY", [P, 2, HALF])
        rows_landed = [m.sem(f"rows_landed{i}") for i in range(DEEP)]
        stored = [m.sem(f"stored{i}") for i in range(DEEP)]
        x_turned, xT_ready, staged, up_done, hT_ready, down_done, y_ready = (m.sem(n) for n in (
            "x_turned", "xT_ready", "staged", "up_done", "hT_ready", "down_done", "y_ready"))
        AHEAD = DEEP
        gathered = [m.sem(f"gathered{i}") for i in range(RING)]
        added = m.sem("added")
        block = m.block()
        src, dst = ([s.rearrange("(g p j) d -> g p (j d)", p=P, j=GROUP) for s in slots] for slots in (G.slots_in, G.slots_out))
        flat = "p j d -> p (j d)"

        def done(g):
            return g + 1 + AHEAD

        def owners(g, engine):
            at = tile_expert[0:1, g * GROUP:(g + 1) * GROUP] if isinstance(g, int) else tile_expert[0:1, bass.ds(g * GROUP, GROUP)]
            _, e = nc.values_load_multi_w_load_instructions(
                at, engines=[engine], min_val=0, max_val=EXPERTS - 1,
                skip_runtime_bounds_check_because="the plan clamps it to the last expert")
            return e

        def stores(half):
            return 16 * ((half + 1) * HALF_GROUPS // DEEP + 1)

        @block.sync
        def _(sp):
            def rows_of(slots, g):
                return slots[g] if isinstance(g, int) else slots[bass.ds(g, 1)].rearrange("g p n -> (g p) n")

            def load(half, g, u):
                sp.dma_start(rows[:, u % DEEP, :, :].rearrange(flat), rows_of(src[half], g)).then_inc(rows_landed[u % DEEP], 16)

            def store(half, g, u):
                sp.wait_ge(y_ready, done(half * HALF_GROUPS + g))
                sp.dma_start(rows_of(dst[half], g), y[:, u % DEEP, :, :].rearrange(flat)).then_inc(stored[u % DEEP], 16)

            for s in stored:
                sp.sem_inc(s, 16)
            sp.dma_start(wd[:], W["w_downT"]).then_inc(wd_landed, 16)
            sp.wait_ge(L.scattered[0], 16 * TPH * TOPK)
            for u in range(DEEP):
                load(0, u, u)
            for half in range(HALVES):
                with sp.Fori(0, HALF_GROUPS // DEEP - 1) as i:
                    for u in range(DEEP):
                        sp.wait_ge(x_turned, done(i * DEEP + half * HALF_GROUPS + u))
                        load(half, i * DEEP + DEEP + u, u)
                        store(half, i * DEEP + u, u)
                if half + 1 < HALVES:
                    sp.wait_ge(L.scattered[half + 1], 16 * TPH * TOPK)
                for u in range(DEEP):
                    if half + 1 < HALVES:
                        sp.wait_ge(x_turned, done((half + 1) * HALF_GROUPS - DEEP + u))
                        load(half + 1, u, u)
                    store(half, HALF_GROUPS - DEEP + u, u)
            for s in stored:
                sp.wait_ge(s, stores(HALVES - 1))

        @block.gpsimd
        def _(pool):
            for t in range(EARLY_TILES, TILES):
                scatter(nc, G, L, t)
            pool.wait_ge(L.scattered[1], 16 * TPH * TOPK)
            for t in range(TILES):
                if t % TPH == 0:
                    for s in stored:
                        pool.wait_ge(s, stores(t // TPH))
                if t >= RING:
                    pool.wait_ge(added, t - RING + 1)
                for k in range(TOPK):
                    nc.gpsimd.indirect_dma_start(got[:, t % RING, k, :], None, G.slots_out[t // TPH],
                                                 bass.IndirectOffsetOnAxis(place[:, t, k:k + 1], 0)).then_inc(gathered[t % RING], 16)

        @block.tensor
        def _(pe):
            for s in (x_turned, up_done, down_done):
                pe.sem_inc(s, AHEAD)
            pe.wait_ge(L.wg_landed, 16)
            pe.wait_ge(L.owners_landed, 16)

            def turn(g, u, landings):
                pe.wait_ge(rows_landed[u % DEEP], 16 * landings)
                pe.wait_ge(xT_ready, done(g - 2))
                for j in range(GROUP):
                    last = nc.tensor.transpose(psX[:, u % 2, j * P:(j + 1) * P], rows[:, u % DEEP, j, :], G.ident[:])
                last.then_inc(x_turned, 1)

            def up(g, u):
                pe.wait_ge(L.wg_landed, 16)
                pe.wait_ge(xT_ready, done(g))
                pe.wait_ge(staged, done(g))
                pe.wait_ge(hT_ready, done(g - 2))
                for j in range(GROUP):
                    last = nc.tensor.matmul(psH[:, u % 2, j, :], up_w[:, u % DEEP, j, :], xT[:, u % 2, j * P:(j + 1) * P],
                                            start=True, stop=True)
                last.then_inc(up_done, 1)

            def down(g, u, e):
                pe.wait_ge(hT_ready, done(g))
                pe.wait_ge(y_ready, done(g - 2))
                for j in range(GROUP):
                    last = nc.tensor.matmul(psY[:, u % 2, j * DM:(j + 1) * DM], hT[:, u % 2, j, :],
                                            wd2[:, bass.ds(e[j] * DM, DM)], start=True, stop=True)
                last.then_inc(down_done, 1)

            turn(0, 0, 1)
            def step(g, u, landings):
                up(g, u)
                if landings is not None:
                    turn(g + 1, u + 1, landings)
                if not (isinstance(g, int) and g == 0):
                    down(g - 1, u - 1, owners(g - 1, PE))

            for g in range(PEEL):
                if g == 1:
                    pe.wait_ge(wd_landed, 16)
                step(g, g, (g + 1) // DEEP + 1)
            with pe.Fori(0, (GROUPS - 1 - PEEL) // DEEP) as i:
                for u in range(DEEP):
                    step(i * DEEP + PEEL + u, PEEL + u, i + 2)
            step(GROUPS - 1, GROUPS - 1, None)
            down(GROUPS - 1, GROUPS - 1, owners(GROUPS - 1, PE))

        @block.scalar
        def _(act):
            for s in (xT_ready, hT_ready, y_ready):
                act.sem_inc(s, AHEAD)

            def take_xT(g, u):
                act.wait_ge(x_turned, done(g))
                act.wait_ge(up_done, done(g - 2))
                nc.scalar.activation(xT[:, u % 2, :], psX[:, u % 2, :], ACT.Copy).then_inc(xT_ready, 1)

            def take_y(g, u, left):
                act.wait_ge(down_done, done(g))
                act.wait_ge(stored[u % DEEP], 16 * (left + 1))
                nc.scalar.activation(y[:, u % DEEP, :, :].rearrange(flat), psY[:, u % 2, :], ACT.Copy).then_inc(y_ready, 1)

            def step(g, u, left, more=True):
                act.wait_ge(up_done, done(g))
                act.wait_ge(down_done, done(g - 2))
                nc.scalar.activation(hT[:, u % 2, :, :], psH[:, u % 2, :, :], ACT.Silu).then_inc(hT_ready, 1)
                if more:
                    take_xT(g + 1, u + 1)
                if not (isinstance(g, int) and g == 0):
                    take_y(g - 1, u - 1, left)

            take_xT(0, 0)
            for g in range(PEEL):
                step(g, g, 0)
            with act.Fori(0, (GROUPS - 1 - PEEL) // DEEP) as i:
                for u in range(DEEP):
                    step(i * DEEP + PEEL + u, PEEL + u, i + (PEEL + u - 1) // DEEP)
            step(GROUPS - 1, GROUPS - 1, (GROUPS - 2) // DEEP, more=False)
            take_y(GROUPS - 1, GROUPS - 1, (GROUPS - 1) // DEEP)

        @block.vector
        def _(dve):
            x = G.x[:].rearrange("p b t d -> p (b t) d")
            dve.sem_inc(staged, AHEAD)
            dve.wait_ge(L.owners_landed, 16)
            dve.wait_ge(L.wg_landed, 16)

            def stage(g, u):
                e = owners(g, DVE)
                dve.wait_ge(L.wg_landed, 16)
                dve.wait_ge(up_done, done(g - DEEP))
                for j in range(GROUP):
                    last = nc.vector.tensor_copy(up_w[:, u % DEEP, j, :], wg2[:, bass.ds(e[j] * INTER, INTER)])
                last.then_inc(staged, 1)

            def combine(i, ring):
                dve.wait_ge(gathered[ring], 16 * TOPK * i + 16 * TOPK)
                t = bass.ds(i * RING + ring, 1)
                xt, wt = x[:, t, :].rearrange("p a d -> p (a d)"), w8[:, t, :].rearrange("p a k -> p (a k)")
                rows8 = got[:, ring, :, :]
                nc.vector.tensor_tensor(rows8, rows8, bc(wt, DM), ALU.mult)
                nc.vector.drain()
                nc.vector.reduce_sum(sum8[:], rows8.rearrange("p k d -> p d k"), AX.X)
                nc.vector.drain()
                nc.vector.tensor_tensor(xt, xt, sum8[:], ALU.add).then_inc(added, 1)

            with dve.Fori(0, FIRST_STAGES // DEEP) as i:
                for u in range(DEEP):
                    stage(i * DEEP + u, u)
            with dve.Fori(0, TPH // RING) as i:
                for ring in range(RING):
                    for u in range(DEEP):
                        stage(i * (RING * DEEP) + FIRST_STAGES + ring * DEEP + u, u)
                    combine(i, ring)
            with dve.Fori(TPH // RING, TILES // RING) as i:
                for ring in range(RING):
                    combine(i, ring)


def attn_b(nc, stage, G, W):
    with Memory(nc, stage) as m:
        L = Shared()
        L.v = m.sbuf("v", [P, TILES, HB, WB])
        L.parts = m.sbuf("parts", [P, 2, 2, 3, SEQ], BF16)
        L.wo = m.sbuf("wo", [P, DM])
        L.wo_landed, L.ones_stored = m.sem("wo_landed"), m.sem("ones_stored")
        L.stored = [m.sem(f"stored{w}") for w in range(2)]
        with Memory(nc, stage + "n") as n:
            normed(G, n)
            layernorm(nc, stage + "0", G)
            project_b(nc, stage + "1", G, W, L)
        attend_b(nc, stage + "2", G, L)


def project_b(nc, stage, G, W, L):
    with Memory(nc, stage) as m:
        wq, wk, wv, bo = (m.sbuf(n, [P, DM]) for n in ("wq", "wk", "wv", "bo"))
        xT = m.sbuf("xT", [P, 2, SEQ])
        parts, stored = L.parts, L.stored
        rest = m.sbuf("rest", [P, 2, SEQ])
        ones = m.sbuf("ones", [3 * HB, SEQ], BF16)
        ps = m.psum("ps", [P, 2, 2, HALF])
        psv = m.psum("psv", [P, 2, HALF])
        landed, ones_made, xT_ready, qk_done, qk_taken, v_done, v_taken, high_ready, parts_ready = (m.sem(n) for n in (
            "landed", "ones_made", "xT_ready", "qk_done", "qk_taken", "v_done", "v_taken", "high_ready", "parts_ready"))
        block = m.block()
        AHEAD = 2

        def pairs(eng, batch):
            with eng.Fori(0, BATCH // 2) as i:
                for w in range(2):
                    batch(2 * i + w, w, i)

        @block.sync
        def _(sp):
            for dst, src in ((wq, W["bwqT"]), (wk, W["bwkT"]), (wv, W["bwvT"]), (bo, W["bo"].unsqueeze(0).to_broadcast([P, DM]))):
                sp.dma_start(dst[:], src).then_inc(landed, 16)
            sp.dma_start(L.wo[:], W["bwoT"]).then_inc(L.wo_landed, 16)
            for s in stored:
                sp.sem_inc(s, 16)
            sp.wait_ge(ones_made, 1)
            sp.dma_start(G.one_rows, ones[:]).then_inc(L.ones_stored, 16)

            def store(b, w, i):
                cols = bass.ds(b * SEQ, SEQ)
                for n, dst, count in ((0, G.q_parts, 3), (1, G.k_parts, 3), (1, G.k_parts[3 * P:5 * P, :], 2)):
                    sp.wait_ge(parts_ready, 2 * b + n + 1)
                    sp.dma_start(dst[0:count * P, cols].rearrange("(i p) n -> p i n", p=P), parts[:, w, n, 0:count, :]).then_inc(stored[w], 16)

            pairs(sp, store)

        @block.gpsimd
        def _(pool):
            def bring(b, w, i):
                pool.wait_ge(v_done, b - 2 + 1 + AHEAD)
                nc.gpsimd.tensor_copy(xT[:, w, :], G.xnT[:, bass.ds(b, 1), :].rearrange("p b n -> p (b n)")).then_inc(xT_ready, 1)

            pairs(pool, bring)

        @block.tensor
        def _(pe):
            pe.wait_ge(landed, 64)
            pe.sem_inc(v_done, AHEAD)

            def multiply(b, w, i):
                pe.wait_ge(xT_ready, b + 1)
                for n, wqk in enumerate((wq, wk)):
                    pe.wait_ge(qk_taken, 2 * (b - 1) + n + 1 + AHEAD)
                    for u in range(2):
                        last = nc.tensor.matmul(ps[:, n, u, :], wqk[:], xT[:, w, u * HALF:(u + 1) * HALF], start=True, stop=True)
                    last.then_inc(qk_done, 1)
                pe.wait_ge(v_taken, b - 1 + 1 + AHEAD)
                for t in range(TPB):
                    last = nc.tensor.matmul(psv[:, t // 4, (t % 4) * DM:(t % 4 + 1) * DM], xT[:, w, t * P:(t + 1) * P], wv[:],
                                            start=True, stop=True)
                last.then_inc(v_done, 1)

            pairs(pe, multiply)

        @block.scalar
        def _(act):
            act.sem_inc(v_taken, AHEAD)

            def take(b, w, i):
                for n in range(2):
                    act.wait_ge(qk_done, 2 * b + n + 1)
                    if n == 0:
                        act.wait_ge(stored[w], 16 * STORES * i + 16)
                    nc.scalar.activation(parts[:, w, n, 0, :], ps[:, n, :, :].rearrange("p u n -> p (u n)"), ACT.Copy).then_inc(high_ready, 1)
                act.wait_ge(v_done, b + 1 + AHEAD)
                nc.scalar.activation(L.v[:, bass.ds(b * TPB, TPB), :, :],
                                     psv[:].rearrange("p u (t h d) -> p (u t) h d", h=HB, d=WB), ACT.Copy).then_inc(v_taken, 1)

            pairs(act, take)

        @block.vector
        def _(dve):
            nc.vector.memset(ones[:], 1.0).then_inc(ones_made, 1)
            dve.sem_inc(qk_taken, AHEAD)
            dve.wait_ge(landed, 64)

            def cut(b, w, i):
                for n in range(2):
                    dve.wait_ge(high_ready, 2 * b + n + 1)
                    nc.vector.tensor_tensor(rest[:, n, :], ps[:, n, :, :].rearrange("p u n -> p (u n)"), parts[:, w, n, 0, :],
                                            ALU.subtract).then_inc(qk_taken, 1)
                    nc.vector.drain()
                    nc.vector.tensor_copy(parts[:, w, n, 1, :], rest[:, n, :])
                    nc.vector.drain()
                    nc.vector.tensor_tensor(parts[:, w, n, 2, :], rest[:, n, :], parts[:, w, n, 1, :], ALU.subtract).then_inc(parts_ready, 1)
                xb = G.x[:, bass.ds(b, 1), :, :].rearrange("p b t d -> p (b t) d")
                nc.vector.tensor_tensor(xb, xb, bo[:].unsqueeze(1).to_broadcast([P, TPB, DM]), ALU.add)

            pairs(dve, cut)


def attend_b(nc, stage, G, L):
    SCALE = float(1.0 / np.sqrt(WB))
    HG = 4
    GB = HB // HG
    LAST = BATCH - 1
    QT = SEQ // P
    STEPS = [(1, kt, max(0, kt - 4) * P) for kt in range(8)] + [(0, kt, kt * P) for kt in range(4)]
    HALF1_STEPS = 8
    MAXIMA = [(h, qt, kh) for h in range(HG) for qt, kh in ((4, 0), (0, 0), (5, 0), (1, 0), (6, 0), (2, 0),
                                                            (7, 0), (4, 1), (3, 0), (5, 1), (7, 1), (6, 1))]
    assert sorted(MAXIMA) == [(h, qt, kh) for h in range(HG) for qt in range(QT) for kh in range(1 + (qt >= 4))]
    DIAGONAL = [e for e, (half, kt, q0) in enumerate(STEPS) if kt >= 4 * half]
    LAG = 2
    KEPT = LAG + 1
    CONTEXT_STEP = 11
    TURN_STEP = 9
    EARLY_STEPS = range(TURN_STEP, len(STEPS))
    LATE_STEPS = range(TURN_STEP - 1)
    PARTS = 4
    PLACE_SHARE = (2, 3, 2, 1)
    NM = len(MAXIMA)
    SLOT = NM + 1 + 2
    BATCH_USES = GB * SLOT + 4
    with Memory(nc, stage) as m:
        qS, kS = (m.sbuf(n, [P, GB, HG, SEQ], BF16) for n in ("qS", "kS"))
        ident_bf = m.sbuf("ident_bf", [P, P], BF16)
        mask_q = m.sbuf("mask_q", [P, P], BF16)
        vb = m.sbuf("vb", [P, QT, HB, VW])
        pT = m.sbuf("pT", [P, KEPT, HG, HALF])
        peak = m.sbuf("peak", [P, HG, QT])
        peak2 = m.sbuf("peak2", [P, HG, QT // 2, 2])
        negp = m.sbuf("negp", [HG * QT, 2, 3, P], BF16)
        negr = m.sbuf("negr", [HG * QT, P])
        ctxu = m.sbuf("ctxu", [P, 2, HALF])
        inv = m.sbuf("inv", [P, 4, HG])
        ctx = m.sbuf("ctx", [P, QT, HB, WB])
        ctxT = m.sbuf("ctxT", [P, SEQ])
        psE = m.psum("psE", [P, 2, 2, HALF])
        psM = m.psum("psM", [P, 2, HALF])
        psV = m.psum("psV", [P, 2, HALF])
        made, ones_landed, v_room, v_ready, slot_done, masked, weights_seen = (m.sem(n) for n in (
            "made", "ones_landed", "v_room", "v_ready", "slot_done", "masked", "weights_seen"))
        stack_landed = [m.sem(f"stack_landed{g}") for g in range(GB)]
        peaks_landed = [m.sem(f"peaks_landed{g}") for g in range(GB)]
        m_done, m_taken, peak_ready, split_ready, e_done, e_taken, pv_done, ctx_taken, ctx_ready, ctxT_ready = (m.sem(n) for n in (
            "m_done", "m_taken", "peak_ready", "split_ready", "e_done", "e_taken", "pv_done", "ctx_taken", "ctx_ready", "ctxT_ready"))
        block = m.block()
        AHEAD = 2

        def batches(eng, batch):
            with eng.Fori(0, LAST) as b:
                batch(b, False)
            batch(LAST, True)

        places = [(e, part) for steps in (EARLY_STEPS, LATE_STEPS) for e in steps for part in range(PARTS)]
        share = [PLACE_SHARE[part] * (HALF - STEPS[e if part < 2 else e - LAG][2]) for e, part in places]

        def maxima_at(e, part):
            at = places.index((e, part)) if (e, part) in places else 0
            return range(NM * sum(share[:at]) // sum(share), NM * sum(share[:at + 1]) // sum(share)) if (e, part) in places else ()

        EARLY = NM * sum(share[:len(EARLY_STEPS) * PARTS]) // sum(share)
        FIRST_USES = NM + 1 + EARLY

        def uses(b, g, last):
            return FIRST_USES + b * BATCH_USES + g * SLOT - (g > 0) - (EARLY if last and g == GB - 1 else 0)

        def others(g, last):
            return not (last and g == GB - 1), not (last and g >= GB - 2)

        @block.sync
        def _(sp):
            def load(b, g):
                heads, cols = slice(g * HG, (g + 1) * HG), bass.ds(b * SEQ, SEQ)
                for dst, src, step in ((qS, G.q_parts, 0), (kS, G.k_parts, P)):
                    for i in range(3):
                        sp.dma_start(dst[3 * WB * i:3 * WB * (i + 1), g, :, :],
                                     src[i * step:i * step + 3 * P, cols].rearrange("(r h) n -> r h n", h=HB)[:, heads, :]
                                     ).then_inc(stack_landed[g], 16)

            def peaks(n, g):
                sp.wait_ge(split_ready, n + 1)
                for i in range(3):
                    sp.dma_start(qS[STACK + i:STACK + i + 1, g, :, :].rearrange("a h (t q) -> a (h t) q", q=P),
                                 negp[:, g % 2, i, :]).then_inc(peaks_landed[g], 16)

            sp.wait_ge(L.stored[0], 16 * STORES + 16)
            for g in range(GB):
                load(0, g)
            sp.wait_ge(L.ones_stored, 16)
            sp.dma_start(kS[STACK:STACK + 3, :, :, :].rearrange("a g h n -> a (g h) n"), G.one_rows.rearrange("(a h) n -> a h n", a=3)).then_inc(ones_landed, 16)
            peaks(0, 0)
            for s in L.stored:
                sp.wait_ge(s, 16 * STORES * (BATCH // 2) + 16)

            def batch(b, last):
                for g in range(GB):
                    if not (last and g == GB - 1):
                        peaks(b * GB + g + 1, (g + 1) % GB)
                    if not last:
                        sp.wait_ge(slot_done, b * GB + g + 1)
                        load(b + 1, g)

            batches(sp, batch)

        @block.gpsimd
        def _(pool):
            def values(b, g):
                heads = slice(g * HG, (g + 1) * HG)
                nc.gpsimd.tensor_copy(vb[:, :, heads, 0:WB], L.v[:, bass.ds(b * QT, QT), heads, :]).then_inc(v_ready, 1)

            nc.gpsimd.memset(mask_q[:], 0.0)
            nc.gpsimd.tensor_copy(ident_bf[:], G.ident[:]).then_inc(made, 1)
            pool.wait_ge(made, 1)
            nc.gpsimd.affine_select(out=mask_q[:], in_=mask_q[:], compare_op=ALU.is_ge, fill=MASKED, base=0,
                                    pattern=[[-1, P]], channel_multiplier=1).then_inc(made, 1)
            nc.gpsimd.memset(vb[:], 0.0).then_inc(v_room, 1)
            pool.wait_ge(v_room, 1)
            nc.gpsimd.memset(vb[:, :, :, WB:WB + 1], 1.0)
            for g in range(GB):
                values(0, g)

            def batch(b, last):
                for g in range(GB):
                    if g > 0 and not last:
                        pool.wait_ge(slot_done, b * GB + g)
                        values(b + 1, g - 1)
                    for i, e in enumerate(DIAGONAL):
                        q0 = STEPS[e][2]
                        tile = pT[:, e % KEPT, :, q0:q0 + P]
                        pool.wait_ge(e_taken, (b * GB + g) * 24 + 2 * e + 2 + AHEAD)
                        pool.sem_inc(weights_seen, 1)
                        nc.gpsimd.affine_select(out=tile, in_=tile, compare_op=ALU.is_ge, fill=0.0, base=0,
                                                pattern=[[0, HG], [1, P]], channel_multiplier=-1).then_inc(masked, 1)
                if not last:
                    pool.wait_ge(slot_done, b * GB + GB)
                    values(b + 1, GB - 1)

            batches(pool, batch)

        @block.tensor
        def _(pe):
            pe.wait_ge(made, 2)
            pe.wait_ge(L.wo_landed, 16)

            def use(c):
                pe.wait_ge(m_taken, c + 1)

            def maximum(c, parity, g, k):
                h, qt, kh = MAXIMA[k]
                n = min(HALF, (qt + 1) * P - kh * HALF)
                diagonal = (qt + 1) * P - kh * HALF <= HALF
                use(c)
                edge = n - P if diagonal else n
                if edge:
                    last = nc.tensor.matmul(psM[:, parity, 0:edge], qS[0:STACK, g, h, qt * P:(qt + 1) * P],
                                            kS[0:STACK, g, h, kh * HALF:kh * HALF + edge], start=True, stop=True)
                if diagonal:
                    nc.tensor.matmul(psM[:, parity, edge:n], qS[0:STACK, g, h, qt * P:(qt + 1) * P],
                                     kS[0:STACK, g, h, kh * HALF + edge:kh * HALF + n], start=True, stop=False)
                    last = nc.tensor.matmul(psM[:, parity, edge:n], ident_bf[:], mask_q[:], start=False, stop=True)
                last.then_inc(m_done, 1)

            def turn_maxima(c, parity, n):
                pe.wait_ge(peak_ready, n + 1)
                use(c)
                nc.tensor.transpose(psM[0:HG * QT, parity, 0:P], peak[:].rearrange("p h t -> p (h t)"), G.ident[:]).then_inc(m_done, 1)

            def scores(b, g, e, pair):
                half, kt, q0 = STEPS[e]
                pe.wait_ge(e_taken, (b * GB + g) * 24 + 2 * e + pair + 1)
                for i in range(2):
                    h = 2 * pair + i
                    last = nc.tensor.matmul(psE[:, pair, i, q0:HALF], kS[0:STACK + 3, g, h, kt * P:(kt + 1) * P],
                                            qS[0:STACK + 3, g, h, half * HALF + q0:(half + 1) * HALF], start=True, stop=True)
                last.then_inc(e_done, 1)

            def weigh(b, g, e, pair):
                half, kt, q0 = STEPS[e]
                if pair == 0:
                    if e in DIAGONAL:
                        pe.wait_ge(masked, (b * GB + g) * len(DIAGONAL) + DIAGONAL.index(e) + 1)
                    else:
                        pe.wait_ge(e_taken, (b * GB + g) * 24 + 2 * e + 2 + AHEAD)
                    if kt == 0:
                        pe.wait_ge(ctx_taken, (b * GB + g) * 2 + 1 - half + AHEAD - 1)
                for h in (2 * pair, 2 * pair + 1):
                    last = nc.tensor.matmul(psV[32 * h:32 * h + 32, half, q0:HALF], vb[:, kt, g * HG + h, :], pT[:, e % KEPT, h, q0:HALF],
                                            start=(kt == 0), stop=True, skip_group_check=True)
                if pair == 1:
                    last.then_inc(pv_done, 1)

            def turn_context(b, g, half, c, parity):
                pe.wait_ge(ctx_taken, (b * GB + g) * 2 + 1 - half + 1 + AHEAD)
                use(c)
                for t in range(4):
                    last = nc.tensor.transpose(psM[:, parity, t * P:(t + 1) * P], ctxu[:, half, t * P:(t + 1) * P], G.ident[:])
                last.then_inc(m_done, 1)

            pe.wait_ge(stack_landed[0], 16 * LOADS)
            for k in range(NM):
                maximum(k, k % 2, 0, k)
            turn_maxima(NM, NM % 2, 0)
            pe.wait_ge(stack_landed[1], 16 * LOADS)
            for k in range(EARLY):
                maximum(NM + 1 + k, (NM + 1 + k) % 2, 1, k)
            pe.wait_ge(ones_landed, 16)

            def batch(b, last):
                for g in range(GB):
                    n = b * GB + g
                    more, more2 = others(g, last)
                    c, parity = uses(b, g, last), uses(0, g, last) % 2
                    pe.wait_ge(peaks_landed[g], 48 * b + 48)
                    pe.wait_ge(v_ready, n + 1)
                    for e in range(len(STEPS)):
                        if e == TURN_STEP:
                            if more:
                                turn_maxima(c, parity, n + 1)
                                c, parity = c + 1, 1 - parity
                            if more2:
                                pe.wait_ge(stack_landed[(g + 2) % GB], 16 * LOADS * (b + (g + 2) // GB + 1))
                        if e == CONTEXT_STEP:
                            turn_context(b, g, 1, c, parity)
                            c, parity = c + 1, 1 - parity
                        for part in range(PARTS):
                            if part < 2:
                                scores(b, g, e, part)
                            elif e >= LAG:
                                weigh(b, g, e - LAG, part - 2)
                            if part == 0 and e == 2 and g > 0:
                                turn_context(b, g - 1, 0, c, parity)
                                c, parity = c + 1, 1 - parity
                                pe.wait_ge(m_done, c)
                                pe.sem_inc(slot_done, 1)
                            early = e in EARLY_STEPS
                            if more2 if early else more:
                                for k in maxima_at(e, part):
                                    maximum(c, parity, (g + 1 + early) % GB, k)
                                    c, parity = c + 1, 1 - parity
                    for e in range(len(STEPS) - LAG, len(STEPS)):
                        for pair in range(2):
                            weigh(b, g, e, pair)
                turn_context(b, GB - 1, 0, c, parity)
                c, parity = c + 1, 1 - parity
                pe.wait_ge(m_done, c)
                pe.sem_inc(slot_done, 1)
                pe.wait_ge(ctx_ready, 2 * GB * b + 2 * GB)
                for u in range(2):
                    use(c)
                    for t in range(4):
                        last = nc.tensor.transpose(psM[:, parity, t * P:(t + 1) * P],
                                                   ctx[:, 4 * u + t, :, :].rearrange("p h d -> p (h d)"), G.ident[:])
                    last.then_inc(m_done, 1)
                    c, parity = c + 1, 1 - parity
                for u in range(2):
                    pe.wait_ge(ctxT_ready, 2 * b + u + 1)
                    use(c)
                    for t in range(4):
                        last = nc.tensor.matmul(psM[:, parity, t * DM:(t + 1) * DM], ctxT[:, (4 * u + t) * P:(4 * u + t + 1) * P],
                                                L.wo[:], start=True, stop=True)
                    last.then_inc(m_done, 1)
                    c, parity = c + 1, 1 - parity

            batches(pe, batch)

        @block.scalar
        def _(act):
            act.sem_inc(e_taken, AHEAD)
            act.sem_inc(ctx_taken, AHEAD)

            def batch(b, last):
                for g in range(GB):
                    n = b * GB + g
                    for e, (half, kt, q0) in enumerate(STEPS):
                        for pair in range(2):
                            act.wait_ge(e_done, n * 24 + 2 * e + pair + 1)
                            if e >= KEPT:
                                act.wait_ge(pv_done, n * 12 + e - KEPT + 1)
                            heads = slice(2 * pair, 2 * pair + 2)
                            nc.scalar.activation(pT[:, e % KEPT, heads, q0:HALF], psE[:, pair, :, q0:HALF], ACT.Exp,
                                                 scale=SCALE).then_inc(e_taken, 1)
                        if e == HALF1_STEPS + LAG - 1:
                            act.wait_ge(pv_done, n * 12 + HALF1_STEPS)
                            nc.scalar.activation(ctxu[:, 1, :], psV[:, 1, :], ACT.Copy).then_inc(ctx_taken, 1)
                    act.wait_ge(pv_done, n * 12 + 12)
                    nc.scalar.activation(ctxu[:, 0, :], psV[:, 0, :], ACT.Copy).then_inc(ctx_taken, 1)

            batches(act, batch)

        @block.vector
        def _(dve):
            dve.sem_inc(m_taken, AHEAD)

            def maximum(c, parity, k):
                h, qt, kh = MAXIMA[k]
                size = min(HALF, (qt + 1) * P - kh * HALF)
                to = peak[:, h, qt:qt + 1] if qt < 4 else peak2[:, h, qt - 4, kh:kh + 1]
                dve.wait_ge(m_done, c + 1)
                nc.vector.reduce_max(to, psM[:, parity, 0:size], AX.X).then_inc(m_taken, 1)

            def peaks():
                nc.vector.drain()
                nc.vector.reduce_max(peak[:, :, 4:8], peak2[:], AX.X).then_inc(peak_ready, 1)

            def split(c, parity, g):
                dve.wait_ge(m_done, c + 1)
                turned = psM[0:HG * QT, parity, 0:P]
                high, mid, low = (negp[:, g % 2, i, :] for i in range(3))
                nc.vector.tensor_scalar(high, turned, -1.0, None, ALU.mult)
                nc.vector.drain()
                nc.vector.scalar_tensor_tensor(negr[:], turned, -1.0, high, ALU.mult, ALU.subtract).then_inc(m_taken, 1)
                nc.vector.drain()
                nc.vector.tensor_copy(mid, negr[:])
                nc.vector.drain()
                nc.vector.tensor_tensor(low, negr[:], mid, ALU.subtract).then_inc(split_ready, 1)

            def context(c, parity, g, half):
                dve.wait_ge(m_done, c + 1)
                turned = psM[:, parity, :].rearrange("p (t h w) -> p t h w", t=4, h=HG)
                nc.vector.reciprocal(inv[:], turned[:, :, :, WB])
                nc.vector.drain()
                nc.vector.tensor_tensor(ctx[:, 4 * half:4 * half + 4, g * HG:(g + 1) * HG, :], turned[:, :, :, 0:WB],
                                        inv[:].unsqueeze(3).to_broadcast([P, 4, HG, WB]), ALU.mult).then_inc(m_taken, 1)
                nc.vector.drain()
                dve.sem_inc(ctx_ready, 1)

            for k in range(NM):
                maximum(k, k % 2, k)
            peaks()
            split(NM, NM % 2, 0)
            for k in range(EARLY):
                maximum(NM + 1 + k, (NM + 1 + k) % 2, k)

            def batch(b, last):
                xb = G.x[:, bass.ds(b, 1), :, :].rearrange("p b t d -> p (b t) d")
                for g in range(GB):
                    more, more2 = others(g, last)
                    c, parity = uses(b, g, last), uses(0, g, last) % 2
                    for e in range(len(STEPS)):
                        if e == TURN_STEP:
                            if more:
                                peaks()
                                split(c, parity, (g + 1) % GB)
                                c, parity = c + 1, 1 - parity
                        if e == CONTEXT_STEP:
                            context(c, parity, g, 1)
                            c, parity = c + 1, 1 - parity
                        for part in range(PARTS):
                            if part == 0 and e == 2 and g > 0:
                                context(c, parity, g - 1, 0)
                                c, parity = c + 1, 1 - parity
                            if more2 if e in EARLY_STEPS else more:
                                for k in maxima_at(e, part):
                                    maximum(c, parity, k)
                                    c, parity = c + 1, 1 - parity
                context(c, parity, GB - 1, 0)
                c, parity = c + 1, 1 - parity
                for u in range(2):
                    dve.wait_ge(m_done, c + 1)
                    nc.vector.tensor_copy(ctxT[:, u * HALF:(u + 1) * HALF], psM[:, parity, :]).then_inc(m_taken, 1)
                    nc.vector.drain()
                    dve.sem_inc(ctxT_ready, 1)
                    c, parity = c + 1, 1 - parity
                for u in range(2):
                    dve.wait_ge(m_done, c + 1)
                    nc.vector.tensor_tensor(xb[:, 4 * u:4 * u + 4, :], xb[:, 4 * u:4 * u + 4, :],
                                            psM[:, parity, :].rearrange("p (t d) -> p t d", d=DM), ALU.add).then_inc(m_taken, 1)
                    c, parity = c + 1, 1 - parity

            batches(dve, batch)


def build(nc, A, out):
    G, W = Shared(), A
    with Memory(nc, "g") as m:
        G.x = m.sbuf("x", [P, BATCH, TPB, DM])
        G.ident = m.sbuf("ident", [P, P])
        G.ones = m.sbuf("ones", [P, P])
        G.slots_in, G.slots_out = ([nc.dram_tensor(f"{n}{i}", [HALF_SLOTS, DM], F32, kind="Internal").ap() for i in range(HALVES)]
                                   for n in ("slots_in", "slots_out"))
        G.owner_dram = nc.dram_tensor("owner", [HALVES * HALF_TILES, 1], I32, kind="Internal").ap()
        G.q_parts, G.k_parts = (nc.dram_tensor(n, [parts * P, TOKENS], BF16, kind="Internal").ap()
                                for n, parts in (("q_parts", 3), ("k_parts", 5)))
        G.one_rows = nc.dram_tensor("one_rows", [3 * HB, SEQ], BF16, kind="Internal").ap()
        with Memory(nc, "a0") as a:
            normed(G, a)
            G.zeros = a.sbuf("zeros", [P, HALF_SLOTS // ZERO_FILLS // P * DM])
            setup(nc, A["x"], G)
            layernorm(nc, "a0", G)
            attn_a(nc, G, W)
            ffn_a(nc, G, W)
        moe(nc, "m", G, W)
        attn_b(nc, "b", G, W)
        moe(nc, "n", G, W)
        finish(nc, G.x, out)


def normed(G, m):
    G.xn = m.sbuf("xn", [P, BATCH, TPB, DM])
    G.xnT = m.sbuf("xnT", [P, BATCH, SEQ])


def finish(nc, x, out):
    with Memory(nc, "end") as e:
        stored = e.sem("stored")
        block = e.block()

        @block.sync
        def _(sp):
            sp.dma_start(out.rearrange("b (t p) d -> p b t d", p=P), x[:]).then_inc(stored, 16)
            sp.wait_ge(stored, 16)


def kernel(**inputs):
    import concourse.bacc as bacc
    from concourse.bass_utils import run_bass_kernel_spmd

    a = {n: np.ascontiguousarray(v) for n, v in inputs.items()}
    wq, wk = a["L0_attn_a_Wq"], a["L0_attn_a_Wk"]
    arrays = {
        "x": a["L0_attn_a_x"],
        "wq": wq, "wk": wk, "wv": a["L0_attn_a_Wv"], "wo": a["L0_attn_a_Wo"],
        "wqT": wq.reshape(DM, HD).T, "wkT": wk.reshape(DM, HD).T, "projT": a["L0_attn_a_proj"].T,
        **{n: a["L0_attn_a_" + o] for n, o in (("w1", "W1"), ("b1", "b1"), ("w2", "W2"), ("b2", "b2"), ("ln1_g", "ln1_g"),
                                               ("ln1_b", "ln1_b"), ("ln2_g", "ln2_g"), ("ln2_b", "ln2_b"))},
        "routerT": a["L0_ffn_router_w"].T, "expert_bias": a["L0_ffn_expert_bias"],
        "w_gateT": a["L0_ffn_w_gate"].transpose(2, 0, 1), "w_downT": a["L0_ffn_w_down"].transpose(2, 0, 1),
        "bwqT": a["L0_attn_b_Wq"].reshape(HB, WB, DM).transpose(2, 1, 0).reshape(DM, DM),
        "bwkT": a["L0_attn_b_Wk"].reshape(HB, WB, DM).transpose(2, 1, 0).reshape(DM, DM),
        "bwvT": a["L0_attn_b_Wv"].T, "bwoT": a["L0_attn_b_Wo"].T, "bo": a["L0_attn_b_bo"],
        "w_gate_sharedT": a["L0_ffn_w_gate_shared"].T, "w_down_sharedT": a["L0_ffn_w_down_shared"].T,
    }
    arrays["b1"] = arrays["b1"].reshape(FFC, P).T
    arrays = {n: np.ascontiguousarray(v) for n, v in arrays.items()}
    nc = bacc.Bacc("TRN2", target_bir_lowering=False, num_devices=1)
    A = {n: nc.dram_tensor(f"in_{n}", v.shape, mybir.dt.from_np(v.dtype), kind="ExternalInput").ap() for n, v in arrays.items()}
    out = nc.dram_tensor("out_x", (BATCH, SEQ, DM), F32, kind="ExternalOutput").ap()
    build(nc, A, out)
    r = run_bass_kernel_spmd(nc, [{f"in_{n}": v for n, v in arrays.items()}], core_ids=[0])
    return r.results[0]["out_x"]
```
